# Optimizing a Trainium2 kernel written in Bass

```python
import numpy as np
import jax
import jax.numpy as jnp

def _softmax(x, axis=-1):
    return jax.nn.softmax(x, axis=axis)

def _gelu(x):
    return jax.nn.gelu(x, approximate=True)

def _silu(x):
    return jax.nn.silu(x)

def _sigmoid(x):
    return jax.nn.sigmoid(x)

def _layernorm(x, axis=-1, eps=1e-05):
    m = jnp.mean(x, axis=axis, keepdims=True)
    v = jnp.var(x, axis=axis, keepdims=True)
    return (x - m) / jnp.sqrt(v + eps)

def _scatter_add(tgt, idx, src, axis=0):
    return tgt.at[idx].add(src)

def _segment_sum(src, seg, n):
    return jax.ops.segment_sum(src, seg, n)
kernel_name = 'mk_early_fusion_embed_d1_tok_img768_r4_afc35c'

def setup_inputs(seed: int=0):
    np.random.seed(seed)
    _w = jnp.asarray

    def _rec_inputs():
        import jax
        import jax.numpy as jnp
        _rk = jax.random.key(seed)
        x = 7.57192e-06 + 1.00007 * jax.random.normal(jax.random.fold_in(_rk, 1), (64, 3, 224, 224), jnp.float32)
        x_txt = jax.random.randint(jax.random.fold_in(_rk, 51), (64, 32), 0, 30522, jnp.int32)
        mask_BS_i1_0 = jnp.where(jnp.ones((64, 32), dtype=bool), 1, 0).astype(jnp.int32)
        _lenS = jnp.full((64,), 32, jnp.int32)
        return (x, x_txt, mask_BS_i1_0, _lenS)
    x, x_txt, mask_BS_i1_0, _lenS = _rec_inputs()

    def _L0_tok_setup():
        import jax, jax.numpy as jnp
        import numpy as np
        B, C, H, W_IMG, P, D = (64, 3, 224, 224, 16, 192)
        N_PATCH = H // P * (W_IMG // P)
        SEQ = N_PATCH + 1

        def _patchify(x):
            b = x.shape[0]
            hp, wp = (H // P, W_IMG // P)
            x = x.reshape(b, C, hp, P, wp, P)
            x = x.transpose(0, 2, 4, 1, 3, 5)
            return x.reshape(b, hp * wp, C * P * P)
        key = jax.random.key(seed)
        k1, k2, k3, k4, k5 = jax.random.split(key, 5)
        in_feat = P * P * C
        return {'x': jax.random.normal(k1, (B, C, H, W_IMG), dtype=jnp.float32), 'W': jax.random.normal(k2, (in_feat, D), dtype=jnp.float32) * (1.0 / np.sqrt(in_feat)), 'b': jax.random.normal(k3, (D,), dtype=jnp.float32) * 0.02, 'pos_table': jax.random.normal(k4, (SEQ, D), dtype=jnp.float32) * 0.02, 'class_token': jax.random.normal(k5, (1, 1, D), dtype=jnp.float32)}
    _L0_tok_all = _L0_tok_setup()
    _L0_tok_in = {k: v for k, v in _L0_tok_all.items() if k in ('W', 'b', 'pos_table', 'class_token')}
    del _L0_tok_all

    def _L0_txt_setup():
        import jax, jax.numpy as jnp
        import numpy as np
        VOCAB, MAX_POS, HIDDEN, NTYPE = (30522, 128, 192, 2)
        PROB_LEN = 5
        SEP_ID = 102
        EPS = 1e-12
        key = jax.random.key(seed)
        ks = jax.random.split(key, 6)
        B, S = (64, 128)
        input_ids = jax.random.randint(ks[0], (B, S), 0, VOCAB, dtype=jnp.int64 if jax.config.jax_enable_x64 else jnp.int32)
        token_type_ids = jax.random.randint(ks[1], (B, S), 0, NTYPE, dtype=input_ids.dtype)
        text_len = jnp.clip(jax.random.randint(ks[2], (B,), 0, S + 1, dtype=input_ids.dtype), 16, S)
        word_emb = jax.random.normal(ks[3], (VOCAB, HIDDEN), jnp.float32) * 0.02
        word_emb = word_emb.at[0].set(0.0)
        pos_emb = jax.random.normal(ks[4], (MAX_POS, HIDDEN), jnp.float32) * 0.02
        type_emb = jax.random.normal(ks[5], (NTYPE, HIDDEN), jnp.float32) * 0.02
        ln_gamma = jnp.ones((HIDDEN,), jnp.float32)
        ln_beta = jnp.zeros((HIDDEN,), jnp.float32)
        return dict(input_ids=input_ids, token_type_ids=token_type_ids, text_len=text_len, word_emb=word_emb, pos_emb=pos_emb, type_emb=type_emb, ln_gamma=ln_gamma, ln_beta=ln_beta)
    _L0_txt_all = _L0_txt_setup()
    _L0_txt_in = {k: v for k, v in _L0_txt_all.items() if k in ('word_emb', 'pos_emb', 'type_emb', 'ln_gamma', 'ln_beta')}
    del _L0_txt_all

    def _L0_attn_setup():
        import jax, jax.numpy as jnp
        import numpy as np
        SEQ_LEN = 1024
        EMB = 3
        FILTER_ORDER = 16
        CH = 192
        BATCH = 16
        SHIFT = 0.0
        MODULATE = True
        USE_BIAS = True
        FAST_DECAY_PCT = 0.3
        SLOW_DECAY_PCT = 1.5
        TARGET = 0.01

        def _pos_emb(L):
            t = jnp.linspace(0.0, 1.0, L)
            bands = (EMB - 1) // 2
            t_rescaled = jnp.linspace(0.0, float(L - 1), L)
            w = 2.0 * jnp.pi * t_rescaled / L
            f = jnp.linspace(0.0001, float(max(bands - 1, 0)), bands)
            z_c = jnp.exp(-1j * f[None, :] * w[:, None])
            z = jnp.concatenate([t[:, None], jnp.real(z_c), jnp.imag(z_c)], axis=-1)
            return (z.astype(jnp.float32), t.astype(jnp.float32))

        def _implicit_filter(L, w1, b1, w2, b2, w3, b3, freq, deltas_abs):
            z, t = _pos_emb(L)
            h = jnp.sin(freq * (z @ w1.T + b1))
            h = jnp.sin(freq * (h @ w2.T + b2))
            h = h @ w3.T + b3
            if MODULATE:
                decay = jnp.exp(-t[:, None] * deltas_abs[None, :])
                h = h * (decay + SHIFT)
            return h

        def fft_conv(u, k):
            seqlen = u.shape[-2]
            fft_size = 2 * seqlen
            u_f = jnp.fft.rfft(u.astype(jnp.float32), n=fft_size, axis=-2)
            k_f = jnp.fft.rfft(k.astype(jnp.float32), n=fft_size, axis=-2) / fft_size
            y = jnp.fft.irfft(u_f * k_f, n=fft_size, axis=-2)[..., :seqlen, :]
            return y.astype(u.dtype)
        key = jax.random.key(seed)
        ks = jax.random.split(key, 8)
        u = jax.random.normal(ks[0], (BATCH, SEQ_LEN, CH), dtype=jnp.float32)
        w1 = jax.random.normal(ks[1], (FILTER_ORDER, EMB), dtype=jnp.float32) * 0.5
        b1 = jax.random.normal(ks[2], (FILTER_ORDER,), dtype=jnp.float32) * 0.1
        w2 = jax.random.normal(ks[3], (FILTER_ORDER, FILTER_ORDER), dtype=jnp.float32) * 0.25
        b2 = jax.random.normal(ks[4], (FILTER_ORDER,), dtype=jnp.float32) * 0.1
        w3 = jax.random.normal(ks[5], (CH, FILTER_ORDER), dtype=jnp.float32) * 0.25
        b3 = jax.random.normal(ks[6], (CH,), dtype=jnp.float32) * 0.1
        freq = jnp.ones((FILTER_ORDER,), dtype=jnp.float32)
        max_decay = np.log(TARGET) / FAST_DECAY_PCT
        min_decay = np.log(TARGET) / SLOW_DECAY_PCT
        deltas_abs = jnp.abs(jnp.linspace(min_decay, max_decay, CH)).astype(jnp.float32)
        bias = jax.random.normal(ks[7], (CH,), dtype=jnp.float32)
        return {'u': u, 'w1': w1, 'b1': b1, 'w2': w2, 'b2': b2, 'w3': w3, 'b3': b3, 'freq': freq, 'deltas_abs': deltas_abs, 'bias': bias}
    _L0_attn_all = _L0_attn_setup()
    _L0_attn_in = {k: v for k, v in _L0_attn_all.items() if k in ('w1', 'b1', 'w2', 'b2', 'w3', 'b3', 'freq', 'deltas_abs', 'bias')}
    del _L0_attn_all

    def _L0_ffn_setup():
        import jax, jax.numpy as jnp
        import numpy as np
        DIM = 192
        HIDDEN = 192
        NUM_EXPERTS = 4
        B, S = (16, 512)
        key = jax.random.key(seed)
        ks = jax.random.split(key, 7)
        sd = 1.0 / np.sqrt(DIM)
        sh = 1.0 / np.sqrt(HIDDEN)
        return {'x': jax.random.normal(ks[0], (B, S, DIM), dtype=jnp.float32), 'router_w': jax.random.uniform(ks[1], (DIM, NUM_EXPERTS), jnp.float32, -sd, sd), 'router_b': jax.random.uniform(ks[2], (NUM_EXPERTS,), jnp.float32, -sd, sd), 'w1': jax.random.uniform(ks[3], (NUM_EXPERTS, DIM, HIDDEN), jnp.float32, -sd, sd), 'b1': jax.random.uniform(ks[4], (NUM_EXPERTS, HIDDEN), jnp.float32, -sd, sd), 'w2': jax.random.uniform(ks[5], (NUM_EXPERTS, HIDDEN, DIM), jnp.float32, -sd, sd), 'b2': jax.random.uniform(ks[6], (NUM_EXPERTS, DIM), jnp.float32, -sd, sd)}
    _L0_ffn_all = _L0_ffn_setup()
    _L0_ffn_in = {k: v for k, v in _L0_ffn_all.items() if k in ('router_w', 'router_b', 'w1', 'b1', 'w2', 'b2')}
    del _L0_ffn_all
    return {'x': x, 'x_txt': x_txt, 'mask_BS_i1_0': mask_BS_i1_0, '_lenS': _lenS, 'L0_tok_W': _L0_tok_in['W'], 'L0_tok_b': _L0_tok_in['b'], 'L0_tok_pos_table': _L0_tok_in['pos_table'], 'L0_tok_class_token': _L0_tok_in['class_token'], 'L0_txt_word_emb': _L0_txt_in['word_emb'], 'L0_txt_pos_emb': _L0_txt_in['pos_emb'], 'L0_txt_type_emb': _L0_txt_in['type_emb'], 'L0_txt_ln_gamma': _L0_txt_in['ln_gamma'], 'L0_txt_ln_beta': _L0_txt_in['ln_beta'], 'L0_attn_w1': _L0_attn_in['w1'], 'L0_attn_b1': _L0_attn_in['b1'], 'L0_attn_w2': _L0_attn_in['w2'], 'L0_attn_b2': _L0_attn_in['b2'], 'L0_attn_w3': _L0_attn_in['w3'], 'L0_attn_b3': _L0_attn_in['b3'], 'L0_attn_freq': _L0_attn_in['freq'], 'L0_attn_deltas_abs': _L0_attn_in['deltas_abs'], 'L0_attn_bias': _L0_attn_in['bias'], 'L0_ffn_router_w': _L0_ffn_in['router_w'], 'L0_ffn_router_b': _L0_ffn_in['router_b'], 'L0_ffn_w1': _L0_ffn_in['w1'], 'L0_ffn_b1': _L0_ffn_in['b1'], 'L0_ffn_w2': _L0_ffn_in['w2'], 'L0_ffn_b2': _L0_ffn_in['b2']}

def reference(x, x_txt, mask_BS_i1_0, _lenS, L0_tok_W, L0_tok_b, L0_tok_pos_table, L0_tok_class_token, L0_txt_word_emb, L0_txt_pos_emb, L0_txt_type_emb, L0_txt_ln_gamma, L0_txt_ln_beta, L0_attn_w1, L0_attn_b1, L0_attn_w2, L0_attn_b2, L0_attn_w3, L0_attn_b3, L0_attn_freq, L0_attn_deltas_abs, L0_attn_bias, L0_ffn_router_w, L0_ffn_router_b, L0_ffn_w1, L0_ffn_b1, L0_ffn_w2, L0_ffn_b2):
    import jax
    import jax.numpy as jnp

    def _L0_tok_ref(x, W, b, pos_table, class_token):
        import jax, jax.numpy as jnp
        import numpy as np
        B, C, H, W_IMG, P, D = (64, 3, 224, 224, 16, 192)
        N_PATCH = H // P * (W_IMG // P)
        SEQ = N_PATCH + 1

        def _patchify(x):
            b = x.shape[0]
            hp, wp = (H // P, W_IMG // P)
            x = x.reshape(b, C, hp, P, wp, P)
            x = x.transpose(0, 2, 4, 1, 3, 5)
            return x.reshape(b, hp * wp, C * P * P)
        patches = _patchify(x)
        tokens = jnp.einsum('bnf,fd->bnd', patches, W) + b
        cls = jnp.broadcast_to(class_token, (x.shape[0], 1, D))
        seq = jnp.concatenate([cls, tokens], axis=1)
        return seq + pos_table[None, :, :]

    def _L0_txt_ref(input_ids, token_type_ids, text_len, word_emb, pos_emb, type_emb, ln_gamma, ln_beta):
        import jax, jax.numpy as jnp
        import numpy as np
        VOCAB, MAX_POS, HIDDEN, NTYPE = (30522, 128, 192, 2)
        PROB_LEN = 5
        SEP_ID = 102
        EPS = 1e-12
        B, S = input_ids.shape
        we = word_emb[input_ids]
        len_range = jnp.arange(S, dtype=text_len.dtype)[None, :]
        tl = text_len[:, None]
        m1 = len_range < tl - 1
        m2b = len_range < tl - 1 - PROB_LEN
        m3 = (m1 & ~m2b).astype(we.dtype)[..., None]
        prob_avg = jnp.sum(we * m3, axis=1, keepdims=True) / PROB_LEN
        m4 = (len_range == tl - 1 - PROB_LEN).astype(we.dtype)[..., None]
        m5 = (len_range == tl - PROB_LEN).astype(we.dtype)[..., None]
        m2 = m2b.astype(we.dtype)[..., None]
        m6 = 1.0 - (m2 + m4 + m5)
        sep_vec = word_emb[SEP_ID]
        pad_vec = word_emb[0]
        we_blend = we * m2 + prob_avg * m4 + sep_vec * m5 + pad_vec * m6
        emb = we_blend + pos_emb[:S][None, :, :] + type_emb[token_type_ids]
        mu = jnp.mean(emb, axis=-1, keepdims=True)
        var = jnp.mean(jnp.square(emb - mu), axis=-1, keepdims=True)
        out = (emb - mu) * jax.lax.rsqrt(var + EPS) * ln_gamma + ln_beta
        return out

    def _L0_attn_ref(u, w1, b1, w2, b2, w3, b3, freq, deltas_abs, bias):
        import jax, jax.numpy as jnp
        import numpy as np
        SEQ_LEN = 1024
        EMB = 3
        FILTER_ORDER = 16
        CH = 192
        BATCH = 16
        SHIFT = 0.0
        MODULATE = True
        USE_BIAS = True
        FAST_DECAY_PCT = 0.3
        SLOW_DECAY_PCT = 1.5
        TARGET = 0.01

        def _pos_emb(L):
            t = jnp.linspace(0.0, 1.0, L)
            bands = (EMB - 1) // 2
            t_rescaled = jnp.linspace(0.0, float(L - 1), L)
            w = 2.0 * jnp.pi * t_rescaled / L
            f = jnp.linspace(0.0001, float(max(bands - 1, 0)), bands)
            z_c = jnp.exp(-1j * f[None, :] * w[:, None])
            z = jnp.concatenate([t[:, None], jnp.real(z_c), jnp.imag(z_c)], axis=-1)
            return (z.astype(jnp.float32), t.astype(jnp.float32))

        def _implicit_filter(L, w1, b1, w2, b2, w3, b3, freq, deltas_abs):
            z, t = _pos_emb(L)
            h = jnp.sin(freq * (z @ w1.T + b1))
            h = jnp.sin(freq * (h @ w2.T + b2))
            h = h @ w3.T + b3
            if MODULATE:
                decay = jnp.exp(-t[:, None] * deltas_abs[None, :])
                h = h * (decay + SHIFT)
            return h

        def fft_conv(u, k):
            seqlen = u.shape[-2]
            fft_size = 2 * seqlen
            u_f = jnp.fft.rfft(u.astype(jnp.float32), n=fft_size, axis=-2)
            k_f = jnp.fft.rfft(k.astype(jnp.float32), n=fft_size, axis=-2) / fft_size
            y = jnp.fft.irfft(u_f * k_f, n=fft_size, axis=-2)[..., :seqlen, :]
            return y.astype(u.dtype)
        L = u.shape[-2]
        k = _implicit_filter(L, w1, b1, w2, b2, w3, b3, freq, deltas_abs)
        y = fft_conv(u, k)
        if USE_BIAS:
            y = y + u * bias
        return y

    def _L0_ffn_ref(x, router_w, router_b, w1, b1, w2, b2):
        import jax, jax.numpy as jnp
        import numpy as np
        DIM = 192
        HIDDEN = 192
        NUM_EXPERTS = 4
        B, S = (16, 512)
        logits = jnp.einsum('bsd,de->bse', x, router_w) + router_b
        probs = jax.nn.softmax(logits, axis=-1)
        idx = jnp.argmax(probs, axis=-1)
        dispatch = jax.nn.one_hot(idx, NUM_EXPERTS, dtype=x.dtype)
        h = jnp.einsum('bsd,edh->besh', x, w1) + b1[None, :, None, :]
        h = jax.nn.gelu(h, approximate=False)
        y = jnp.einsum('besh,ehd->besd', h, w2) + b2[None, :, None, :]
        out = jnp.einsum('besd,bse->bsd', y, dispatch)
        out = out + x
        return out
    h = _L0_tok_ref(x, L0_tok_W, L0_tok_b, L0_tok_pos_table, L0_tok_class_token)
    h = jnp.concatenate([h, _L0_txt_ref(x_txt, mask_BS_i1_0, _lenS, L0_txt_word_emb, L0_txt_pos_emb, L0_txt_type_emb, L0_txt_ln_gamma, L0_txt_ln_beta)], axis=1)
    h = h + _L0_attn_ref(_layernorm(h, axis=-1), L0_attn_w1, L0_attn_b1, L0_attn_w2, L0_attn_b2, L0_attn_w3, L0_attn_b3, L0_attn_freq, L0_attn_deltas_abs, L0_attn_bias)
    h = h + _L0_ffn_ref(_layernorm(h, axis=-1), L0_ffn_router_w, L0_ffn_router_b, L0_ffn_w1, L0_ffn_b1, L0_ffn_w2, L0_ffn_b2)
    return h

_drawn_inputs = setup_inputs


def setup_inputs(seed=0):
    import zlib

    import numpy as np

    out = dict(_drawn_inputs(seed))
    spreads = {'L0_txt_ln_gamma': (1.0, 0.2), 'L0_txt_ln_beta': (0.0, 0.1), 'L0_attn_freq': (1.0, 0.6)}
    factors = {'L0_tok_b': 2.838,
     'L0_attn_w1': 23.498,
     'L0_attn_b1': 8.0,
     'L0_attn_w2': 28.424,
     'L0_attn_b2': 28.686,
     'L0_attn_w3': 25.237,
     'L0_attn_b3': 200.0,
     'L0_attn_deltas_abs': 200.0,
     'L0_ffn_b1': 8.0,
     'L0_ffn_b2': 3.16}
    for name, (base, spread) in spreads.items():
        noise = np.random.default_rng([zlib.crc32(name.encode()), seed]).standard_normal(out[name].shape)
        drawn = base * np.exp(spread * noise) if base else spread * noise
        out[name] = jnp.asarray(drawn.astype(out[name].dtype))
    for name, factor in factors.items():
        out[name] = (out[name] * factor).astype(out[name].dtype)
    return out
```

```python
import concourse.bass as bass
from concourse import mybir

F32 = mybir.dt.float32
F16 = mybir.dt.float16
I32 = mybir.dt.int32
U32 = mybir.dt.uint32
ALU = mybir.AluOpType
ACT = mybir.ActivationFunctionType
AX = mybir.AxisListType.X

B = 64
D = 192
NPATCH = 196
KC = 6
TXT = 32
L = 1 + NPATCH + TXT
NQ = 2 * B
CLS = L - 1 - 128
RW = D + 4
RU = D + 3
MEAN, RSTD, ROWID = D, D + 1, D + 2
PAIRS = B // 2
VOCAB, SEP = 30522, 102
NTOK = B * L
E4 = 4
HC = 96
REGION = NTOK + 128
DUMMY = E4 * REGION
SLOTS = 120
STEPS = SLOTS // 2

XS, WS = 16.0, 256.0
US, GS = 1024.0, 512.0
KS = 1.0 / 16
CONV_OUT = 1.0 / (KS * US * 2 * L)
CONV_BIAS = KS * 2 * L

KP = 360
COPY = 2 * D * KP + 128
CG = 8
NG = D // CG
TC = 64
TAPW = 256
RUN = (2 * CG - 1) * KP + TAPW
LN_EPS, TXT_EPS = 1e-5, 1e-12
PI = 3.141592653589793
MAGIC = 12582912.0
PI2A, PI2B = 6.28125, 0.0019350051879882812
PI2C = 2 * PI - PI2A - PI2B


def build(nc, a):
    import contextlib
    ctx = contextlib.ExitStack()
    with ctx:
        def sb(name, shape, dt):
            return ctx.enter_context(nc.sbuf_tensor(name, shape, dt))

        def sem(name):
            return ctx.enter_context(nc.semaphore(name))

        out = a["out"]
        taps_dram = nc.dram_tensor("taps", (2, COPY), F16, kind="Internal").ap()
        tap0_dram = nc.dram_tensor("tap0", (D,), F32, kind="Internal").ap()
        sorted_dram = nc.dram_tensor("sorted_rows", (DUMMY + 128, RU), F32, kind="Internal").ap()

        h = sb("h", [128, NQ, RW], F32)
        ARENA = 104576
        arena = sb("arena", [128, ARENA // 4], F32)
        top = [0]

        def carve(shape, dt):
            n = 1
            for s in shape:
                n *= s
            size = (n * (2 if dt == F16 else 4) + 31) // 32 * 8
            v = arena[:, top[0]:top[0] + size]
            top[0] += size
            assert top[0] * 4 <= ARENA, (top[0] * 4, shape)
            if dt != F32:
                v = v.bitcast(dt)
            v = v[:, 0:n]
            if len(shape) == 2:
                v = v.rearrange("p (a b) -> p a b", b=shape[1])
            elif len(shape) == 3:
                v = v.rearrange("p (a b c) -> p a b c", b=shape[1], c=shape[2])
            elif len(shape) == 4:
                v = v.rearrange("p (a b c d) -> p a b c d", b=shape[1], c=shape[2], d=shape[3])
            return v

        xin = carve([4, KC, 384], F32)
        xhi = carve([2, KC, 384], F16)
        xlo = carve([2, KC, 384], F16)
        whi = carve([KC, D], F16)
        wlo = carve([KC, D], F16)
        posb = carve([6, D], F32)
        lout = carve([2, D], F32)
        tokb = lout[:, 0, :]
        uclh = carve([2, D], F16)
        idsp = carve([16], I32)
        lenp = carve([16], I32)
        tmask = carve([3, 16], F32)
        blk = carve([128], F32)
        trow = carve([D], F32)
        text_top = top[0]
        we = carve([16, D], F32)
        lenrep = carve([1024], I32)
        amat = carve([1024], F32)
        coef = carve([1024], F32)
        coefi = carve([1024], I32)
        stats = carve([NQ, 6], F32)
        top[0] = text_top
        wraw = carve([KC, D], F32)
        zt = carve([L], F32)
        tgrid = carve([L], F32)
        ang = carve([L], F32)
        red = carve([L], F32)
        sin1 = carve([L], F32)
        sin2 = carve([L], F32)
        tap = carve([2, L], F32)
        taphl = carve([2, 2, KP], F16)
        fw1 = carve([16], F32)
        fw2 = carve([16], F32)
        fw3 = carve([D], F32)
        fb = carve([4], F32)
        cb = carve([2, 3], F32)

        top[0] = 0
        uhi = carve([2, TC, NQ], F16)
        ulo = carve([2, TC, NQ], F16)
        toep = carve([2, RUN], F16)
        ctap = carve([2, CG, TAPW], F16)
        utmp = carve([2, 16, TC], F32)

        top[0] = 0
        ztok = carve([16, D], F32)
        zthi = carve([2, 2, 2, 128], F16)
        ztlo = carve([2, 2, 2, 128], F16)
        rwraw = carve([2, E4], F32)
        rwhi = carve([2, E4], F16)
        rwlo = carve([2, E4], F16)
        logit = carve([16, E4], F32)
        prob = carve([16, E4], F32)
        pick = carve([16, E4], F32)
        onehot = carve([16, E4], F16)
        rank = carve([16, E4], F32)
        rmax = carve([16], F32)
        rsum = carve([16], F32)
        run = carve([2, E4], F32)
        destf = carve([16], F32)
        tabf = carve([4, SLOTS], F32)
        table = carve([2, SLOTS], I32)
        rstats = carve([16, 6], F32)
        padrow = carve([RW], I32)
        ltri = carve([128], F16)
        onesm = carve([128], F16)
        w1raw = carve([E4 * 2, D], F32)
        w2raw = carve([E4 * 2, D], F32)
        w1hi = carve([E4 * 2, D], F16)
        w1lo = carve([E4 * 2, D], F16)
        w2hi = carve([E4 * 2, D], F16)
        w2lo = carve([E4 * 2, D], F16)
        row = carve([6, 2, RW], F32)
        x2 = carve([4, 2, D], F32)
        xthi = carve([2, 2, 2, 128], F16)
        xtlo = carve([2, 2, 2, 128], F16)
        act1 = carve([2, 2, D], F32)
        gthi = carve([2, 2, 2, 128], F16)
        gtlo = carve([2, 2, 2, 128], F16)
        res = carve([2, 2, D], F32)

        ident = sb("ident", [128, 128], F32)
        mean = sb("mean", [128, NQ], F32)
        rstd = sb("rstd", [128, NQ], F32)
        s1 = sb("s1", [128, NQ], F32)
        s2 = sb("s2", [128, NQ], F32)
        dest = sb("dest", [128, NQ], I32)
        rowid = sb("rowid", [128, NQ], I32)
        ucls = sb("ucls", [128, 4, D], F32)
        urow = sb("urow", [128, D], F16)
        cls6 = sb("cls6", [128, 8], F32)
        clsm = sb("clsm", [128, 4], F32)
        small = sb("small", [128, 96], F32)
        padid = sb("padid", [128, E4], I32)
        tabn = sb("tabn", [1, 24], F32)
        tabi = sb("tabi", [1, 4], I32)
        psum = [ctx.enter_context(nc.psum_tensor(f"bank{i}", [128, 512], F32)) for i in range(8)]
        s32, s32v, tgt, spart = small[:, 0:32], small[:, 32:64], small[:, 64:66], small[:, 66:67]
        vmask, rbias, pickw, regbase, piota = small[:, 67:68], small[:, 68:72], small[:, 72:76], small[:, 76:80], small[:, 80:81]
        tilej = small[:, 81:89]

        const_in = sem("const_in")
        x_in = [sem(f"x_in{i}") for i in range(4)]
        w_split = sem("w_split")
        x_hi, x_lo = sem("x_hi"), sem("x_lo")
        proj, proj_out = sem("proj"), sem("proj_out")
        act_chain = sem("act_chain")
        ask = sem("ask")
        pe_filter = sem("pe_filter")
        dve_filter = sem("dve_filter")
        v = sem("vector_chain")
        taps_out = sem("taps_out")
        tap0_in = sem("tap0_in")
        text_in = sem("text_in")
        gathered = sem("gathered")
        text_mat, text_mm, text_norm, text_affine, gb_in = (sem("text_mat"), sem("text_mm"), sem("text_norm"),
                                                            sem("text_affine"), sem("gb_in"))
        pchain = sem("pool_chain")
        rows_clear = sem("rows_clear")
        cls_sum = sem("cls_sum")
        h_in = sem("h_in")
        cls_split, urow_in = sem("cls_split"), sem("urow_in")
        zeroed = sem("zeroed")
        stat2 = sem("stat2")
        a_done = sem("a_done")
        u_norm, u_hi, u_lo = sem("u_norm"), sem("u_hi"), sem("u_lo")
        toep_in = [sem("toep_in0"), sem("toep_in1")]
        conv, conv_free = sem("conv"), sem("conv_free")
        cls_out, cls_in = sem("cls_out"), sem("cls_in")
        d_in = sem("d_in")
        d_split, low_split = sem("d_split"), sem("low_split")
        z_norm, z_t, z_hi, z_lo, z_log, z_rank = (sem("z_norm"), sem("z_t"), sem("z_hi"), sem("z_lo"), sem("z_log"),
                                                  sem("z_rank"))
        z_pick, z_exp, routed = sem("z_pick"), sem("z_exp"), sem("routed")
        v1 = sem("vector_chain_routing")
        v2 = sem("vector_chain_table")
        scattered, table_out, dummy_in = sem("scattered"), sem("table_out"), sem("dummy_in")
        stores_begun = sem("stores_begun")
        row_in = [sem(f"row_in{i}") for i in range(6)]
        row_out = [sem(f"row_out{i}") for i in range(6)]
        x2_done, r_done, lo1_done, lo2_done, fin_done = (sem("x2_done"), sem("r_done"), sem("lo1_done"), sem("lo2_done"),
                                                         sem("fin_done"))
        t1_done, l1_done, t2_done, l2_done = sem("t1_done"), sem("l1_done"), sem("t2_done"), sem("l2_done")
        hi1_done, act_done, hi2_done = sem("hi1_done"), sem("act_done"), sem("hi2_done")
        block = ctx.enter_context(nc.Block())
        ds = bass.ds

        CONV_STEPS = D // 4

        def flat(t):
            return t.rearrange("p a b c -> p (a b c)")

        def bank3(i, n, m):
            return psum[i][:, 0:n * m].rearrange("p (a b) -> p a b", b=m)

        @block.sync
        def _(sp):
            wiring = [(ident[:, :], a["ident"]), (blk, a["blk"]), (small[:, 0:89], a["small"]),
                      (idsp, a["idsp"]), (lenp, a["lenp"]), (rowid[:, :], a["rowid"]),
                      (posb.rearrange("p a b -> p (a b)"), a["pos"]), (tokb, a["tokb"]),
                      (wraw, a["wp"]),
                      (zt[0:3, :], a["zt"]), (tgrid[0:96, :], a["tgrid"]),
                      (fw1[0:3, :], a["fw1"]), (fw2[0:16, :], a["fw2"]), (fw3[0:16, :], a["fw3"]),
                      (fb[0:16, :], a["fb"]), (cb[0:96, :, :], a["cb"]),
                      (ucls[0:1, 0, :], a["cls"]), (ucls[0:1, 3, :], a["pos0"])]
            for dst, src in wiring:
                sp.dma_start(dst, src).then_inc(const_in, 16)
            sp.dma_start(xin[:, 0, :, 0:256], a["xl"]).then_inc(x_in[0], 16)
            for n in range(1, 4):
                sp.dma_start(xin[:, n, :, :], a["xt"][n - 1]).then_inc(x_in[n], 16)
            sp.wait_ge(dve_filter, 2)
            for half in range(2):
                for copy in range(2):
                    sp.dma_start(taps_dram[copy, half * 96 * 2 * KP:(half * 96 + 96) * 2 * KP].rearrange("(c x) -> c x", x=2 * KP),
                                 taphl[0:96, half, :, :].rearrange("p a b -> p (a b)")).then_inc(taps_out, 16)
                    if half:
                        sp.dma_start(taps_dram[copy:copy + 1, COPY - 128:COPY], taphl[0:1, 0, 0, 0:128]).then_inc(taps_out, 16)
                sp.dma_start(tap0_dram[half * 96:half * 96 + 96].unsqueeze(1), tap[0:96, half, 0:1]).then_inc(taps_out, 16)
            sp.wait_ge(taps_out, 16 * 8)
            sp.dma_start(ucls[0:1, 2, :], tap0_dram.unsqueeze(0)).then_inc(tap0_in, 16)
            sp.wait_ge(cls_out, 1)
            for half in range(2):
                if half:
                    sp.wait_ge(text_mat, 1)
                sp.dma_start(lenrep, a["lenv"][0:1, half * 1024:half * 1024 + 1024].to_broadcast([128, 1024])).then_inc(text_in, 16)
                sp.dma_start(coefi[0:E4, :], a["lenv"][:, half * 1024:half * 1024 + 1024]).then_inc(text_in, 16)
                if half == 0:
                    sp.dma_start(trow[0:E4, :], a["trows"]).then_inc(text_in, 16)
            sp.wait_ge(text_mm, 16)
            sp.dma_start(amat[:, 0:2 * D], a["gb"]).then_inc(gb_in, 16)
            sp.wait_ge(cls_sum, 1)
            sp.wait_ge(rows_clear, 1)
            sp.dma_start(h[CLS:CLS + 1, B:NQ, 0:D], ucls[0:1, 0:1, :].to_broadcast([1, B, D])).then_inc(h_in, 16)
            sp.wait_ge(cls_split, 1)
            sp.wait_ge(zeroed, 1)
            sp.dma_start(urow[0:1, :], uclh[0:1, 0, :]).then_inc(urow_in, 16)
            sp.dma_start(urow[1:2, :], uclh[0:1, 0, :]).then_inc(urow_in, 16)
            sp.dma_start(urow[2:3, :], uclh[0:1, 1, :]).then_inc(urow_in, 16)
            sp.wait_ge(proj_out, 1)
            for n in range(4):
                sp.dma_start(h[64 + n:65 + n, B:NQ, 0:D],
                             lout[64 * (n % 2):64 * (n % 2) + 64, n // 2, :]).then_inc(h_in, 16)
            with sp.Fori(0, 7) as i:
                for k in range(4):
                    sp.wait_ge(x_hi, 4 * i + k + 1)
                    sp.wait_ge(x_lo, 4 * i + k + 1)
                    sp.dma_start(xin[:, k, :, :], a["xt"][ds(4 * i + k + 3, 1)].rearrange("a p k t -> (a p) k t")).then_inc(x_in[k], 16)
            sp.wait_ge(x_hi, 29)
            sp.wait_ge(x_lo, 29)
            sp.dma_start(xin[:, 0, :, :], a["xt"][31]).then_inc(x_in[0], 16)
            sp.wait_ge(text_affine, 1)
            hj = h[:, B:NQ, :].rearrange("p (k b) c -> p k b c", b=4)
            for b4 in range(4):
                sp.dma_start(hj[68:100, :, b4, 0:D], we[32 * b4:32 * b4 + 32, :, :]).then_inc(h_in, 16)
            sp.wait_ge(a_done, 1)
            sp.wait_ge(zeroed, 2)
            sp.wait_ge(proj, 33)
            for g in range(NG):
                if g >= 2:
                    sp.wait_ge(conv, 2 * (g - 1))
                src = bass.AP(taps_dram.tensor, g * CG * 2 * KP + 128, [[COPY - 64, 2], [-1, 64], [1, RUN]])
                sp.dma_start(toep[:, g % 2], src).then_inc(toep_in[g % 2], 16)
                src = bass.AP(taps_dram.tensor, g * CG * 2 * KP + 129, [[KP, 2], [2 * KP, CG], [1, TAPW]])
                sp.dma_start(ctap[0:2, g % 2], src).then_inc(toep_in[g % 2], 16)
                src = bass.AP(taps_dram.tensor, g * CG * 2 * KP + 129, [[KP, 1], [2 * KP, CG], [1, TAPW]])
                sp.dma_start(ctap[2:3, g % 2], src).then_inc(toep_in[g % 2], 16)
            sp.wait_ge(cls_out, 1)
            sp.wait_ge(conv_free, 4 + CONV_STEPS)
            sp.dma_start(h[CLS:CLS + 1, B:NQ, 0:D], ucls[0:1, 3:4, :].to_broadcast([1, B, D])).then_inc(cls_in, 16)
            for dst, src in [(rwraw[0:HC], a["rw"]), (w1raw[0:HC + 1], a["w1"]), (w2raw[0:HC + 1], a["w2"]),
                             (padrow, a["padrow"]), (tabf[0:1, 3, :], a["slots"]), (ltri, a["ltri"])]:
                sp.dma_start(dst, src).then_inc(d_in, 16)
            sp.wait_ge(d_in, 96)
            sp.dma_start(sorted_dram[DUMMY:DUMMY + 128], padrow[:, 0:RU].bitcast(F32)).then_inc(dummy_in, 16)
            sp.wait_ge(dummy_in, 16)
            sp.wait_ge(scattered, 16 * (NQ + E4))
            sp.wait_ge(table_out, 1)

            def load_rows(s, k):
                for t in range(2):
                    start = sp.value_load(table[0:1, 0, ds(2 * s + t, 1)], min_val=0, max_val=DUMMY)
                    sp.dma_start(row[:, k, t, 0:RU], sorted_dram[ds(start, 128), :]).then_inc(row_in[k], 16)

            for s in range(6):
                load_rows(s, s)
            with sp.Fori(0, STEPS // 6 - 1) as i:
                for k in range(6):
                    sp.wait_ge(row_out[k], 32 * i + 32)
                    load_rows(6 * i + 6 + k, k)

        @block.gpsimd
        def _(pool):
            pool.memset(h[96:128, B:NQ, 0:D], 0.0).then_inc(rows_clear, 1)
            pool.wait_ge(rows_clear, 1)
            pool.memset(urow[:, :].bitcast(F32), 0.0).then_inc(zeroed, 1)
            pool.wait_ge(zeroed, 1)
            pool.wait_ge(const_in, 16 * 18)
            pool.wait_ge(cls_out, 1)
            for k in range(16):
                pool.indirect_dma_start(we[:, k, :], None, a["word"], bass.IndirectOffsetOnAxis(
                    ap=idsp[:, k:k + 1].bitcast(U32), axis=0)).then_inc(gathered, 16)
            pool.wait_ge(text_norm, 1)
            pool.wait_ge(gb_in, 16)
            gam = amat[:, 0:D].unsqueeze(1).to_broadcast([128, 16, D])
            bet = amat[:, D:2 * D].unsqueeze(1).to_broadcast([128, 16, D])
            pool.tensor_tensor(we, we, gam, ALU.mult).then_inc(pchain, 1)
            pool.wait_ge(pchain, 1)
            pool.tensor_tensor(we, we, bet, ALU.add).then_inc(text_affine, 1)
            pool.wait_ge(a_done, 1)
            pool.wait_ge(h_in, 16 * 9)
            pool.wait_ge(proj, 33)
            pool.memset(ctap.rearrange("p a c t -> p (a c t)").bitcast(F32), 0.0).then_inc(zeroed, 1)
            for g in range(8):
                pool.wait_ge(routed, g + 1)
                for q in range(16 * g, 16 * g + 16):
                    pool.indirect_dma_start(sorted_dram[:, :], bass.IndirectOffsetOnAxis(
                        ap=dest[:, q:q + 1].bitcast(U32), axis=0), h[:, q, 0:RU], None,
                        bounds_check=DUMMY - 1, oob_is_err=False).then_inc(scattered, 16)
            pool.wait_ge(table_out, 1)
            pool.wait_ge(d_in, 96)
            for e in range(E4):
                pool.indirect_dma_start(sorted_dram[:, :], bass.IndirectOffsetOnAxis(
                    ap=padid[:, e:e + 1].bitcast(U32), axis=0), padrow[:, 0:RU].bitcast(F32), None).then_inc(scattered, 16)

            def store_rows(s, k):
                pool.wait_ge(fin_done, s + 1)
                pool.sem_inc(stores_begun, 1)
                for t in range(2):
                    pool.indirect_dma_start(out[:, :], bass.IndirectOffsetOnAxis(
                        ap=row[:, k, t, ROWID:ROWID + 1].bitcast(U32), axis=0),
                        res[:, k % 2, t, :], None, bounds_check=NTOK - 1, oob_is_err=False).then_inc(row_out[k], 16)

            with pool.Fori(0, STEPS // 6) as i:
                for k in range(6):
                    store_rows(6 * i + k, k)
            for k in range(6):
                pool.wait_ge(row_out[k], 32 * STEPS // 6)

        @block.scalar
        def _(act):
            act.wait_ge(const_in, 16 * 18)
            act.activation(whi, wraw, ACT.Copy, scale=WS).then_inc(act_chain, 1)
            act.wait_ge(ask, 1)
            act.activation(sin1[0:16], red[0:16], ACT.Sin).then_inc(act_chain, 1)
            act.wait_ge(ask, 2)
            act.activation(sin2[0:16], red[0:16], ACT.Sin).then_inc(act_chain, 1)
            act.wait_ge(ask, 3)
            act.activation(ang[0:96], tgrid[0:96], ACT.Exp, scale=cb[0:96, 0, 1:2]).then_inc(act_chain, 1)
            act.activation(red[0:96], tgrid[0:96], ACT.Exp, scale=cb[0:96, 1, 1:2]).then_inc(act_chain, 1)
            act.wait_ge(ask, 4)
            act.activation(clsm[0:1, 2:3], clsm[0:1, 1:2], ACT.Sqrt).then_inc(act_chain, 1)
            act.wait_ge(ask, 5)
            act.activation(s2[:, 0:16], s1[:, 0:16], ACT.Sqrt).then_inc(act_chain, 1)
            act.wait_ge(x_in[0], 16)
            act.activation(xhi[:, 0, :, 0:256], xin[:, 0, :, 0:256], ACT.Copy, scale=XS).then_inc(x_hi, 1)

            def pixels(n, k, turn):
                act.wait_ge(x_in[k], 16 * turn)
                act.wait_ge(proj, n - 1)
                act.activation(xhi[:, k % 2], xin[:, k], ACT.Copy, scale=XS).then_inc(x_hi, 1)

            with act.Fori(0, 8) as i:
                for k in range(4):
                    n = 4 * i + k + 1
                    pixels(n, (k + 1) % 4, i + (2 if k == 3 else 1))
            act.wait_ge(ask, 6)
            act.activation(s2[:, :], s1[:, :], ACT.Sqrt).then_inc(act_chain, 1)
            for third in range(3):
                if third == 2:
                    act.wait_ge(conv, CONV_STEPS // 3)
                with act.Fori(0, 4) as i:
                    for k in range(2):
                        act.wait_ge(u_norm, 8 * third + 2 * i + k + 1)
                        dst = uhi[:, third % 2, :, ds(32 * i + 16 * k, 16)].rearrange("p c q -> p q c")
                        act.activation(dst, utmp[:, k], ACT.Copy).then_inc(u_hi, 1)
            act.wait_ge(d_in, 96)
            act.activation(rwhi[0:HC], rwraw[0:HC], ACT.Copy, scale=WS).then_inc(d_split, 1)
            act.activation(w1hi[0:HC + 1], w1raw[0:HC + 1], ACT.Copy, scale=WS).then_inc(d_split, 1)
            act.activation(w2hi[0:HC + 1], w2raw[0:HC + 1], ACT.Copy, scale=WS).then_inc(d_split, 1)
            with act.Fori(0, 8) as g:
                act.wait_ge(ask, g * 2 + 7)
                act.activation(s2[:, 0:16], s1[:, 0:16], ACT.Sqrt).then_inc(act_chain, 1)
                for t in range(8):
                    act.wait_ge(z_t, g * 8 + t + 1)
                    if t >= 2:
                        act.wait_ge(z_log, g * 8 + t - 1)
                    act.activation(zthi[0:HC, t % 2], psum[t % 2][0:HC, :].rearrange("p (a b c) -> p a b c", a=2, b=2),
                                   ACT.Copy, scale=US).then_inc(z_hi, 1)
                act.wait_ge(ask, g * 2 + 8)
                act.activation(prob, logit, ACT.Exp).then_inc(z_exp, 1)

            def hi1(n, k):
                act.wait_ge(t1_done, n + 1)
                act.activation(xthi[0:HC, k % 2], psum[k % 2][0:HC, :].rearrange("p (a b c) -> p a b c", a=2, b=2),
                               ACT.Copy, scale=US).then_inc(hi1_done, 1)

            def gelu(n, k):
                act.wait_ge(l1_done, n + 1)
                act.activation(act1[:, k % 2], bank3(2 + k % 2, 2, D), ACT.Gelu, scale=1 / (US * WS)).then_inc(act_done, 1)

            def hi2(n, k):
                act.wait_ge(t2_done, n + 1)
                act.activation(gthi[0:HC, k % 2], psum[4 + k % 2][0:HC, :].rearrange("p (a b c) -> p a b c", a=2, b=2),
                               ACT.Copy, scale=GS).then_inc(hi2_done, 1)

            def step(n, k, first, last):
                if not last:
                    if first is None or n >= 2:
                        act.wait_ge(l1_done, n - 1)
                    hi1(n, k)
                if first is None or n >= 1:
                    if not last or n - 1 < STEPS:
                        if first is None or n >= 3:
                            act.wait_ge(t2_done, n - 2)
                        gelu(n - 1, (k - 1) % 6)
                if first is None or n >= 2:
                    if not last or n - 2 < STEPS:
                        if first is None or n >= 4:
                            act.wait_ge(l2_done, n - 3)
                        hi2(n - 2, (k - 2) % 6)

            for n in range(6):
                step(n, n, True, False)
            with act.Fori(0, STEPS // 6 - 1) as i:
                for k in range(6):
                    step(6 * i + k + 6, k, None, False)
            for n in range(STEPS, STEPS + 2):
                step(n, n % 6, None, True)

        @block.tensor
        def _(pe):
            pe.wait_ge(const_in, 16 * 18)
            pe.matmul(psum[0][0:16, 0:L], fw1[0:3, :], zt[0:3, :], start=True, stop=True).then_inc(pe_filter, 1)
            pe.wait_ge(act_chain, 2)
            pe.matmul(psum[0][0:16, 0:L], fw2[0:16, :], sin1[0:16, :], start=True, stop=True).then_inc(pe_filter, 1)
            pe.wait_ge(act_chain, 3)
            for half in range(2):
                pe.matmul(psum[1 + half][0:96, 0:L], fw3[0:16, half * 96:half * 96 + 96], sin2[0:16, :],
                          start=True, stop=True).then_inc(pe_filter, 1)
            pe.wait_ge(gathered, 256)
            for half in range(2):
                pe.wait_ge(text_mat, half + 1)
                for k in range(8):
                    o = psum[half * 4 + k // 2][:, (k % 2) * D:(k % 2) * D + D]
                    if half == 0 and k == 0:
                        pe.wait_ge(cls_out, 1)
                    pe.matmul(o, amat[:, k * 128:k * 128 + 128], we[:, half * 8 + k, :], start=True, stop=False)
                    pe.matmul(o, coef[0:E4, k * 128:k * 128 + 128], trow[0:E4, :], start=False, stop=True).then_inc(text_mm, 1)
            pe.wait_ge(w_split, 1)

            def project(k, o, t):
                xh, xl = xhi[:, k % 2, :, t * 128:t * 128 + 128], xlo[:, k % 2, :, t * 128:t * 128 + 128]
                for c in range(KC):
                    pe.matmul(o, xh[:, c, :], whi[:, c, :], start=(c == 0), stop=False)
                    pe.matmul(o, xh[:, c, :], wlo[:, c, :], start=False, stop=False)
                    mm = pe.matmul(o, xl[:, c, :], whi[:, c, :], start=False, stop=(c == KC - 1))
                return mm

            pe.wait_ge(x_hi, 1)
            pe.wait_ge(x_lo, 1)
            pe.wait_ge(text_norm, 1)
            for t in range(2):
                mm = project(0, psum[0][:, t * D:t * D + D], t)
            mm.then_inc(proj, 1)
            with pe.Fori(0, 8) as i:
                for k in range(4):
                    n = 4 * i + k + 1
                    pe.wait_ge(x_hi, n + 1)
                    pe.wait_ge(x_lo, n + 1)
                    pe.wait_ge(proj_out, n - 1)
                    bank = 2 * ((k + 1) % 2)
                    project(k + 1, psum[bank][:, 0:D], 0)
                    project(k + 1, psum[bank][:, D:2 * D], 1)
                    project(k + 1, psum[bank + 1][:, 0:D], 2).then_inc(proj, 1)
            pe.wait_ge(urow_in, 48)
            pe.wait_ge(proj_out, 33)
            for third in range(3):
                pe.wait_ge(u_lo, 8 * (third + 1))
                with pe.Fori(0, 4) as i:
                    for gg in range(2):
                        pe.wait_ge(toep_in[gg], 48 * (i + 4 * third + 1))
                        for half in range(2):
                            e = 2 * gg + half
                            pe.wait_ge(conv_free, 4 * i + 16 * third + e + 1)
                            for cc in range(4):
                                c = 4 * half + cc
                                th = toep[:, gg, 2 * c * KP:2 * c * KP + TAPW]
                                tl = toep[:, gg, (2 * c + 1) * KP:(2 * c + 1) * KP + TAPW]
                                ch = 16 * i + 8 * gg + c
                                uh = uhi[:, third % 2, ds(ch, 1), :].rearrange("p a q -> p (a q)")
                                ul = ulo[:, third % 2, ds(ch, 1), :].rearrange("p a q -> p (a q)")
                                uh0 = uhi[:, third % 2, ds(ch, 1), 0:B].rearrange("p a q -> p (a q)")
                                ul0 = ulo[:, third % 2, ds(ch, 1), 0:B].rearrange("p a q -> p (a q)")
                                uc = urow[:, ds(64 * third + ch, 1)].to_broadcast([128, B])
                                o = psum[e][:, cc * 128:cc * 128 + 128]
                                o0, o1 = psum[e][:, cc * 128:cc * 128 + B], psum[e][:, cc * 128 + B:cc * 128 + 128]
                                kw = dict(start=False, stop=False, skip_group_check=True)
                                pe.matmul(o, th[:, 0:128], uh, start=(cc == 0), stop=False, skip_group_check=True)
                                pe.matmul(o, th[:, 0:128], ul, **kw)
                                pe.matmul(o, tl[:, 0:128], uh, **kw)
                                pe.matmul(o1, th[:, 128:256], uh0, **kw)
                                pe.matmul(o1, th[:, 128:256], ul0, **kw)
                                pe.matmul(o1, tl[:, 128:256], uh0, **kw)
                                pe.matmul(o0, ctap[:, gg, c, 0:128], uc, **kw)
                                mm = pe.matmul(o1, ctap[:, gg, c, 128:256], uc, start=False, stop=True, skip_group_check=True)
                            mm.then_inc(conv, 1)
            pe.wait_ge(conv_free, 4 + CONV_STEPS)
            pe.wait_ge(d_split, 3)
            pe.wait_ge(low_split, 3)
            with pe.Fori(0, 8) as g:
                pe.wait_ge(z_norm, g + 1)
                pe.wait_ge(routed, g)
                for t in range(9):
                    if t < 8:
                        if t >= 2:
                            pe.wait_ge(z_hi, g * 8 + t - 1)
                            pe.wait_ge(z_lo, g * 8 + t - 1)
                        for tile in range(2):
                            for c in range(2):
                                mm = pe.transpose(psum[t % 2][0:HC, (2 * tile + c) * 128:(2 * tile + c) * 128 + 128],
                                                  ztok[:, 2 * t + tile, c * HC:c * HC + HC], ident[:, :])
                        mm.then_inc(z_t, 1)
                    if t >= 1:
                        pe.wait_ge(z_hi, g * 8 + t)
                        pe.wait_ge(z_lo, g * 8 + t)
                        for tile in range(2):
                            at = E4 * (2 * (t - 1) + tile)
                            o = psum[2][:, at:at + E4]
                            zh, zl = zthi[0:HC, (t - 1) % 2, tile], ztlo[0:HC, (t - 1) % 2, tile]
                            for c in range(2):
                                pe.matmul(o, zh[:, c], rwhi[0:HC, c], start=(c == 0), stop=False)
                                pe.matmul(o, zh[:, c], rwlo[0:HC, c], start=False, stop=False)
                                mm = pe.matmul(o, zl[:, c], rwhi[0:HC, c], start=False, stop=(c == 1))
                        mm.then_inc(z_log, 1)
                pe.wait_ge(z_pick, g + 1)
                picks = onehot.rearrange("p a b -> p (a b)")
                pe.matmul(psum[3][:, 0:64], ltri, picks, start=True, stop=True)
                pe.matmul(psum[3][:, 64:128], onesm, picks, start=True, stop=True).then_inc(z_rank, 1)
            pe.wait_ge(table_out, 1)

            def transposes(src, bank, s_done):
                for tile in range(2):
                    for c in range(2):
                        mm = pe.transpose(psum[bank][0:HC, (2 * tile + c) * 128:(2 * tile + c) * 128 + 128],
                                          src[:, tile, c * HC:c * HC + HC], ident[:, :])
                mm.then_inc(s_done, 1)

            def experts(n):
                return [pe.value_load(table[0:1, 1, ds(2 * n + tile, 1)], min_val=0, max_val=2 * E4 - 2) for tile in range(2)]

            def layer(es, hi, lo, wh, wl, bank, s_done):
                for tile, e2 in enumerate(es):
                    o = psum[bank][:, tile * D:tile * D + D]
                    for c in range(2):
                        K = HC + c
                        w_h = wh[0:K, ds(e2 + c, 1), :].rearrange("p a d -> p (a d)")
                        w_l = wl[0:K, ds(e2 + c, 1), :].rearrange("p a d -> p (a d)")
                        pe.matmul(o, hi[0:K, tile, c], w_h, start=(c == 0), stop=False)
                        pe.matmul(o, hi[0:K, tile, c], w_l, start=False, stop=False)
                        mm = pe.matmul(o, lo[0:K, tile, c], w_h, start=False, stop=(c == 1))
                mm.then_inc(s_done, 1)

            def step(n, k, first, last):
                if not last:
                    pe.wait_ge(x2_done, n + 1)
                    if first is None or n >= 2:
                        pe.wait_ge(hi1_done, n - 1)
                        pe.wait_ge(lo1_done, n - 1)
                    transposes(x2[:, k % 2], k % 2, t1_done)
                if (first is None or n >= 1) and (not last or n - 1 < STEPS):
                    es = experts(n - 1)
                    pe.wait_ge(hi1_done, n)
                    pe.wait_ge(lo1_done, n)
                    if first is None or n >= 3:
                        pe.wait_ge(act_done, n - 2)
                    j = (k - 1) % 2
                    layer(es, xthi[:, j], xtlo[:, j], w1hi, w1lo, 2 + j, l1_done)
                if (first is None or n >= 2) and (not last or n - 2 < STEPS):
                    pe.wait_ge(act_done, n - 1)
                    if first is None or n >= 4:
                        pe.wait_ge(hi2_done, n - 3)
                        pe.wait_ge(lo2_done, n - 3)
                    j = k % 2
                    transposes(act1[:, j], 4 + j, t2_done)
                if first is None or n >= 3:
                    es = experts(n - 3)
                    pe.wait_ge(hi2_done, n - 2)
                    pe.wait_ge(lo2_done, n - 2)
                    if first is None or n >= 5:
                        pe.wait_ge(fin_done, n - 4)
                    j = (k - 3) % 2
                    layer(es, gthi[:, j], gtlo[:, j], w2hi, w2lo, 6 + j, l2_done)

            for n in range(6):
                step(n, n, True, False)
            with pe.Fori(0, STEPS // 6 - 1) as i:
                for k in range(6):
                    step(6 * i + k + 6, k, None, False)
            for n in range(STEPS, STEPS + 3):
                step(n, n % 6, None, True)

        @block.vector
        def _(dve):
            count = [0]

            def link(ins):
                count[0] += 1
                ins.then_inc(v, 1)
                dve.wait_ge(v, count[0])

            def deviation(chain, st, var, mu, tmp, inv, eps, answered):
                st2 = [st[:, :, i] for i in range(6)]
                chain(dve.tensor_tensor(mu, st2[1], st2[4], ALU.add))
                chain(dve.tensor_scalar(mu, mu, 0.5, None, ALU.mult))
                chain(dve.tensor_tensor(var, st2[1], st2[4], ALU.subtract))
                chain(dve.scalar_tensor_tensor(out=var, in0=var, scalar=0.25, in1=var, op0=ALU.mult, op1=ALU.mult))
                chain(dve.tensor_tensor(tmp, st2[2], st2[5], ALU.add))
                chain(dve.scalar_tensor_tensor(out=var, in0=tmp, scalar=1.0 / D, in1=var, op0=ALU.mult, op1=ALU.add))
                dve.tensor_scalar(var, var, eps, None, ALU.add).then_inc(ask, 1)
                dve.wait_ge(act_chain, answered)
                chain(dve.reciprocal(inv, tmp))
                for _ in range(2):
                    chain(dve.tensor_tensor(tmp, inv, inv, ALU.mult))
                    chain(dve.tensor_tensor(tmp, tmp, var, ALU.mult))
                    chain(dve.tensor_scalar(tmp, tmp, -0.5, 1.5, ALU.mult, ALU.add))
                    chain(dve.tensor_tensor(inv, inv, tmp, ALU.mult))

            dve.wait_ge(const_in, 16 * 18)
            dve.wait_ge(act_chain, 1)
            dve.scalar_tensor_tensor(out=wlo, in0=wraw, scalar=WS, in1=whi, op0=ALU.mult, op1=ALU.subtract).then_inc(w_split, 1)
            link(dve.tensor_tensor(posb[:, 0:5, :], posb[:, 0:5, :], tokb.unsqueeze(1).to_broadcast([128, 5, D]), ALU.add))

            for layer in range(2):
                dve.wait_ge(pe_filter, layer + 1)
                link(dve.tensor_scalar(ang[0:16], psum[0][0:16, 0:L], fb[0:16, layer:layer + 1], fb[0:16, 2:3],
                                       ALU.add, ALU.mult))
                link(dve.tensor_scalar(red[0:16], ang[0:16], 1 / (2 * PI), MAGIC, ALU.mult, ALU.add))
                link(dve.tensor_scalar(red[0:16], red[0:16], -MAGIC, None, ALU.add))
                for part in (PI2A, PI2B, PI2C):
                    link(dve.scalar_tensor_tensor(out=ang[0:16], in0=red[0:16], scalar=-part, in1=ang[0:16],
                                                  op0=ALU.mult, op1=ALU.add))
                dve.tensor_scalar(red[0:16], ang[0:16], 3.1415925, -3.1415925, ALU.min, ALU.max).then_inc(ask, 1)
            link(dve.memset(taphl[0:96].rearrange("p a b c -> p (a b c)").bitcast(F32), 0.0))
            dve.wait_ge(act_chain, 3)
            link(dve.tensor_scalar(cb[0:96, :, 1], cb[0:96, :, 1], -1.0, None, ALU.mult))
            dve.tensor_scalar(cb[0:96, :, 2], cb[0:96, :, 2], CONV_BIAS, None, ALU.mult).then_inc(ask, 1)
            dve.wait_ge(act_chain, 5)
            dve.wait_ge(pe_filter, 4)
            for half, decay in ((0, ang), (1, red)):
                t = tap[0:96, half, :]
                link(dve.scalar_tensor_tensor(out=t, in0=psum[1 + half][0:96, 0:L], scalar=cb[0:96, half, 0:1],
                                              in1=decay[0:96], op0=ALU.add, op1=ALU.mult))
                link(dve.tensor_scalar(t, t, KS, None, ALU.mult))
                link(dve.tensor_tensor(t[:, 0:1], t[:, 0:1], cb[0:96, half, 2:3], ALU.add))
                link(dve.tensor_copy(taphl[0:96, half, 0, 128:128 + L], t))
                dve.tensor_tensor(taphl[0:96, half, 1, 128:128 + L], t, taphl[0:96, half, 0, 128:128 + L],
                                  ALU.subtract).then_inc(dve_filter, 1)
            dve.wait_ge(dve_filter, 2)

            c0, cu, ck, cp = (ucls[0:1, i, :] for i in range(4))
            dve.tensor_tensor(c0, c0, cp, ALU.add).then_inc(cls_sum, 1)
            dve.wait_ge(cls_sum, 1)
            link(dve.bn_stats(cls6[0:1, 0:6], c0))
            deviation(link, cls6[0:1, 0:6].unsqueeze(1), clsm[0:1, 1:2], clsm[0:1, 0:1], clsm[0:1, 2:3],
                      clsm[0:1, 3:4], LN_EPS, 6)
            link(dve.tensor_scalar(cu, c0, clsm[0:1, 0:1], clsm[0:1, 3:4], ALU.subtract, ALU.mult))
            link(dve.tensor_scalar(uclh[0:1, 0, :], cu, US, None, ALU.mult))
            dve.scalar_tensor_tensor(out=uclh[0:1, 1, :], in0=cu, scalar=US, in1=uclh[0:1, 0, :], op0=ALU.mult,
                                     op1=ALU.subtract).then_inc(cls_split, 1)
            dve.wait_ge(tap0_in, 16)
            link(dve.tensor_tensor(ck, ck, cu, ALU.mult))
            dve.scalar_tensor_tensor(out=cp, in0=ck, scalar=CONV_OUT * US, in1=c0, op0=ALU.mult, op1=ALU.add).then_inc(cls_out, 1)

            dve.wait_ge(cls_out, 1)
            link(dve.tensor_scalar(tmask[:, 0, :], lenp, spart, None, ALU.subtract))
            link(dve.tensor_scalar(tmask[:, 1, :], tmask[:, 0, :], 6.0, None, ALU.is_gt))
            link(dve.tensor_scalar(tmask[:, 2, :], tmask[:, 0, :], 1.0, None, ALU.is_gt))
            link(dve.tensor_tensor(tmask[:, 2, :], tmask[:, 2, :], tmask[:, 1, :], ALU.subtract))
            for half in range(2):
                dve.wait_ge(text_in, 48 + 32 * half)
                if half:
                    dve.wait_ge(text_mm, 8)
                a3 = amat.rearrange("p (a b) -> p a b", b=32)
                link(dve.tensor_tensor(a3, lenrep.rearrange("p (a b) -> p a b", b=32),
                                       s32.unsqueeze(1).to_broadcast([128, 32, 32]), ALU.subtract))
                link(dve.tensor_scalar(amat, amat, 6.0, 0.2, ALU.is_equal, ALU.mult))
                for k in range(8):
                    ak = amat[:, k * 128:k * 128 + 128]
                    kk = half * 8 + k
                    link(dve.scalar_tensor_tensor(out=ak, in0=blk, scalar=tmask[:, 2, kk:kk + 1], in1=ak,
                                                  op0=ALU.mult, op1=ALU.mult))
                    link(dve.scalar_tensor_tensor(out=ak, in0=ident[:, :], scalar=tmask[:, 1, kk:kk + 1], in1=ak,
                                                  op0=ALU.mult, op1=ALU.add))
                link(dve.tensor_tensor(coef[0:4].rearrange("p (a b) -> p a b", b=32),
                                       coefi[0:4].rearrange("p (a b) -> p a b", b=32),
                                       s32v[0:4].unsqueeze(1).to_broadcast([4, 32, 32]), ALU.subtract))
                dve.tensor_scalar(coef[0:4], coef[0:4], tgt[0:4, 0:1], tgt[0:4, 1:2], ALU.max,
                                  ALU.is_equal).then_inc(text_mat, 1)
            for k in range(8):
                dve.wait_ge(text_mm, 2 * k + 2)
                link(dve.tensor_tensor(we[:, 2 * k:2 * k + 2, :], bank3(k, 2, D),
                                       posb[:, 5:6, :].to_broadcast([128, 2, D]), ALU.add))
            for k in range(16):
                ins = dve.bn_stats(stats[:, k, :], we[:, k, :])
            link(ins)
            deviation(link, stats[:, 0:16, :], s1[:, 0:16], mean[:, 0:16], s2[:, 0:16], rstd[:, 0:16], TXT_EPS, 7)
            for k in range(16):
                ins = dve.tensor_scalar(we[:, k, :], we[:, k, :], mean[:, k:k + 1], rstd[:, k:k + 1], ALU.subtract, ALU.mult)
            ins.then_inc(text_norm, 1)

            SC = 1 / (XS * WS)

            def second(n, slot, turn, width):
                dve.wait_ge(x_in[slot], 16 * turn)
                dve.wait_ge(x_hi, n + 1)
                dve.scalar_tensor_tensor(out=xlo[:, slot % 2, :, 0:width], in0=xin[:, slot, :, 0:width], scalar=XS,
                                         in1=xhi[:, slot % 2, :, 0:width], op0=ALU.mult, op1=ALU.subtract).then_inc(x_lo, 1)

            def tokens(n, k):
                dve.wait_ge(proj, n + 1)
                b = 2 * (n - 1)
                o0, o1 = bank3(2 * (k % 2), 2, D), psum[2 * (k % 2) + 1][:, 0:D]
                dve.scalar_tensor_tensor(out=h[:, ds(b, 2), 0:D], in0=o0, scalar=SC, in1=posb[:, 0:2, :],
                                         op0=ALU.mult, op1=ALU.add)
                dve.scalar_tensor_tensor(out=h[0:64, ds(b + B, 1), 0:D].rearrange("p a c -> p (a c)"), in0=o1[0:64],
                                         scalar=SC, in1=posb[0:64, 2, :], op0=ALU.mult, op1=ALU.add)
                dve.scalar_tensor_tensor(out=h[0:64, ds(b + B + 1, 1), 0:D].rearrange("p a c -> p (a c)"), in0=o1[64:128],
                                         scalar=SC, in1=posb[64:128, 2, :], op0=ALU.mult, op1=ALU.add).then_inc(proj_out, 1)
                dve.wait_ge(proj_out, n + 1)
                for t in range(2):
                    ins = dve.bn_stats(stats[:, ds(b + t, 1), :].rearrange("p a c -> p (a c)"),
                                       h[:, ds(b + t, 1), 0:D].rearrange("p a c -> p (a c)"))
                return ins

            second(0, 0, 1, 256)
            second(1, 1, 1, 384)
            dve.wait_ge(proj, 1)
            dve.scalar_tensor_tensor(out=lout, in0=bank3(0, 2, D), scalar=SC, in1=posb[:, 3:5, :], op0=ALU.mult,
                                     op1=ALU.add).then_inc(proj_out, 1)
            with dve.Fori(0, 7) as i:
                for k in range(4):
                    n = 4 * i + k + 1
                    dve.wait_ge(proj, n)
                    second(n + 1, (k + 2) % 4, i + (2 if k >= 2 else 1), 384)
                    tokens(n, k + 1)
            for n in range(29, 33):
                if n < 32:
                    dve.wait_ge(proj, n)
                    second(n + 1, (n + 1) % 4, (n + 1) // 4 + 1, 384)
                tokens(n, n % 4)
            dve.wait_ge(urow_in, 48)
            dve.wait_ge(h_in, 16 * 9)
            with dve.Fori(0, 8) as i:
                for k in range(8):
                    ins = dve.bn_stats(stats[:, ds(8 * i + k + B, 1), :].rearrange("p a c -> p (a c)"),
                                       h[:, ds(8 * i + k + B, 1), 0:D].rearrange("p a c -> p (a c)"))
                ins.then_inc(stat2, 1)
            dve.wait_ge(stat2, 8)
            deviation(link, stats, s1[:, :], mean[:, :], s2[:, :], rstd[:, :], LN_EPS, 8)
            dve.tensor_scalar(s2[:, :], rstd[:, :], US, None, ALU.mult).then_inc(a_done, 1)
            dve.wait_ge(a_done, 1)
            dve.wait_ge(proj, 33)

            def normalise(third, i, k):
                for t in range(16):
                    q = 32 * i + 16 * k + t
                    ins = dve.tensor_scalar(utmp[:, k, t, :], h[:, ds(q, 1), 64 * third:64 * third + 64].rearrange("p a c -> p (a c)"),
                                            mean[:, ds(q, 1)], s2[:, ds(q, 1)], ALU.subtract, ALU.mult)
                ins.then_inc(u_norm, 1)

            def split(third, i, k):
                dve.wait_ge(u_norm, 8 * third + 2 * i + k + 1)
                dve.wait_ge(u_hi, 8 * third + 2 * i + k + 1)
                q = ds(32 * i + 16 * k, 16)
                hi = uhi[:, third % 2, :, q].rearrange("p c q -> p q c")
                lo = ulo[:, third % 2, :, q].rearrange("p c q -> p q c")
                dve.tensor_tensor(lo, utmp[:, k], hi, ALU.subtract).then_inc(u_lo, 1)

            def add_channels(third, i, j):
                dve.wait_ge(conv, 16 * third + 4 * i + j + 1)
                hc = h[:, :, ds(64 * third + 16 * i + 4 * j, 4)].rearrange("p q c -> p c q")
                dve.scalar_tensor_tensor(out=hc, in0=bank3(j, 4, NQ), scalar=CONV_OUT, in1=hc, op0=ALU.mult,
                                         op1=ALU.add).then_inc(conv_free, 1)

            dve.sem_inc(conv_free, 4)
            with dve.Fori(0, 4) as i:
                for k in range(2):
                    normalise(0, i, k)
                    split(0, i, k)
            for third in range(1, 3):
                with dve.Fori(0, 4) as i:
                    for k in range(2):
                        normalise(third, i, k)
                        add_channels(third - 1, i, 2 * k)
                        add_channels(third - 1, i, 2 * k + 1)
                        if third == 2 and k == 0:
                            dve.wait_ge(conv, 16)
                        split(third, i, k)
            with dve.Fori(0, 4) as i:
                for j in range(4):
                    add_channels(2, i, j)

            dve.wait_ge(conv_free, 4 + CONV_STEPS)
            dve.wait_ge(conv, CONV_STEPS)
            link(dve.memset(onesm, 1.0))
            for e in range(2):
                link(dve.tensor_copy(run[:, e, :], regbase))
            dve.wait_ge(d_in, 96)
            for n, (wl, raw, wh, K) in enumerate(((rwlo, rwraw, rwhi, HC), (w1lo, w1raw, w1hi, HC + 1), (w2lo, w2raw, w2hi, HC + 1))):
                dve.wait_ge(d_split, n + 1)
                dve.scalar_tensor_tensor(out=wl[0:K], in0=raw[0:K], scalar=WS, in1=wh[0:K], op0=ALU.mult,
                                         op1=ALU.subtract).then_inc(low_split, 1)
            dve.wait_ge(cls_in, 16)
            hrow = h[:, :, ROWID:ROWID + 1].bitcast(I32)
            link(dve.tensor_copy(hrow, rowid[:, :].unsqueeze(2)))
            PER = 39
            with dve.Fori(0, 8) as g:
                n1 = [0]

                def chain(ins):
                    n1[0] += 1
                    ins.then_inc(v1, 1)
                    dve.wait_ge(v1, g * PER + n1[0])

                q0 = 16 * g
                for t in range(16):
                    ins = dve.bn_stats(rstats[:, t, :], h[:, ds(q0 + t, 1), 0:D].rearrange("p a c -> p (a c)"))
                chain(ins)
                mu, inv = mean[:, 0:16], rstd[:, 0:16]
                deviation(chain, rstats, s1[:, 0:16], mu, s2[:, 0:16], inv, LN_EPS, g + 9)
                dve.tensor_copy(h[:, ds(q0, 16), MEAN:MEAN + 1], mu.unsqueeze(2))
                dve.tensor_copy(h[:, ds(q0, 16), RSTD:RSTD + 1], inv.unsqueeze(2))
                for t in range(16):
                    ins = dve.tensor_scalar(ztok[:, t, :], h[:, ds(q0 + t, 1), 0:D].rearrange("p a c -> p (a c)"),
                                            mean[:, t:t + 1], rstd[:, t:t + 1], ALU.subtract, ALU.mult)
                ins.then_inc(z_norm, 1)
                for t in range(8):
                    dve.wait_ge(z_hi, g * 8 + t + 1)
                    if t >= 2:
                        dve.wait_ge(z_log, g * 8 + t - 1)
                    dve.scalar_tensor_tensor(out=flat(ztlo[0:HC, t % 2]), in0=psum[t % 2][0:HC, :],
                                             scalar=US, in1=flat(zthi[0:HC, t % 2]), op0=ALU.mult, op1=ALU.subtract).then_inc(z_lo, 1)
                dve.wait_ge(z_log, g * 8 + 8)
                w = [128, 16, E4]
                chain(dve.scalar_tensor_tensor(out=logit, in0=bank3(2, 16, E4), scalar=1 / (US * WS),
                                               in1=rbias.unsqueeze(1).to_broadcast(w), op0=ALU.mult, op1=ALU.add))
                chain(dve.tensor_reduce(rmax, logit, AX, ALU.max))
                dve.tensor_tensor(logit, logit, rmax.unsqueeze(2).to_broadcast(w), ALU.subtract).then_inc(ask, 1)
                dve.wait_ge(z_exp, g + 1)
                chain(dve.tensor_reduce(rsum, prob, AX, ALU.add))
                chain(dve.reciprocal(rsum, rsum))
                chain(dve.tensor_tensor(prob, prob, rsum.unsqueeze(2).to_broadcast(w), ALU.mult))
                chain(dve.tensor_reduce(rmax, prob, AX, ALU.max))
                chain(dve.tensor_tensor(pick, prob, rmax.unsqueeze(2).to_broadcast(w), ALU.is_equal))
                chain(dve.tensor_tensor(pick, pick, pickw.unsqueeze(1).to_broadcast(w), ALU.mult))
                chain(dve.tensor_reduce(rmax, pick, AX, ALU.max))
                chain(dve.tensor_tensor(pick, pick, rmax.unsqueeze(2).to_broadcast(w), ALU.is_equal))
                chain(dve.tensor_scalar(rmax, piota.to_broadcast([128, 16]), CLS + 0.5, None, ALU.is_gt))
                chain(dve.tensor_scalar(rmax, rmax, tilej[:, ds(g, 1)], None, ALU.mult))
                chain(dve.tensor_scalar(rsum, rmax, -1.0, 1.0, ALU.mult, ALU.add))
                chain(dve.tensor_tensor(pick, pick, rsum.unsqueeze(2).to_broadcast(w), ALU.mult))
                dve.tensor_copy(onehot, pick).then_inc(z_pick, 1)
                dve.wait_ge(z_rank, g + 1)
                total = psum[3][:, 64:128].rearrange("p (a b) -> p a b", b=E4)
                chain(dve.tensor_copy(prob, total))
                chain(dve.memset(logit, 1.0))
                for e in range(E4):
                    ins = dve.tensor_tensor_scan(rank[:, :, e], logit[:, :, e], prob[:, :, e], run[:, 0, e:e + 1],
                                                 ALU.mult, ALU.add)
                chain(ins)
                dve.tensor_copy(run[:, 1, :], rank[:, 15, :])
                chain(dve.tensor_tensor(prob, rank, prob, ALU.subtract))
                chain(dve.tensor_tensor(prob, prob, bank3(3, 16, E4), ALU.add))
                chain(dve.tensor_tensor(prob, prob, pick, ALU.mult))
                chain(dve.tensor_reduce(destf, prob, AX, ALU.add))
                chain(dve.scalar_tensor_tensor(out=destf, in0=rmax, scalar=float(1 << 20), in1=destf, op0=ALU.mult, op1=ALU.add))
                chain(dve.tensor_copy(run[:, 0, :], run[:, 1, :]))
                dve.tensor_copy(dest[:, ds(q0, 16)], destf).then_inc(routed, 1)
                assert n1[0] == PER, n1[0]

            n2 = [0]

            def tlink(ins):
                n2[0] += 1
                ins.then_inc(v2, 1)
                dve.wait_ge(v2, n2[0])

            dve.wait_ge(routed, 8)
            tlink(dve.tensor_scalar(destf[:, 0:4], run[:, 0, :], piota, None, ALU.add))
            tlink(dve.tensor_copy(padid[:, :], destf[:, 0:4]))
            tn = tabn[0:1, :]
            tlink(dve.tensor_tensor(tn[:, 0:4], run[0:1, 0, :], regbase[0:1], ALU.subtract))
            tlink(dve.tensor_scalar(tn[:, 0:4], tn[:, 0:4], 127.0, None, ALU.add))
            tlink(dve.tensor_copy(tabi[0:1, :], tn[:, 0:4]))
            tlink(dve.tensor_scalar(tabi[0:1, :], tabi[0:1, :], 7, None, ALU.logical_shift_right))
            tlink(dve.tensor_copy(tn[:, 0:4], tabi[0:1, :]))
            tlink(dve.tensor_copy(tn[:, 4:5], tn[:, 0:1]))
            for e in range(1, 4):
                tlink(dve.tensor_tensor(tn[:, 4 + e:5 + e], tn[:, 3 + e:4 + e], tn[:, e:e + 1], ALU.add))
            tlink(dve.tensor_scalar(tn[:, 8:12], tn[:, 0:4], -128.0, float(REGION), ALU.mult, ALU.add))
            f = [tabf[0:1, i, :] for i in range(4)]
            tlink(dve.tensor_scalar(f[0], f[3], 128.0, None, ALU.mult))
            tlink(dve.memset(f[1], 0.0))
            for e in range(3):
                tlink(dve.tensor_scalar(f[2], f[3], tn[:, 4 + e:5 + e], None, ALU.is_ge))
                tlink(dve.scalar_tensor_tensor(out=f[1], in0=f[2], scalar=2.0, in1=f[1], op0=ALU.mult, op1=ALU.add))
                tlink(dve.scalar_tensor_tensor(out=f[0], in0=f[2], scalar=tn[:, 8 + e:9 + e], in1=f[0], op0=ALU.mult, op1=ALU.add))
            tlink(dve.tensor_scalar(f[2], f[3], tn[:, 7:8], None, ALU.is_ge))
            tlink(dve.tensor_scalar(f[3], f[0], -1.0, float(DUMMY), ALU.mult, ALU.add))
            tlink(dve.tensor_tensor(f[3], f[3], f[2], ALU.mult))
            tlink(dve.tensor_tensor(f[0], f[0], f[3], ALU.add))
            tlink(dve.tensor_copy(table[0:1, 0, :], f[0]))
            tlink(dve.tensor_copy(table[0:1, 1, :], f[1]))
            for one, zero, val in ((xthi, xtlo, US), (gthi, gtlo, GS)):
                dve.memset(one[96:97].rearrange("p a b c d -> p (a b c d)"), val)
                ins = dve.memset(zero[96:97].rearrange("p a b c d -> p (a b c d)"), 0.0)
            ins.then_inc(table_out, 1)

            def norm(n, k):
                for t in range(2):
                    ins = dve.tensor_scalar(x2[:, k % 2, t, :], row[:, k, t, 0:D], row[:, k, t, MEAN:MEAN + 1],
                                            row[:, k, t, RSTD:RSTD + 1], ALU.subtract, ALU.mult)
                ins.then_inc(x2_done, 1)
                dve.wait_ge(x2_done, n + 1)
                dve.tensor_tensor(row[:, k, :, 0:D], row[:, k, :, 0:D], x2[:, k % 2], ALU.add).then_inc(r_done, 1)

            def low(n, k, bank, hi, lo, scale, s_hi, s_lo):
                dve.wait_ge(s_hi, n + 1)
                dve.scalar_tensor_tensor(out=flat(lo[0:HC, k % 2]), in0=psum[bank + k % 2][0:HC, :], scalar=scale,
                                         in1=flat(hi[0:HC, k % 2]), op0=ALU.mult, op1=ALU.subtract).then_inc(s_lo, 1)

            def final(n, k):
                dve.wait_ge(l2_done, n + 1)
                dve.wait_ge(r_done, n + 1)
                dve.scalar_tensor_tensor(out=res[:, k % 2], in0=bank3(6 + k % 2, 2, D), scalar=1 / (GS * WS),
                                         in1=row[:, k, :, 0:D], op0=ALU.mult, op1=ALU.add).then_inc(fin_done, 1)

            def step(n, k, it, first, last):
                if not last:
                    nxt = n + 1
                    if first is None or nxt >= 2:
                        dve.wait_ge(t1_done, nxt - 1)
                    if it is not None or nxt < STEPS:
                        kk = (k + 1) % 6
                        dve.wait_ge(row_in[kk], 32 * it + (32 if kk else 64) if it is not None else 32 * (nxt // 6 + 1))
                        norm(nxt, kk)
                    if first is None or n >= 2:
                        dve.wait_ge(l1_done, n - 1)
                    low(n, k, 0, xthi, xtlo, US, hi1_done, lo1_done)
                if (first is None or n >= 2) and (not last or n - 2 < STEPS):
                    if first is None or n >= 4:
                        dve.wait_ge(l2_done, n - 3)
                    low(n - 2, (k - 2) % 6, 4, gthi, gtlo, GS, hi2_done, lo2_done)
                if first is None or n >= 3:
                    kk = (k - 3) % 6
                    if first is None or n >= 5:
                        prev = (k - 5) % 6
                        if it is not None:
                            dve.wait_ge(row_out[prev], 32 * it + (32 if k == 5 else 0))
                        else:
                            dve.wait_ge(row_out[prev], 32 * ((n - 5) // 6 + 1))
                    final(n - 3, kk)

            dve.wait_ge(row_in[0], 32)
            norm(0, 0)
            for n in range(6):
                step(n, n, None, True, False)
            with dve.Fori(1, STEPS // 6 - 1) as i:
                for k in range(6):
                    step(6 * i + k, k, i, None, False)
            for n in range(STEPS - 6, STEPS + 3):
                step(n, n % 6, None, None, n >= STEPS)


_SHAPES = {
    "xt": ((PAIRS, 128, KC, 384), F32), "xl": ((128, KC, 256), F32), "wp": ((128, KC, D), F32), "tokb": ((128, D), F32),
    "pos": ((128, 6 * D), F32), "cls": ((1, D), F32), "pos0": ((1, D), F32), "ident": ((128, 128), F32),
    "blk": ((128, 128), F32), "small": ((128, 89), F32), "idsp": ((128, 16), I32), "lenp": ((128, 16), I32),
    "lenv": ((E4, 2048), I32), "rowid": ((128, NQ), I32), "trows": ((E4, D), F32), "gb": ((128, 2 * D), F32),
    "word": ((VOCAB, D), F32), "zt": ((3, L), F32), "tgrid": ((96, L), F32), "fw1": ((3, 16), F32),
    "fw2": ((16, 16), F32), "fw3": ((16, D), F32), "fb": ((16, 4), F32), "cb": ((96, 2, 3), F32),
    "rw": ((HC, 2, E4), F32), "w1": ((HC + 1, 2 * E4, D), F32), "w2": ((HC + 1, 2 * E4, D), F32),
    "padrow": ((128, RW), I32), "slots": ((1, SLOTS), F32), "ltri": ((128, 128), F16),
}


def _layout(i):
    import numpy as np
    f = np.float32
    g = lambda k: np.asarray(i[k])
    x = g("x").reshape(B, 3, 14, 16, 14, 16).transpose(1, 3, 5, 0, 2, 4).reshape(KC, 128, B, NPATCH)
    xt = np.empty((PAIRS, 128, KC, 3, 128), f)
    y = x.reshape(KC, 128, PAIRS, 2, NPATCH).transpose(2, 1, 0, 3, 4)
    xt[:, :, :, 0:2, :] = y[..., 0:128]
    xt[:, :, :, 2, 0:64] = y[:, :, :, 0, 128:192]
    xt[:, :, :, 2, 64:128] = y[:, :, :, 1, 128:192]
    xl = x[:, :, :, 192:196].transpose(1, 0, 3, 2).reshape(128, KC, 256)
    pt = g("L0_tok_pos_table")
    pos = np.zeros((128, 6, D), f)
    pos[:, 0] = pos[:, 1] = pt[1:129]
    pos[0:64, 2] = pos[64:128, 2] = pt[129:193]
    for n in range(4):
        pos[64 * (n % 2):64 * (n % 2) + 64, 3 + n // 2] = pt[193 + n]
    pos[:, 5] = np.concatenate([g("L0_txt_pos_emb")[0:TXT]] * 4)
    p = np.arange(128)
    small = np.zeros((128, 89), f)
    small[:, 0:32] = np.arange(32)
    small[0:2, 32:64] = np.arange(32)
    small[0:4, 64:66] = [[4, 5], [4, 4], [-1e9, 0], [-1e9, 1]]
    small[:, 66] = p % 32
    small[:, 68:72] = g("L0_ffn_router_b")
    small[:, 72:76] = [4, 3, 2, 1]
    small[:, 76:80] = np.arange(E4) * REGION
    small[:, 80] = p
    small[:, 85:89] = 1
    ln, mk = g("_lenS").astype(np.int32), g("mask_BS_i1_0").astype(np.int32)
    lenv = np.stack([np.repeat(ln, TXT)] * 2 + [mk.reshape(-1)] * 2)
    ids = g("x_txt").astype(np.int32).reshape(16, 128).T
    lenp = np.repeat(ln, TXT).reshape(16, 128).T
    rowid = np.zeros((128, NQ), np.int32)
    rowid[:, 0:B] = np.arange(B) * L + 1 + p[:, None]
    rowid[:, B:] = np.arange(B) * L + np.where(p == CLS, 0, 129 + p)[:, None]
    t = np.linspace(0, 1, L, dtype=f)
    w = f(2 * np.pi) * np.linspace(0, L - 1, L, dtype=f) / f(L)
    zt = np.stack([t, np.cos(f(1e-4) * w), -np.sin(f(1e-4) * w)]).astype(f)
    halves = lambda v: np.asarray(v).reshape(2, 96).T
    cb = np.stack([halves(g("L0_attn_b3")), halves(g("L0_attn_deltas_abs")), halves(g("L0_attn_bias"))], axis=2)
    fb = np.zeros((16, 4), f)
    fb[:, 0], fb[:, 1], fb[:, 2] = g("L0_attn_b1"), g("L0_attn_b2"), g("L0_attn_freq")

    def expert(w, b):
        r = np.zeros((HC + 1, E4, 2, D), f)
        r[0:HC] = w.reshape(E4, 2, HC, D).transpose(2, 0, 1, 3)
        r[HC, :, 1] = b
        return r.reshape(HC + 1, 2 * E4, D)

    padrow = np.zeros((128, RW), np.int32)
    padrow[:, ROWID] = 1 << 20
    word = g("L0_txt_word_emb")
    return {
        "xt": xt.reshape(PAIRS, 128, KC, 384), "xl": xl, "wp": g("L0_tok_W").reshape(KC, 128, D).transpose(1, 0, 2),
        "tokb": np.tile(g("L0_tok_b"), (128, 1)), "pos": pos.reshape(128, 6 * D), "cls": g("L0_tok_class_token").reshape(1, D),
        "pos0": pt[0:1], "ident": np.eye(128, dtype=f), "blk": np.kron(np.eye(4), np.ones((32, 32))).astype(f),
        "small": small, "idsp": ids, "lenp": lenp, "lenv": lenv, "rowid": rowid,
        "trows": np.stack([word[SEP], word[0], g("L0_txt_type_emb")[0], g("L0_txt_type_emb")[1]]),
        "gb": np.tile(np.concatenate([g("L0_txt_ln_gamma"), g("L0_txt_ln_beta")]), (128, 1)), "word": word,
        "zt": zt, "tgrid": np.tile(t, (96, 1)), "fw1": g("L0_attn_w1").T, "fw2": g("L0_attn_w2").T, "fw3": g("L0_attn_w3").T,
        "fb": fb, "cb": cb, "rw": g("L0_ffn_router_w").reshape(2, HC, E4).transpose(1, 0, 2),
        "w1": expert(g("L0_ffn_w1"), g("L0_ffn_b1")), "w2": expert(g("L0_ffn_w2"), g("L0_ffn_b2")),
        "padrow": padrow, "slots": np.arange(SLOTS, dtype=f).reshape(1, SLOTS), "ltri": np.triu(np.ones((128, 128)), 1).astype(np.float16),
    }


def kernel(**inputs):
    import numpy as np
    import concourse.bacc as bacc
    from concourse.bass_utils import run_bass_kernel_spmd as run

    nc = bacc.Bacc("TRN2", target_bir_lowering=False, num_devices=1)
    arrays, args = {}, {}
    for name, v in _layout(inputs).items():
        shape, dt = _SHAPES[name]
        v = np.ascontiguousarray(v)
        assert v.shape == shape and mybir.dt.from_np(v.dtype) == dt, (name, v.shape, v.dtype)
        arrays[f"in_{name}"] = v
        args[name] = nc.dram_tensor(f"in_{name}", shape, dt, kind="ExternalInput").ap()
    args["out"] = nc.dram_tensor("out_rows", (NTOK, D), F32, kind="ExternalOutput").ap()
    build(nc, args)
    r = run(nc, [arrays], core_ids=[0])
    return r.results[0]["out_rows"].reshape(B, L, D)
```

```python
import concourse.bass as bass
from concourse import mybir

F32 = mybir.dt.float32
F16 = mybir.dt.float16
I32 = mybir.dt.int32
U32 = mybir.dt.uint32
ALU = mybir.AluOpType
ACT = mybir.ActivationFunctionType
AX = mybir.AxisListType.X

B = 64
D = 192
NPATCH = 196
KC = 6
TXT = 32
L = 1 + NPATCH + TXT
NQ = 2 * B
CLS = L - 1 - 128
RW = D + 4
MEAN, RSTD, ROWID, NMR = D, D + 1, D + 2, D + 3
PAIRS = B // 2
VOCAB, SEP = 30522, 102
NTOK = B * L
E4 = 4
HC = 96
REGION = NTOK + 128
DUMMY = E4 * REGION
SLOTS = 120
STEPS = SLOTS // 2
RING = 12
RT = 32
RG = NQ // RT

XS, WS = 16.0, 256.0
US, GS = 1024.0, 512.0
KS = 1.0 / 16
CONV_OUT = 1.0 / (KS * US * 2 * L)
CONV_BIAS = KS * 2 * L

KP = 360
COPY = 2 * D * KP + 128
CG = 8
NG = D // CG
TC = 64
TAPW = 256
RUN = (2 * CG - 1) * KP + TAPW
LN_EPS, TXT_EPS = 1e-5, 1e-12
PI = 3.141592653589793
MAGIC = 12582912.0
PI2A, PI2B = 6.28125, 0.0019350051879882812
PI2C = 2 * PI - PI2A - PI2B


def build(nc, a):
    import contextlib
    ctx = contextlib.ExitStack()
    with ctx:
        def sb(name, shape, dt):
            return ctx.enter_context(nc.sbuf_tensor(name, shape, dt))

        def sem(name):
            return ctx.enter_context(nc.semaphore(name))

        out = a["out"]
        taps_dram = nc.dram_tensor("taps", (2, COPY), F16, kind="Internal").ap()
        tap0_dram = nc.dram_tensor("tap0", (D,), F32, kind="Internal").ap()
        sorted_dram = nc.dram_tensor("sorted_rows", (DUMMY + 128, RW), F32, kind="Internal").ap()

        h = sb("h", [128, NQ, RW], F32)
        ARENA = 104576
        arena = sb("arena", [128, ARENA // 4], F32)
        top = [0]

        def carve(shape, dt):
            n = 1
            for s in shape:
                n *= s
            size = (n * (2 if dt == F16 else 4) + 31) // 32 * 8
            v = arena[:, top[0]:top[0] + size]
            top[0] += size
            assert top[0] * 4 <= ARENA, (top[0] * 4, shape)
            if dt != F32:
                v = v.bitcast(dt)
            v = v[:, 0:n]
            if len(shape) == 2:
                v = v.rearrange("p (a b) -> p a b", b=shape[1])
            elif len(shape) == 3:
                v = v.rearrange("p (a b c) -> p a b c", b=shape[1], c=shape[2])
            elif len(shape) == 4:
                v = v.rearrange("p (a b c d) -> p a b c d", b=shape[1], c=shape[2], d=shape[3])
            return v

        xin = carve([4, KC, 384], F32)
        xhi = carve([2, KC, 384], F16)
        xlo = carve([2, KC, 384], F16)
        whi = carve([KC, D], F16)
        wlo = carve([KC, D], F16)
        posb = carve([6, D], F32)
        lout = carve([2, D], F32)
        tokb = lout[:, 0, :]
        uclh = carve([2, D], F16)
        idsp = carve([16], I32)
        lenp = carve([16], I32)
        tmask = carve([3, 16], F32)
        blk = carve([128], F32)
        trow = carve([D], F32)
        text_top = top[0]
        we = carve([16, D], F32)
        lenrep = carve([1024], I32)
        amat = carve([1024], F32)
        coef = carve([1024], F32)
        coefi = carve([1024], I32)
        stats = carve([NQ, 6], F32)
        top[0] = text_top
        wraw = carve([KC, D], F32)
        zt = carve([L], F32)
        tgrid = carve([L], F32)
        ang = carve([L], F32)
        red = carve([L], F32)
        sin1 = carve([L], F32)
        sin2 = carve([L], F32)
        tap = carve([2, L], F32)
        taphl = carve([2, 2, KP], F16)
        fw1 = carve([16], F32)
        fw2 = carve([16], F32)
        fw3 = carve([D], F32)
        fb = carve([4], F32)
        cb = carve([2, 3], F32)

        top[0] = 0
        uhi = carve([2, TC, NQ], F16)
        ulo = carve([2, TC, NQ], F16)
        toep = carve([2, RUN], F16)
        ctap = carve([2, CG, TAPW], F16)
        utmp = carve([2, 16, TC], F32)

        top[0] = 0
        ztok = carve([4, 2, D], F32)
        zthi = carve([2, 2, 2, 128], F16)
        ztlo = carve([2, 2, 2, 128], F16)
        rwraw = carve([2, E4], F32)
        rwhi = carve([2, E4], F16)
        rwlo = carve([2, E4], F16)
        logit = carve([RT, E4], F32)
        prob = carve([RT, E4], F32)
        pick = carve([RT, E4], F32)
        onehot = carve([RT, E4], F16)
        rank = carve([RT, E4], F32)
        rmax = carve([RT], F32)
        rsum = carve([RT], F32)
        run = carve([2, E4], F32)
        destf = carve([RT], F32)
        tabf = carve([4, SLOTS], F32)
        table = carve([2, SLOTS], I32)
        rstats = carve([RT, 6], F32)
        rnmr = carve([RT], F32)
        padrow = carve([RW], I32)
        ltri = carve([128], F16)
        onesm = carve([128], F16)
        w1raw = carve([E4 * 2, D], F32)
        w2raw = carve([E4 * 2, D], F32)
        w1hi = carve([E4 * 2, D], F16)
        w1lo = carve([E4 * 2, D], F16)
        w2hi = carve([E4 * 2, D], F16)
        w2lo = carve([E4 * 2, D], F16)
        row = h[:, 0:2 * RING, :].rearrange("p (k t) c -> p k t c", t=2)
        x2 = carve([4, 2, D], F32)
        xthi = carve([2, 2, 2, 128], F16)
        xtlo = carve([2, 2, 2, 128], F16)
        act1 = carve([2, 2, D], F32)
        gthi = carve([2, 2, 2, 128], F16)
        gtlo = carve([2, 2, 2, 128], F16)

        ident = sb("ident", [128, 128], F32)
        mean = sb("mean", [128, NQ], F32)
        rstd = sb("rstd", [128, NQ], F32)
        s1 = sb("s1", [128, NQ], F32)
        s2 = sb("s2", [128, NQ], F32)
        dest = sb("dest", [128, NQ], I32)
        rowid = sb("rowid", [128, NQ], I32)
        ucls = sb("ucls", [128, 4, D], F32)
        urow = sb("urow", [128, D], F16)
        cls6 = sb("cls6", [128, 8], F32)
        clsm = sb("clsm", [128, 4], F32)
        small = sb("small", [128, 96], F32)
        padid = sb("padid", [128, E4], I32)
        tabn = sb("tabn", [1, 24], F32)
        tabi = sb("tabi", [1, 4], I32)
        psum = [ctx.enter_context(nc.psum_tensor(f"bank{i}", [128, 512], F32)) for i in range(8)]
        s32, s32v, tgt, spart = small[:, 0:32], small[:, 32:64], small[:, 64:66], small[:, 66:67]
        vmask, rbias, pickw, regbase, piota = small[:, 67:68], small[:, 68:72], small[:, 72:76], small[:, 76:80], small[:, 80:81]
        tilej = small[:, 81:81 + RG]

        const_in = sem("const_in")
        x_in = [sem(f"x_in{i}") for i in range(4)]
        w_split = sem("w_split")
        x_hi, x_lo = sem("x_hi"), sem("x_lo")
        proj, proj_out = sem("proj"), sem("proj_out")
        act_chain = sem("act_chain")
        ask = sem("ask")
        pe_filter = sem("pe_filter")
        dve_filter = sem("dve_filter")
        v = sem("vector_chain")
        taps_out = sem("taps_out")
        tap0_in = sem("tap0_in")
        text_in = sem("text_in")
        gathered = sem("gathered")
        text_mat, text_mm, text_norm, text_affine, gb_in = (sem("text_mat"), sem("text_mm"), sem("text_norm"),
                                                            sem("text_affine"), sem("gb_in"))
        pchain = sem("pool_chain")
        rows_clear = sem("rows_clear")
        cls_sum = sem("cls_sum")
        h_in = sem("h_in")
        cls_split, urow_in = sem("cls_split"), sem("urow_in")
        zeroed = sem("zeroed")
        stat2 = sem("stat2")
        a_done = sem("a_done")
        u_norm, u_hi, u_lo = sem("u_norm"), sem("u_hi"), sem("u_lo")
        toep_in = [sem("toep_in0"), sem("toep_in1")]
        conv, conv_free = sem("conv"), sem("conv_free")
        cls_out, cls_in = sem("cls_out"), sem("cls_in")
        d_in = sem("d_in")
        d_split, low_split = sem("d_split"), sem("low_split")
        z_stat, z_t, z_hi, z_lo, z_log, z_rank = (sem("z_stat"), sem("z_t"), sem("z_hi"), sem("z_lo"), sem("z_log"),
                                                  sem("z_rank"))
        z_pick, z_exp, routed = sem("z_pick"), sem("z_exp"), sem("routed")
        v1 = sem("vector_chain_routing")
        v2 = sem("vector_chain_table")
        scattered, table_out, dummy_in = sem("scattered"), sem("table_out"), sem("dummy_in")
        stores_begun = sem("stores_begun")
        row_in = [sem(f"row_in{i}") for i in range(RING)]
        row_out = [sem(f"row_out{i}") for i in range(RING)]
        zn_act, zn_dve = sem("zn_act"), sem("zn_dve")
        x2_act, x2_dve, r_done, lo1_done, lo2_done, fin_done = (sem("x2_act"), sem("x2_dve"), sem("r_done"), sem("lo1_done"), sem("lo2_done"),
                                                         sem("fin_done"))
        t1_done, l1_done, t2_done, l2_done = sem("t1_done"), sem("l1_done"), sem("t2_done"), sem("l2_done")
        hi1_done, act_done, hi2_done = sem("hi1_done"), sem("act_done"), sem("hi2_done")
        block = ctx.enter_context(nc.Block())
        ds = bass.ds

        CONV_STEPS = D // 4

        def flat(t):
            return t.rearrange("p a b c -> p (a b c)")

        def bank3(i, n, m):
            return psum[i][:, 0:n * m].rearrange("p (a b) -> p a b", b=m)

        @block.sync
        def _(sp):
            wiring = [(ident[:, :], a["ident"]), (blk, a["blk"]), (small[:, :], a["small"]),
                      (idsp, a["idsp"]), (lenp, a["lenp"]), (rowid[:, :], a["rowid"]),
                      (posb.rearrange("p a b -> p (a b)"), a["pos"]), (tokb, a["tokb"]),
                      (wraw, a["wp"]),
                      (zt[0:3, :], a["zt"]), (tgrid[0:96, :], a["tgrid"]),
                      (fw1[0:3, :], a["fw1"]), (fw2[0:16, :], a["fw2"]), (fw3[0:16, :], a["fw3"]),
                      (fb[0:16, :], a["fb"]), (cb[0:96, :, :], a["cb"]),
                      (ucls[0:1, 0, :], a["cls"]), (ucls[0:1, 3, :], a["pos0"])]
            for dst, src in wiring:
                sp.dma_start(dst, src).then_inc(const_in, 16)
            sp.dma_start(xin[:, 0, :, 0:256], a["xl"]).then_inc(x_in[0], 16)
            for n in range(1, 4):
                sp.dma_start(xin[:, n, :, :], a["xt"][n - 1]).then_inc(x_in[n], 16)
            sp.wait_ge(dve_filter, 2)
            for half in range(2):
                for copy in range(2):
                    sp.dma_start(taps_dram[copy, half * 96 * 2 * KP:(half * 96 + 96) * 2 * KP].rearrange("(c x) -> c x", x=2 * KP),
                                 taphl[0:96, half, :, :].rearrange("p a b -> p (a b)")).then_inc(taps_out, 16)
                    if half:
                        sp.dma_start(taps_dram[copy:copy + 1, COPY - 128:COPY], taphl[0:1, 0, 0, 0:128]).then_inc(taps_out, 16)
                sp.dma_start(tap0_dram[half * 96:half * 96 + 96].unsqueeze(1), tap[0:96, half, 0:1]).then_inc(taps_out, 16)
            sp.wait_ge(taps_out, 16 * 8)
            sp.dma_start(ucls[0:1, 2, :], tap0_dram.unsqueeze(0)).then_inc(tap0_in, 16)
            sp.wait_ge(cls_out, 1)
            for half in range(2):
                if half:
                    sp.wait_ge(text_mat, 1)
                sp.dma_start(lenrep, a["lenv"][0:1, half * 1024:half * 1024 + 1024].to_broadcast([128, 1024])).then_inc(text_in, 16)
                sp.dma_start(coefi[0:E4, :], a["lenv"][:, half * 1024:half * 1024 + 1024]).then_inc(text_in, 16)
                if half == 0:
                    sp.dma_start(trow[0:E4, :], a["trows"]).then_inc(text_in, 16)
            sp.wait_ge(text_mm, 16)
            sp.dma_start(amat[:, 0:2 * D], a["gb"]).then_inc(gb_in, 16)
            sp.wait_ge(cls_sum, 1)
            sp.wait_ge(rows_clear, 1)
            sp.dma_start(h[CLS:CLS + 1, B:NQ, 0:D], ucls[0:1, 0:1, :].to_broadcast([1, B, D])).then_inc(h_in, 16)
            sp.wait_ge(cls_split, 1)
            sp.wait_ge(zeroed, 1)
            sp.dma_start(urow[0:1, :], uclh[0:1, 0, :]).then_inc(urow_in, 16)
            sp.dma_start(urow[1:2, :], uclh[0:1, 0, :]).then_inc(urow_in, 16)
            sp.dma_start(urow[2:3, :], uclh[0:1, 1, :]).then_inc(urow_in, 16)
            sp.wait_ge(proj_out, 1)
            for n in range(4):
                sp.dma_start(h[64 + n:65 + n, B:NQ, 0:D],
                             lout[64 * (n % 2):64 * (n % 2) + 64, n // 2, :]).then_inc(h_in, 16)
            with sp.Fori(0, 7) as i:
                for k in range(4):
                    sp.wait_ge(x_hi, 4 * i + k + 1)
                    sp.wait_ge(x_lo, 4 * i + k + 1)
                    sp.dma_start(xin[:, k, :, :], a["xt"][ds(4 * i + k + 3, 1)].rearrange("a p k t -> (a p) k t")).then_inc(x_in[k], 16)
            sp.wait_ge(x_hi, 29)
            sp.wait_ge(x_lo, 29)
            sp.dma_start(xin[:, 0, :, :], a["xt"][31]).then_inc(x_in[0], 16)
            sp.wait_ge(text_affine, 1)
            hj = h[:, B:NQ, :].rearrange("p (k b) c -> p k b c", b=4)
            for b4 in range(4):
                sp.dma_start(hj[68:100, :, b4, 0:D], we[32 * b4:32 * b4 + 32, :, :]).then_inc(h_in, 16)
            sp.wait_ge(a_done, 1)
            sp.wait_ge(zeroed, 2)
            sp.wait_ge(proj, 33)
            for g in range(NG):
                if g >= 2:
                    sp.wait_ge(conv, 2 * (g - 1))
                src = bass.AP(taps_dram.tensor, g * CG * 2 * KP + 128, [[COPY - 64, 2], [-1, 64], [1, RUN]])
                sp.dma_start(toep[:, g % 2], src).then_inc(toep_in[g % 2], 16)
                src = bass.AP(taps_dram.tensor, g * CG * 2 * KP + 129, [[KP, 2], [2 * KP, CG], [1, TAPW]])
                sp.dma_start(ctap[0:2, g % 2], src).then_inc(toep_in[g % 2], 16)
                src = bass.AP(taps_dram.tensor, g * CG * 2 * KP + 129, [[KP, 1], [2 * KP, CG], [1, TAPW]])
                sp.dma_start(ctap[2:3, g % 2], src).then_inc(toep_in[g % 2], 16)
            sp.wait_ge(cls_out, 1)
            sp.wait_ge(conv_free, 4 + CONV_STEPS)
            sp.dma_start(h[CLS:CLS + 1, B:NQ, 0:D], ucls[0:1, 3:4, :].to_broadcast([1, B, D])).then_inc(cls_in, 16)
            for dst, src in [(rwraw[0:HC], a["rw"]), (w1raw[0:HC + 1], a["w1"]), (w2raw[0:HC + 1], a["w2"]),
                             (padrow, a["padrow"]), (tabf[0:1, 3, :], a["slots"]), (ltri, a["ltri"])]:
                sp.dma_start(dst, src).then_inc(d_in, 16)
            sp.wait_ge(d_in, 96)
            sp.dma_start(sorted_dram[DUMMY:DUMMY + 128], padrow[:, 0:RW].bitcast(F32)).then_inc(dummy_in, 16)
            sp.wait_ge(dummy_in, 16)
            sp.wait_ge(scattered, 16 * (NQ + E4))
            sp.wait_ge(table_out, 1)

            def load_rows(s, k):
                for t in range(2):
                    start = sp.value_load(table[0:1, 0, ds(2 * s + t, 1)], min_val=0, max_val=DUMMY)
                    sp.dma_start(row[:, k, t, 0:RW], sorted_dram[ds(start, 128), :]).then_inc(row_in[k], 16)

            for s in range(RING):
                load_rows(s, s)
            with sp.Fori(0, STEPS // RING - 1) as i:
                for k in range(RING):
                    sp.wait_ge(row_out[k], 32 * i + 32)
                    load_rows(RING * i + RING + k, k)

        @block.gpsimd
        def _(pool):
            pool.memset(h[96:128, B:NQ, 0:D], 0.0).then_inc(rows_clear, 1)
            pool.wait_ge(rows_clear, 1)
            pool.memset(urow[:, :].bitcast(F32), 0.0).then_inc(zeroed, 1)
            pool.wait_ge(zeroed, 1)
            pool.wait_ge(const_in, 16 * 18)
            pool.wait_ge(cls_out, 1)
            for k in range(16):
                pool.indirect_dma_start(we[:, k, :], None, a["word"], bass.IndirectOffsetOnAxis(
                    ap=idsp[:, k:k + 1].bitcast(U32), axis=0)).then_inc(gathered, 16)
            pool.wait_ge(text_norm, 1)
            pool.wait_ge(gb_in, 16)
            gam = amat[:, 0:D].unsqueeze(1).to_broadcast([128, 16, D])
            bet = amat[:, D:2 * D].unsqueeze(1).to_broadcast([128, 16, D])
            pool.tensor_tensor(we, we, gam, ALU.mult).then_inc(pchain, 1)
            pool.wait_ge(pchain, 1)
            pool.tensor_tensor(we, we, bet, ALU.add).then_inc(text_affine, 1)
            pool.wait_ge(a_done, 1)
            pool.wait_ge(h_in, 16 * 9)
            pool.wait_ge(proj, 33)
            pool.memset(ctap.rearrange("p a c t -> p (a c t)").bitcast(F32), 0.0).then_inc(zeroed, 1)
            for g in range(RG):
                pool.wait_ge(routed, g + 1)
                for q in range(RT * g, RT * g + RT):
                    pool.indirect_dma_start(sorted_dram[:, :], bass.IndirectOffsetOnAxis(
                        ap=dest[:, q:q + 1].bitcast(U32), axis=0), h[:, q, 0:RW], None,
                        bounds_check=DUMMY - 1, oob_is_err=False).then_inc(scattered, 16)
            pool.wait_ge(table_out, 1)
            pool.wait_ge(d_in, 96)
            for e in range(E4):
                pool.indirect_dma_start(sorted_dram[:, :], bass.IndirectOffsetOnAxis(
                    ap=padid[:, e:e + 1].bitcast(U32), axis=0), padrow[:, 0:RW].bitcast(F32), None).then_inc(scattered, 16)

            def store_rows(s, k):
                pool.wait_ge(fin_done, s + 1)
                pool.sem_inc(stores_begun, 1)
                for t in range(2):
                    pool.indirect_dma_start(out[:, :], bass.IndirectOffsetOnAxis(
                        ap=row[:, k, t, ROWID:ROWID + 1].bitcast(U32), axis=0),
                        row[:, k, t, 0:D], None, bounds_check=NTOK - 1, oob_is_err=False).then_inc(row_out[k], 16)

            with pool.Fori(0, STEPS // RING) as i:
                for k in range(RING):
                    store_rows(RING * i + k, k)
            for k in range(RING):
                pool.wait_ge(row_out[k], 32 * STEPS // RING)

        @block.scalar
        def _(act):
            act.wait_ge(const_in, 16 * 18)
            act.activation(whi, wraw, ACT.Copy, scale=WS).then_inc(act_chain, 1)
            act.wait_ge(ask, 1)
            act.activation(sin1[0:16], red[0:16], ACT.Sin).then_inc(act_chain, 1)
            act.wait_ge(ask, 2)
            act.activation(sin2[0:16], red[0:16], ACT.Sin).then_inc(act_chain, 1)
            act.wait_ge(ask, 3)
            act.activation(ang[0:96], tgrid[0:96], ACT.Exp, scale=cb[0:96, 0, 1:2]).then_inc(act_chain, 1)
            act.activation(red[0:96], tgrid[0:96], ACT.Exp, scale=cb[0:96, 1, 1:2]).then_inc(act_chain, 1)
            act.wait_ge(ask, 4)
            act.activation(clsm[0:1, 2:3], clsm[0:1, 1:2], ACT.Sqrt).then_inc(act_chain, 1)
            act.wait_ge(ask, 5)
            act.activation(s2[:, 0:16], s1[:, 0:16], ACT.Sqrt).then_inc(act_chain, 1)
            act.wait_ge(x_in[0], 16)
            act.activation(xhi[:, 0, :, 0:256], xin[:, 0, :, 0:256], ACT.Copy, scale=XS).then_inc(x_hi, 1)

            def pixels(n, k, turn):
                act.wait_ge(x_in[k], 16 * turn)
                act.wait_ge(proj, n - 1)
                act.activation(xhi[:, k % 2], xin[:, k], ACT.Copy, scale=XS).then_inc(x_hi, 1)

            with act.Fori(0, 8) as i:
                for k in range(4):
                    n = 4 * i + k + 1
                    pixels(n, (k + 1) % 4, i + (2 if k == 3 else 1))
            act.wait_ge(ask, 6)
            act.activation(s2[:, :], s1[:, :], ACT.Sqrt).then_inc(act_chain, 1)
            for third in range(3):
                if third == 2:
                    act.wait_ge(conv, CONV_STEPS // 3)
                with act.Fori(0, 4) as i:
                    for k in range(2):
                        act.wait_ge(u_norm, 8 * third + 2 * i + k + 1)
                        dst = uhi[:, third % 2, :, ds(32 * i + 16 * k, 16)].rearrange("p c q -> p q c")
                        act.activation(dst, utmp[:, k], ACT.Copy).then_inc(u_hi, 1)
            act.wait_ge(d_in, 96)
            act.activation(rwhi[0:HC], rwraw[0:HC], ACT.Copy, scale=WS).then_inc(d_split, 1)
            act.activation(w1hi[0:HC + 1], w1raw[0:HC + 1], ACT.Copy, scale=WS).then_inc(d_split, 1)
            act.activation(w2hi[0:HC + 1], w2raw[0:HC + 1], ACT.Copy, scale=WS).then_inc(d_split, 1)
            with act.Fori(0, RG) as g:
                act.wait_ge(ask, g * 2 + 7)
                act.activation(s2[:, 0:RT], s1[:, 0:RT], ACT.Sqrt).then_inc(act_chain, 1)

                def znorm(t):
                    if t >= 4:
                        act.wait_ge(z_t, g * (RT // 2) + t - 3)
                    act.activation(ztok[:, t % 4, 0, :], h[:, ds(RT * g + 2 * t, 1), 0:D].rearrange("p a c -> p (a c)"),
                                   ACT.Identity, scale=rstd[:, 2 * t:2 * t + 1], bias=rnmr[:, 2 * t:2 * t + 1]).then_inc(zn_act, 1)

                act.wait_ge(z_stat, g + 1)
                znorm(0)
                for t in range(RT // 2):
                    if t + 1 < RT // 2:
                        znorm(t + 1)
                    act.wait_ge(z_t, g * (RT // 2) + t + 1)
                    if t >= 2:
                        act.wait_ge(z_log, g * (RT // 2) + t - 1)
                    act.activation(zthi[0:HC, t % 2], psum[t % 2][0:HC, :].rearrange("p (a b c) -> p a b c", a=2, b=2),
                                   ACT.Copy, scale=US).then_inc(z_hi, 1)
                act.wait_ge(ask, g * 2 + 8)
                act.activation(prob, logit, ACT.Exp).then_inc(z_exp, 1)

            def hi1(n, k):
                act.wait_ge(t1_done, n + 1)
                act.activation(xthi[0:HC, k % 2], psum[k % 2][0:HC, :].rearrange("p (a b c) -> p a b c", a=2, b=2),
                               ACT.Copy, scale=US).then_inc(hi1_done, 1)

            def gelu(n, k):
                act.wait_ge(l1_done, n + 1)
                act.activation(act1[:, k % 2], bank3(2 + k % 2, 2, D), ACT.Gelu, scale=1 / (US * WS)).then_inc(act_done, 1)

            def hi2(n, k):
                act.wait_ge(t2_done, n + 1)
                act.activation(gthi[0:HC, k % 2], psum[4 + k % 2][0:HC, :].rearrange("p (a b c) -> p a b c", a=2, b=2),
                               ACT.Copy, scale=GS).then_inc(hi2_done, 1)

            def norm(n, k, use):
                act.wait_ge(row_in[k], use)
                if not isinstance(n, int) or n >= 4:
                    act.wait_ge(t1_done, n - 3)
                    act.wait_ge(r_done, n - 3)
                act.activation(x2[:, k % 4, 0, :], row[:, k, 0, 0:D], ACT.Identity, scale=row[:, k, 0, RSTD:RSTD + 1],
                               bias=row[:, k, 0, NMR:NMR + 1]).then_inc(x2_act, 1)

            def step(n, k, it):
                inside = it is not None
                if inside or n + 1 < STEPS:
                    kk = (k + 1) % RING
                    norm(n + 1, kk, 32 * it + (64 if kk else 96) if inside else 32 * ((n + 1) // RING + 1))
                if inside or n < STEPS:
                    if inside or n >= 2:
                        act.wait_ge(l1_done, n - 1)
                    hi1(n, k)
                if inside or 1 <= n <= STEPS:
                    if inside or n >= 3:
                        act.wait_ge(t2_done, n - 2)
                    gelu(n - 1, (k - 1) % RING)
                if inside or 2 <= n:
                    if inside or n >= 4:
                        act.wait_ge(l2_done, n - 3)
                    hi2(n - 2, (k - 2) % RING)

            norm(0, 0, 32)
            for n in range(RING):
                step(n, n, None)
            with act.Fori(0, STEPS // RING - 2) as i:
                for k in range(RING):
                    step(RING * i + k + RING, k, i)
            for n in range(STEPS - RING, STEPS + 2):
                step(n, n % RING, None)

        @block.tensor
        def _(pe):
            pe.wait_ge(const_in, 16 * 18)
            pe.matmul(psum[0][0:16, 0:L], fw1[0:3, :], zt[0:3, :], start=True, stop=True).then_inc(pe_filter, 1)
            pe.wait_ge(act_chain, 2)
            pe.matmul(psum[0][0:16, 0:L], fw2[0:16, :], sin1[0:16, :], start=True, stop=True).then_inc(pe_filter, 1)
            pe.wait_ge(act_chain, 3)
            for half in range(2):
                pe.matmul(psum[1 + half][0:96, 0:L], fw3[0:16, half * 96:half * 96 + 96], sin2[0:16, :],
                          start=True, stop=True).then_inc(pe_filter, 1)
            pe.wait_ge(gathered, 256)
            for half in range(2):
                pe.wait_ge(text_mat, half + 1)
                for k in range(8):
                    o = psum[half * 4 + k // 2][:, (k % 2) * D:(k % 2) * D + D]
                    if half == 0 and k == 0:
                        pe.wait_ge(cls_out, 1)
                    pe.matmul(o, amat[:, k * 128:k * 128 + 128], we[:, half * 8 + k, :], start=True, stop=False)
                    pe.matmul(o, coef[0:E4, k * 128:k * 128 + 128], trow[0:E4, :], start=False, stop=True).then_inc(text_mm, 1)
            pe.wait_ge(w_split, 1)

            def project(k, o, t):
                xh, xl = xhi[:, k % 2, :, t * 128:t * 128 + 128], xlo[:, k % 2, :, t * 128:t * 128 + 128]
                for c in range(KC):
                    pe.matmul(o, xh[:, c, :], whi[:, c, :], start=(c == 0), stop=False)
                    pe.matmul(o, xh[:, c, :], wlo[:, c, :], start=False, stop=False)
                    mm = pe.matmul(o, xl[:, c, :], whi[:, c, :], start=False, stop=(c == KC - 1))
                return mm

            pe.wait_ge(x_hi, 1)
            pe.wait_ge(x_lo, 1)
            pe.wait_ge(text_norm, 1)
            for t in range(2):
                mm = project(0, psum[0][:, t * D:t * D + D], t)
            mm.then_inc(proj, 1)
            with pe.Fori(0, 8) as i:
                for k in range(4):
                    n = 4 * i + k + 1
                    pe.wait_ge(x_hi, n + 1)
                    pe.wait_ge(x_lo, n + 1)
                    pe.wait_ge(proj_out, n - 1)
                    bank = 2 * ((k + 1) % 2)
                    project(k + 1, psum[bank][:, 0:D], 0)
                    project(k + 1, psum[bank][:, D:2 * D], 1)
                    project(k + 1, psum[bank + 1][:, 0:D], 2).then_inc(proj, 1)
            pe.wait_ge(urow_in, 48)
            pe.wait_ge(proj_out, 33)
            for third in range(3):
                pe.wait_ge(u_lo, 8 * (third + 1))
                with pe.Fori(0, 4) as i:
                    for gg in range(2):
                        pe.wait_ge(toep_in[gg], 48 * (i + 4 * third + 1))
                        for half in range(2):
                            e = 2 * gg + half
                            pe.wait_ge(conv_free, 4 * i + 16 * third + e + 1)
                            for cc in range(4):
                                c = 4 * half + cc
                                th = toep[:, gg, 2 * c * KP:2 * c * KP + TAPW]
                                tl = toep[:, gg, (2 * c + 1) * KP:(2 * c + 1) * KP + TAPW]
                                ch = 16 * i + 8 * gg + c
                                uh = uhi[:, third % 2, ds(ch, 1), :].rearrange("p a q -> p (a q)")
                                ul = ulo[:, third % 2, ds(ch, 1), :].rearrange("p a q -> p (a q)")
                                uh0 = uhi[:, third % 2, ds(ch, 1), 0:B].rearrange("p a q -> p (a q)")
                                ul0 = ulo[:, third % 2, ds(ch, 1), 0:B].rearrange("p a q -> p (a q)")
                                uc = urow[:, ds(64 * third + ch, 1)].to_broadcast([128, B])
                                o = psum[e][:, cc * 128:cc * 128 + 128]
                                o0, o1 = psum[e][:, cc * 128:cc * 128 + B], psum[e][:, cc * 128 + B:cc * 128 + 128]
                                kw = dict(start=False, stop=False, skip_group_check=True)
                                pe.matmul(o, th[:, 0:128], uh, start=(cc == 0), stop=False, skip_group_check=True)
                                pe.matmul(o, th[:, 0:128], ul, **kw)
                                pe.matmul(o, tl[:, 0:128], uh, **kw)
                                pe.matmul(o1, th[:, 128:256], uh0, **kw)
                                pe.matmul(o1, th[:, 128:256], ul0, **kw)
                                pe.matmul(o1, tl[:, 128:256], uh0, **kw)
                                pe.matmul(o0, ctap[:, gg, c, 0:128], uc, **kw)
                                mm = pe.matmul(o1, ctap[:, gg, c, 128:256], uc, start=False, stop=True, skip_group_check=True)
                            mm.then_inc(conv, 1)
            pe.wait_ge(conv_free, 4 + CONV_STEPS)
            pe.wait_ge(d_split, 3)
            pe.wait_ge(low_split, 3)
            PT = RT // 2
            with pe.Fori(0, RG) as g:
                pe.wait_ge(routed, g)
                for t in range(PT + 1):
                    if t < PT:
                        pe.wait_ge(zn_act, g * PT + t + 1)
                        pe.wait_ge(zn_dve, g * PT + t + 1)
                        if t >= 2:
                            pe.wait_ge(z_hi, g * PT + t - 1)
                            pe.wait_ge(z_lo, g * PT + t - 1)
                        for tile in range(2):
                            for c in range(2):
                                mm = pe.transpose(psum[t % 2][0:HC, (2 * tile + c) * 128:(2 * tile + c) * 128 + 128],
                                                  ztok[:, t % 4, tile, c * HC:c * HC + HC], ident[:, :])
                        mm.then_inc(z_t, 1)
                    if t >= 1:
                        pe.wait_ge(z_hi, g * PT + t)
                        pe.wait_ge(z_lo, g * PT + t)
                        for tile in range(2):
                            at = E4 * (2 * (t - 1) + tile)
                            o = psum[2][:, at:at + E4]
                            zh, zl = zthi[0:HC, (t - 1) % 2, tile], ztlo[0:HC, (t - 1) % 2, tile]
                            for c in range(2):
                                pe.matmul(o, zh[:, c], rwhi[0:HC, c], start=(c == 0), stop=False)
                                pe.matmul(o, zh[:, c], rwlo[0:HC, c], start=False, stop=False)
                                mm = pe.matmul(o, zl[:, c], rwhi[0:HC, c], start=False, stop=(c == 1))
                        mm.then_inc(z_log, 1)
                pe.wait_ge(z_pick, g + 1)
                picks = onehot.rearrange("p a b -> p (a b)")
                pe.matmul(psum[3][:, 0:E4 * RT], ltri, picks, start=True, stop=True)
                pe.matmul(psum[3][:, E4 * RT:2 * E4 * RT], onesm, picks, start=True, stop=True).then_inc(z_rank, 1)
            pe.wait_ge(table_out, 1)

            def transposes(src, bank, s_done):
                for tile in range(2):
                    for c in range(2):
                        mm = pe.transpose(psum[bank][0:HC, (2 * tile + c) * 128:(2 * tile + c) * 128 + 128],
                                          src[:, tile, c * HC:c * HC + HC], ident[:, :])
                mm.then_inc(s_done, 1)

            def experts(m, words):
                _, w = nc.values_load_multi_w_load_instructions(table[0:1, 1, ds(m, words)], engines=[mybir.EngineType.PE],
                                                                min_val=0, max_val=E4 ** 8 - 1)
                return [[(w[j // 4], 2 * (2 * (j % 4) + tile)) for tile in range(2)] for j in range(4 * words)]

            def unpack(e):
                return [pe.snap(((word >> shift) & (E4 - 1)) * 2) for word, shift in e]

            def layer(es, hi, lo, wh, wl, bank, s_done):
                for tile, e2 in enumerate(es):
                    o = psum[bank][:, tile * D:tile * D + D]
                    for c in range(2):
                        K = HC + c
                        w_h = wh[0:K, ds(e2 + c, 1), :].rearrange("p a d -> p (a d)")
                        w_l = wl[0:K, ds(e2 + c, 1), :].rearrange("p a d -> p (a d)")
                        pe.matmul(o, hi[0:K, tile, c], w_h, start=(c == 0), stop=False)
                        pe.matmul(o, hi[0:K, tile, c], w_l, start=False, stop=False)
                        mm = pe.matmul(o, lo[0:K, tile, c], w_h, start=False, stop=(c == 1))
                mm.then_inc(s_done, 1)

            def step(n, k, it, es, n1, n2):
                inside = it is not None
                if inside or n < STEPS:
                    pe.wait_ge(x2_act, n + 1)
                    pe.wait_ge(x2_dve, n + 1)
                    if inside or n >= 2:
                        pe.wait_ge(hi1_done, n - 1)
                        pe.wait_ge(lo1_done, n - 1)
                    transposes(x2[:, k % 4], k % 2, t1_done)
                if inside or 1 <= n <= STEPS:
                    pe.wait_ge(hi1_done, n)
                    pe.wait_ge(lo1_done, n)
                    if inside or n >= 3:
                        pe.wait_ge(act_done, n - 2)
                    j = (k - 1) % 2
                    es[n1] = unpack(es[n1])
                    layer(es[n1], xthi[:, j], xtlo[:, j], w1hi, w1lo, 2 + j, l1_done)
                if inside or 2 <= n <= STEPS + 1:
                    pe.wait_ge(act_done, n - 1)
                    if inside or n >= 4:
                        pe.wait_ge(hi2_done, n - 3)
                        pe.wait_ge(lo2_done, n - 3)
                    j = k % 2
                    transposes(act1[:, j], 4 + j, t2_done)
                if inside or n >= 3:
                    pe.wait_ge(hi2_done, n - 2)
                    pe.wait_ge(lo2_done, n - 2)
                    if inside or n >= 5:
                        pe.wait_ge(fin_done, n - 4)
                    j = (k - 3) % 2
                    if n2 < 2:
                        es[n2] = unpack(es[n2])
                    layer(es[n2], gthi[:, j], gtlo[:, j], w2hi, w2lo, 6 + j, l2_done)

            es = [None, None] + experts(0, RING // 4)
            for n in range(RING):
                step(n, n, None, es, n - 1 + 2, n - 3 + 2)
            with pe.Fori(0, STEPS // RING - 2) as i:
                es = experts((RING // 4) * i + (RING // 4 - 1), RING // 4 + 1)[1:]
                for k in range(RING):
                    step(RING * i + k + RING, k, i, es, k + 2, k)
            es = experts((STEPS - RING) // 4 - 1, RING // 4 + 1)[1:]
            for n in range(STEPS - RING, STEPS + 3):
                k = n - (STEPS - RING)
                step(n, n % RING, None, es, k + 2, k)

        @block.vector
        def _(dve):
            count = [0]

            def link(ins):
                count[0] += 1
                ins.then_inc(v, 1)
                dve.wait_ge(v, count[0])

            def deviation(chain, st, var, mu, tmp, inv, eps, answered):
                st2 = [st[:, :, i] for i in range(6)]
                chain(dve.tensor_tensor(mu, st2[1], st2[4], ALU.add))
                chain(dve.tensor_scalar(mu, mu, 0.5, None, ALU.mult))
                chain(dve.tensor_tensor(var, st2[1], st2[4], ALU.subtract))
                chain(dve.scalar_tensor_tensor(out=var, in0=var, scalar=0.25, in1=var, op0=ALU.mult, op1=ALU.mult))
                chain(dve.tensor_tensor(tmp, st2[2], st2[5], ALU.add))
                chain(dve.scalar_tensor_tensor(out=var, in0=tmp, scalar=1.0 / D, in1=var, op0=ALU.mult, op1=ALU.add))
                dve.tensor_scalar(var, var, eps, None, ALU.add).then_inc(ask, 1)
                dve.wait_ge(act_chain, answered)
                chain(dve.reciprocal(inv, tmp))
                for _ in range(2):
                    chain(dve.tensor_tensor(tmp, inv, inv, ALU.mult))
                    chain(dve.tensor_tensor(tmp, tmp, var, ALU.mult))
                    chain(dve.tensor_scalar(tmp, tmp, -0.5, 1.5, ALU.mult, ALU.add))
                    chain(dve.tensor_tensor(inv, inv, tmp, ALU.mult))

            dve.wait_ge(const_in, 16 * 18)
            dve.wait_ge(act_chain, 1)
            dve.scalar_tensor_tensor(out=wlo, in0=wraw, scalar=WS, in1=whi, op0=ALU.mult, op1=ALU.subtract).then_inc(w_split, 1)
            link(dve.tensor_tensor(posb[:, 0:5, :], posb[:, 0:5, :], tokb.unsqueeze(1).to_broadcast([128, 5, D]), ALU.add))

            for layer in range(2):
                dve.wait_ge(pe_filter, layer + 1)
                link(dve.tensor_scalar(ang[0:16], psum[0][0:16, 0:L], fb[0:16, layer:layer + 1], fb[0:16, 2:3],
                                       ALU.add, ALU.mult))
                link(dve.tensor_scalar(red[0:16], ang[0:16], 1 / (2 * PI), MAGIC, ALU.mult, ALU.add))
                link(dve.tensor_scalar(red[0:16], red[0:16], -MAGIC, None, ALU.add))
                for part in (PI2A, PI2B, PI2C):
                    link(dve.scalar_tensor_tensor(out=ang[0:16], in0=red[0:16], scalar=-part, in1=ang[0:16],
                                                  op0=ALU.mult, op1=ALU.add))
                dve.tensor_scalar(red[0:16], ang[0:16], 3.1415925, -3.1415925, ALU.min, ALU.max).then_inc(ask, 1)
            link(dve.memset(taphl[0:96].rearrange("p a b c -> p (a b c)").bitcast(F32), 0.0))
            dve.wait_ge(act_chain, 3)
            link(dve.tensor_scalar(cb[0:96, :, 1], cb[0:96, :, 1], -1.0, None, ALU.mult))
            dve.tensor_scalar(cb[0:96, :, 2], cb[0:96, :, 2], CONV_BIAS, None, ALU.mult).then_inc(ask, 1)
            dve.wait_ge(act_chain, 5)
            dve.wait_ge(pe_filter, 4)
            for half, decay in ((0, ang), (1, red)):
                t = tap[0:96, half, :]
                link(dve.scalar_tensor_tensor(out=t, in0=psum[1 + half][0:96, 0:L], scalar=cb[0:96, half, 0:1],
                                              in1=decay[0:96], op0=ALU.add, op1=ALU.mult))
                link(dve.tensor_scalar(t, t, KS, None, ALU.mult))
                link(dve.tensor_tensor(t[:, 0:1], t[:, 0:1], cb[0:96, half, 2:3], ALU.add))
                link(dve.tensor_copy(taphl[0:96, half, 0, 128:128 + L], t))
                dve.tensor_tensor(taphl[0:96, half, 1, 128:128 + L], t, taphl[0:96, half, 0, 128:128 + L],
                                  ALU.subtract).then_inc(dve_filter, 1)
            dve.wait_ge(dve_filter, 2)

            c0, cu, ck, cp = (ucls[0:1, i, :] for i in range(4))
            dve.tensor_tensor(c0, c0, cp, ALU.add).then_inc(cls_sum, 1)
            dve.wait_ge(cls_sum, 1)
            link(dve.bn_stats(cls6[0:1, 0:6], c0))
            deviation(link, cls6[0:1, 0:6].unsqueeze(1), clsm[0:1, 1:2], clsm[0:1, 0:1], clsm[0:1, 2:3],
                      clsm[0:1, 3:4], LN_EPS, 6)
            link(dve.tensor_scalar(cu, c0, clsm[0:1, 0:1], clsm[0:1, 3:4], ALU.subtract, ALU.mult))
            link(dve.tensor_scalar(uclh[0:1, 0, :], cu, US, None, ALU.mult))
            dve.scalar_tensor_tensor(out=uclh[0:1, 1, :], in0=cu, scalar=US, in1=uclh[0:1, 0, :], op0=ALU.mult,
                                     op1=ALU.subtract).then_inc(cls_split, 1)
            dve.wait_ge(tap0_in, 16)
            link(dve.tensor_tensor(ck, ck, cu, ALU.mult))
            dve.scalar_tensor_tensor(out=cp, in0=ck, scalar=CONV_OUT * US, in1=c0, op0=ALU.mult, op1=ALU.add).then_inc(cls_out, 1)

            dve.wait_ge(cls_out, 1)
            link(dve.tensor_scalar(tmask[:, 0, :], lenp, spart, None, ALU.subtract))
            link(dve.tensor_scalar(tmask[:, 1, :], tmask[:, 0, :], 6.0, None, ALU.is_gt))
            link(dve.tensor_scalar(tmask[:, 2, :], tmask[:, 0, :], 1.0, None, ALU.is_gt))
            link(dve.tensor_tensor(tmask[:, 2, :], tmask[:, 2, :], tmask[:, 1, :], ALU.subtract))
            for half in range(2):
                dve.wait_ge(text_in, 48 + 32 * half)
                if half:
                    dve.wait_ge(text_mm, 8)
                a3 = amat.rearrange("p (a b) -> p a b", b=32)
                link(dve.tensor_tensor(a3, lenrep.rearrange("p (a b) -> p a b", b=32),
                                       s32.unsqueeze(1).to_broadcast([128, 32, 32]), ALU.subtract))
                link(dve.tensor_scalar(amat, amat, 6.0, 0.2, ALU.is_equal, ALU.mult))
                for k in range(8):
                    ak = amat[:, k * 128:k * 128 + 128]
                    kk = half * 8 + k
                    link(dve.scalar_tensor_tensor(out=ak, in0=blk, scalar=tmask[:, 2, kk:kk + 1], in1=ak,
                                                  op0=ALU.mult, op1=ALU.mult))
                    link(dve.scalar_tensor_tensor(out=ak, in0=ident[:, :], scalar=tmask[:, 1, kk:kk + 1], in1=ak,
                                                  op0=ALU.mult, op1=ALU.add))
                link(dve.tensor_tensor(coef[0:4].rearrange("p (a b) -> p a b", b=32),
                                       coefi[0:4].rearrange("p (a b) -> p a b", b=32),
                                       s32v[0:4].unsqueeze(1).to_broadcast([4, 32, 32]), ALU.subtract))
                dve.tensor_scalar(coef[0:4], coef[0:4], tgt[0:4, 0:1], tgt[0:4, 1:2], ALU.max,
                                  ALU.is_equal).then_inc(text_mat, 1)
            for k in range(8):
                dve.wait_ge(text_mm, 2 * k + 2)
                link(dve.tensor_tensor(we[:, 2 * k:2 * k + 2, :], bank3(k, 2, D),
                                       posb[:, 5:6, :].to_broadcast([128, 2, D]), ALU.add))
            for k in range(16):
                ins = dve.bn_stats(stats[:, k, :], we[:, k, :])
            link(ins)
            deviation(link, stats[:, 0:16, :], s1[:, 0:16], mean[:, 0:16], s2[:, 0:16], rstd[:, 0:16], TXT_EPS, 7)
            for k in range(16):
                ins = dve.tensor_scalar(we[:, k, :], we[:, k, :], mean[:, k:k + 1], rstd[:, k:k + 1], ALU.subtract, ALU.mult)
            ins.then_inc(text_norm, 1)

            SC = 1 / (XS * WS)

            def second(n, slot, turn, width):
                dve.wait_ge(x_in[slot], 16 * turn)
                dve.wait_ge(x_hi, n + 1)
                dve.scalar_tensor_tensor(out=xlo[:, slot % 2, :, 0:width], in0=xin[:, slot, :, 0:width], scalar=XS,
                                         in1=xhi[:, slot % 2, :, 0:width], op0=ALU.mult, op1=ALU.subtract).then_inc(x_lo, 1)

            def tokens(n, k):
                dve.wait_ge(proj, n + 1)
                b = 2 * (n - 1)
                o0, o1 = bank3(2 * (k % 2), 2, D), psum[2 * (k % 2) + 1][:, 0:D]
                dve.scalar_tensor_tensor(out=h[:, ds(b, 2), 0:D], in0=o0, scalar=SC, in1=posb[:, 0:2, :],
                                         op0=ALU.mult, op1=ALU.add)
                dve.scalar_tensor_tensor(out=h[0:64, ds(b + B, 1), 0:D].rearrange("p a c -> p (a c)"), in0=o1[0:64],
                                         scalar=SC, in1=posb[0:64, 2, :], op0=ALU.mult, op1=ALU.add)
                dve.scalar_tensor_tensor(out=h[0:64, ds(b + B + 1, 1), 0:D].rearrange("p a c -> p (a c)"), in0=o1[64:128],
                                         scalar=SC, in1=posb[64:128, 2, :], op0=ALU.mult, op1=ALU.add).then_inc(proj_out, 1)
                dve.wait_ge(proj_out, n + 1)
                for t in range(2):
                    ins = dve.bn_stats(stats[:, ds(b + t, 1), :].rearrange("p a c -> p (a c)"),
                                       h[:, ds(b + t, 1), 0:D].rearrange("p a c -> p (a c)"))
                return ins

            second(0, 0, 1, 256)
            second(1, 1, 1, 384)
            dve.wait_ge(proj, 1)
            dve.scalar_tensor_tensor(out=lout, in0=bank3(0, 2, D), scalar=SC, in1=posb[:, 3:5, :], op0=ALU.mult,
                                     op1=ALU.add).then_inc(proj_out, 1)
            with dve.Fori(0, 7) as i:
                for k in range(4):
                    n = 4 * i + k + 1
                    dve.wait_ge(proj, n)
                    second(n + 1, (k + 2) % 4, i + (2 if k >= 2 else 1), 384)
                    tokens(n, k + 1)
            for n in range(29, 33):
                if n < 32:
                    dve.wait_ge(proj, n)
                    second(n + 1, (n + 1) % 4, (n + 1) // 4 + 1, 384)
                tokens(n, n % 4)
            dve.wait_ge(urow_in, 48)
            dve.wait_ge(h_in, 16 * 9)
            with dve.Fori(0, 8) as i:
                for k in range(8):
                    ins = dve.bn_stats(stats[:, ds(8 * i + k + B, 1), :].rearrange("p a c -> p (a c)"),
                                       h[:, ds(8 * i + k + B, 1), 0:D].rearrange("p a c -> p (a c)"))
                ins.then_inc(stat2, 1)
            dve.wait_ge(stat2, 8)
            deviation(link, stats, s1[:, :], mean[:, :], s2[:, :], rstd[:, :], LN_EPS, 8)
            dve.tensor_scalar(s2[:, :], rstd[:, :], US, None, ALU.mult).then_inc(a_done, 1)
            dve.wait_ge(a_done, 1)
            dve.wait_ge(proj, 33)

            def normalise(third, i, k):
                for t in range(16):
                    q = 32 * i + 16 * k + t
                    ins = dve.tensor_scalar(utmp[:, k, t, :], h[:, ds(q, 1), 64 * third:64 * third + 64].rearrange("p a c -> p (a c)"),
                                            mean[:, ds(q, 1)], s2[:, ds(q, 1)], ALU.subtract, ALU.mult)
                ins.then_inc(u_norm, 1)

            def split(third, i, k):
                dve.wait_ge(u_norm, 8 * third + 2 * i + k + 1)
                dve.wait_ge(u_hi, 8 * third + 2 * i + k + 1)
                q = ds(32 * i + 16 * k, 16)
                hi = uhi[:, third % 2, :, q].rearrange("p c q -> p q c")
                lo = ulo[:, third % 2, :, q].rearrange("p c q -> p q c")
                dve.tensor_tensor(lo, utmp[:, k], hi, ALU.subtract).then_inc(u_lo, 1)

            def add_channels(third, i, j):
                dve.wait_ge(conv, 16 * third + 4 * i + j + 1)
                hc = h[:, :, ds(64 * third + 16 * i + 4 * j, 4)].rearrange("p q c -> p c q")
                dve.scalar_tensor_tensor(out=hc, in0=bank3(j, 4, NQ), scalar=CONV_OUT, in1=hc, op0=ALU.mult,
                                         op1=ALU.add).then_inc(conv_free, 1)

            dve.sem_inc(conv_free, 4)
            with dve.Fori(0, 4) as i:
                for k in range(2):
                    normalise(0, i, k)
                    split(0, i, k)
            for third in range(1, 3):
                with dve.Fori(0, 4) as i:
                    for k in range(2):
                        normalise(third, i, k)
                        add_channels(third - 1, i, 2 * k)
                        add_channels(third - 1, i, 2 * k + 1)
                        if third == 2 and k == 0:
                            dve.wait_ge(conv, 16)
                        split(third, i, k)
            with dve.Fori(0, 4) as i:
                for j in range(4):
                    add_channels(2, i, j)

            dve.wait_ge(conv_free, 4 + CONV_STEPS)
            dve.wait_ge(conv, CONV_STEPS)
            link(dve.memset(onesm, 1.0))
            for e in range(2):
                link(dve.tensor_copy(run[:, e, :], regbase))
            dve.wait_ge(d_in, 96)
            for n, (wl, raw, wh, K) in enumerate(((rwlo, rwraw, rwhi, HC), (w1lo, w1raw, w1hi, HC + 1), (w2lo, w2raw, w2hi, HC + 1))):
                dve.wait_ge(d_split, n + 1)
                dve.scalar_tensor_tensor(out=wl[0:K], in0=raw[0:K], scalar=WS, in1=wh[0:K], op0=ALU.mult,
                                         op1=ALU.subtract).then_inc(low_split, 1)
            dve.wait_ge(cls_in, 16)
            hrow = h[:, :, ROWID:ROWID + 1].bitcast(I32)
            link(dve.tensor_copy(hrow, rowid[:, :].unsqueeze(2)))
            PER, PT = 40, RT // 2
            with dve.Fori(0, RG) as g:
                n1 = [0]

                def chain(ins):
                    n1[0] += 1
                    ins.then_inc(v1, 1)
                    dve.wait_ge(v1, g * PER + n1[0])

                q0 = RT * g
                for t in range(RT):
                    ins = dve.bn_stats(rstats[:, t, :], h[:, ds(q0 + t, 1), 0:D].rearrange("p a c -> p (a c)"))
                chain(ins)
                mu, inv = mean[:, 0:RT], rstd[:, 0:RT]
                deviation(chain, rstats, s1[:, 0:RT], mu, s2[:, 0:RT], inv, LN_EPS, g + 9)
                chain(dve.scalar_tensor_tensor(out=rnmr, in0=mu, scalar=-1.0, in1=inv, op0=ALU.mult, op1=ALU.mult))
                dve.tensor_copy(h[:, ds(q0, RT), MEAN:MEAN + 1], mu.unsqueeze(2))
                dve.tensor_copy(h[:, ds(q0, RT), RSTD:RSTD + 1], inv.unsqueeze(2))
                dve.tensor_copy(h[:, ds(q0, RT), NMR:NMR + 1], rnmr.unsqueeze(2)).then_inc(z_stat, 1)

                def znorm(t):
                    if t >= 4:
                        dve.wait_ge(z_t, g * PT + t - 3)
                    dve.tensor_scalar(ztok[:, t % 4, 1, :], h[:, ds(q0 + 2 * t + 1, 1), 0:D].rearrange("p a c -> p (a c)"),
                                      mean[:, 2 * t + 1:2 * t + 2], rstd[:, 2 * t + 1:2 * t + 2], ALU.subtract,
                                      ALU.mult).then_inc(zn_dve, 1)

                znorm(0)
                for t in range(PT):
                    if t + 1 < PT:
                        znorm(t + 1)
                    dve.wait_ge(z_hi, g * PT + t + 1)
                    if t >= 2:
                        dve.wait_ge(z_log, g * PT + t - 1)
                    dve.scalar_tensor_tensor(out=flat(ztlo[0:HC, t % 2]), in0=psum[t % 2][0:HC, :],
                                             scalar=US, in1=flat(zthi[0:HC, t % 2]), op0=ALU.mult, op1=ALU.subtract).then_inc(z_lo, 1)
                dve.wait_ge(z_log, g * PT + PT)
                w = [128, RT, E4]
                chain(dve.scalar_tensor_tensor(out=logit, in0=bank3(2, RT, E4), scalar=1 / (US * WS),
                                               in1=rbias.unsqueeze(1).to_broadcast(w), op0=ALU.mult, op1=ALU.add))
                chain(dve.tensor_reduce(rmax, logit, AX, ALU.max))
                dve.tensor_tensor(logit, logit, rmax.unsqueeze(2).to_broadcast(w), ALU.subtract).then_inc(ask, 1)
                dve.wait_ge(z_exp, g + 1)
                chain(dve.tensor_reduce(rsum, prob, AX, ALU.add))
                chain(dve.reciprocal(rsum, rsum))
                chain(dve.tensor_tensor(prob, prob, rsum.unsqueeze(2).to_broadcast(w), ALU.mult))
                chain(dve.tensor_reduce(rmax, prob, AX, ALU.max))
                chain(dve.tensor_tensor(pick, prob, rmax.unsqueeze(2).to_broadcast(w), ALU.is_equal))
                chain(dve.tensor_tensor(pick, pick, pickw.unsqueeze(1).to_broadcast(w), ALU.mult))
                chain(dve.tensor_reduce(rmax, pick, AX, ALU.max))
                chain(dve.tensor_tensor(pick, pick, rmax.unsqueeze(2).to_broadcast(w), ALU.is_equal))
                chain(dve.tensor_scalar(rmax, piota.to_broadcast([128, RT]), CLS + 0.5, None, ALU.is_gt))
                chain(dve.tensor_scalar(rmax, rmax, tilej[:, ds(g, 1)], None, ALU.mult))
                chain(dve.tensor_scalar(rsum, rmax, -1.0, 1.0, ALU.mult, ALU.add))
                chain(dve.tensor_tensor(pick, pick, rsum.unsqueeze(2).to_broadcast(w), ALU.mult))
                dve.tensor_copy(onehot, pick).then_inc(z_pick, 1)
                dve.wait_ge(z_rank, g + 1)
                total = psum[3][:, E4 * RT:2 * E4 * RT].rearrange("p (a b) -> p a b", b=E4)
                chain(dve.tensor_copy(prob, total))
                chain(dve.memset(logit, 1.0))
                for e in range(E4):
                    ins = dve.tensor_tensor_scan(rank[:, :, e], logit[:, :, e], prob[:, :, e], run[:, 0, e:e + 1],
                                                 ALU.mult, ALU.add)
                chain(ins)
                dve.tensor_copy(run[:, 1, :], rank[:, RT - 1, :])
                chain(dve.tensor_tensor(prob, rank, prob, ALU.subtract))
                chain(dve.tensor_tensor(prob, prob, bank3(3, RT, E4), ALU.add))
                chain(dve.tensor_tensor(prob, prob, pick, ALU.mult))
                chain(dve.tensor_reduce(destf, prob, AX, ALU.add))
                chain(dve.scalar_tensor_tensor(out=destf, in0=rmax, scalar=float(1 << 20), in1=destf, op0=ALU.mult, op1=ALU.add))
                chain(dve.tensor_copy(run[:, 0, :], run[:, 1, :]))
                dve.tensor_copy(dest[:, ds(q0, RT)], destf).then_inc(routed, 1)
                assert n1[0] == PER, n1[0]

            n2 = [0]

            def tlink(ins):
                n2[0] += 1
                ins.then_inc(v2, 1)
                dve.wait_ge(v2, n2[0])

            dve.wait_ge(routed, RG)
            tlink(dve.tensor_scalar(destf[:, 0:4], run[:, 0, :], piota, None, ALU.add))
            tlink(dve.tensor_copy(padid[:, :], destf[:, 0:4]))
            tn = tabn[0:1, :]
            tlink(dve.tensor_tensor(tn[:, 0:4], run[0:1, 0, :], regbase[0:1], ALU.subtract))
            tlink(dve.tensor_scalar(tn[:, 0:4], tn[:, 0:4], 127.0, None, ALU.add))
            tlink(dve.tensor_copy(tabi[0:1, :], tn[:, 0:4]))
            tlink(dve.tensor_scalar(tabi[0:1, :], tabi[0:1, :], 7, None, ALU.logical_shift_right))
            tlink(dve.tensor_copy(tn[:, 0:4], tabi[0:1, :]))
            tlink(dve.tensor_copy(tn[:, 4:5], tn[:, 0:1]))
            for e in range(1, 4):
                tlink(dve.tensor_tensor(tn[:, 4 + e:5 + e], tn[:, 3 + e:4 + e], tn[:, e:e + 1], ALU.add))
            tlink(dve.tensor_scalar(tn[:, 8:12], tn[:, 0:4], -128.0, float(REGION), ALU.mult, ALU.add))
            f = [tabf[0:1, i, :] for i in range(4)]
            tlink(dve.tensor_scalar(f[0], f[3], 128.0, None, ALU.mult))
            tlink(dve.memset(f[1], 0.0))
            for e in range(3):
                tlink(dve.tensor_scalar(f[2], f[3], tn[:, 4 + e:5 + e], None, ALU.is_ge))
                tlink(dve.scalar_tensor_tensor(out=f[1], in0=f[2], scalar=2.0, in1=f[1], op0=ALU.mult, op1=ALU.add))
                tlink(dve.scalar_tensor_tensor(out=f[0], in0=f[2], scalar=tn[:, 8 + e:9 + e], in1=f[0], op0=ALU.mult, op1=ALU.add))
            tlink(dve.tensor_scalar(f[2], f[3], tn[:, 7:8], None, ALU.is_ge))
            tlink(dve.tensor_scalar(f[3], f[0], -1.0, float(DUMMY), ALU.mult, ALU.add))
            tlink(dve.tensor_tensor(f[3], f[3], f[2], ALU.mult))
            tlink(dve.tensor_tensor(f[0], f[0], f[3], ALU.add))
            tlink(dve.tensor_copy(table[0:1, 0, :], f[0]))
            words = f[1].rearrange("p (a b) -> p a b", b=8)
            tlink(dve.tensor_tensor(words, words, small[0:1, 88:96].unsqueeze(1).to_broadcast([1, SLOTS // 8, 8]), ALU.mult))
            tlink(dve.tensor_reduce(f[2][:, 0:SLOTS // 8], words, AX, ALU.add))
            tlink(dve.tensor_copy(table[0:1, 1, 0:SLOTS // 8], f[2][:, 0:SLOTS // 8]))
            for one, zero, val in ((xthi, xtlo, US), (gthi, gtlo, GS)):
                dve.memset(one[96:97].rearrange("p a b c d -> p (a b c d)"), val)
                ins = dve.memset(zero[96:97].rearrange("p a b c d -> p (a b c d)"), 0.0)
            ins.then_inc(table_out, 1)

            def norm(n, k, use):
                dve.wait_ge(row_in[k], use)
                if not isinstance(n, int) or n >= 4:
                    dve.wait_ge(t1_done, n - 3)
                dve.tensor_scalar(x2[:, k % 4, 1, :], row[:, k, 1, 0:D], row[:, k, 1, MEAN:MEAN + 1],
                                  row[:, k, 1, RSTD:RSTD + 1], ALU.subtract, ALU.mult).then_inc(x2_dve, 1)

            def residual(n, k):
                dve.wait_ge(x2_act, n + 1)
                dve.wait_ge(x2_dve, n + 1)
                dve.tensor_tensor(row[:, k, :, 0:D], row[:, k, :, 0:D], x2[:, k % 4], ALU.add).then_inc(r_done, 1)

            def low(n, k, bank, hi, lo, scale, s_hi, s_lo):
                dve.wait_ge(s_hi, n + 1)
                dve.scalar_tensor_tensor(out=flat(lo[0:HC, k % 2]), in0=psum[bank + k % 2][0:HC, :], scalar=scale,
                                         in1=flat(hi[0:HC, k % 2]), op0=ALU.mult, op1=ALU.subtract).then_inc(s_lo, 1)

            def final(n, k):
                dve.wait_ge(l2_done, n + 1)
                dve.wait_ge(r_done, n + 1)
                dve.scalar_tensor_tensor(out=row[:, k, :, 0:D], in0=bank3(6 + k % 2, 2, D), scalar=1 / (GS * WS),
                                         in1=row[:, k, :, 0:D], op0=ALU.mult, op1=ALU.add).then_inc(fin_done, 1)

            def step(n, k, it):
                inside = it is not None
                if inside or n + 1 < STEPS:
                    kk = (k + 1) % RING
                    norm(n + 1, kk, 32 * it + (64 if kk else 96) if inside else 32 * ((n + 1) // RING + 1))
                if inside or n < STEPS:
                    if inside or n >= 2:
                        dve.wait_ge(l1_done, n - 1)
                    low(n, k, 0, xthi, xtlo, US, hi1_done, lo1_done)
                    residual(n, k)
                if inside or 2 <= n <= STEPS + 1:
                    if inside or n >= 4:
                        dve.wait_ge(l2_done, n - 3)
                    low(n - 2, (k - 2) % RING, 4, gthi, gtlo, GS, hi2_done, lo2_done)
                if inside or n >= 3:
                    final(n - 3, (k - 3) % RING)

            norm(0, 0, 32)
            for n in range(RING):
                step(n, n, None)
            with dve.Fori(0, STEPS // RING - 2) as i:
                for k in range(RING):
                    step(RING * i + k + RING, k, i)
            for n in range(STEPS - RING, STEPS + 3):
                step(n, n % RING, None)


_SHAPES = {
    "xt": ((PAIRS, 128, KC, 384), F32), "xl": ((128, KC, 256), F32), "wp": ((128, KC, D), F32), "tokb": ((128, D), F32),
    "pos": ((128, 6 * D), F32), "cls": ((1, D), F32), "pos0": ((1, D), F32), "ident": ((128, 128), F32),
    "blk": ((128, 128), F32), "small": ((128, 96), F32), "idsp": ((128, 16), I32), "lenp": ((128, 16), I32),
    "lenv": ((E4, 2048), I32), "rowid": ((128, NQ), I32), "trows": ((E4, D), F32), "gb": ((128, 2 * D), F32),
    "word": ((VOCAB, D), F32), "zt": ((3, L), F32), "tgrid": ((96, L), F32), "fw1": ((3, 16), F32),
    "fw2": ((16, 16), F32), "fw3": ((16, D), F32), "fb": ((16, 4), F32), "cb": ((96, 2, 3), F32),
    "rw": ((HC, 2, E4), F32), "w1": ((HC + 1, 2 * E4, D), F32), "w2": ((HC + 1, 2 * E4, D), F32),
    "padrow": ((128, RW), I32), "slots": ((1, SLOTS), F32), "ltri": ((128, 128), F16),
}


def _layout(i):
    import numpy as np
    f = np.float32
    g = lambda k: np.asarray(i[k])
    x = g("x").reshape(B, 3, 14, 16, 14, 16).transpose(1, 3, 5, 0, 2, 4).reshape(KC, 128, B, NPATCH)
    xt = np.empty((PAIRS, 128, KC, 3, 128), f)
    y = x.reshape(KC, 128, PAIRS, 2, NPATCH).transpose(2, 1, 0, 3, 4)
    xt[:, :, :, 0:2, :] = y[..., 0:128]
    xt[:, :, :, 2, 0:64] = y[:, :, :, 0, 128:192]
    xt[:, :, :, 2, 64:128] = y[:, :, :, 1, 128:192]
    xl = x[:, :, :, 192:196].transpose(1, 0, 3, 2).reshape(128, KC, 256)
    pt = g("L0_tok_pos_table")
    pos = np.zeros((128, 6, D), f)
    pos[:, 0] = pos[:, 1] = pt[1:129]
    pos[0:64, 2] = pos[64:128, 2] = pt[129:193]
    for n in range(4):
        pos[64 * (n % 2):64 * (n % 2) + 64, 3 + n // 2] = pt[193 + n]
    pos[:, 5] = np.concatenate([g("L0_txt_pos_emb")[0:TXT]] * 4)
    p = np.arange(128)
    small = np.zeros((128, 96), f)
    small[:, 0:32] = np.arange(32)
    small[0:2, 32:64] = np.arange(32)
    small[0:4, 64:66] = [[4, 5], [4, 4], [-1e9, 0], [-1e9, 1]]
    small[:, 66] = p % 32
    small[:, 68:72] = g("L0_ffn_router_b")
    small[:, 72:76] = [4, 3, 2, 1]
    small[:, 76:80] = np.arange(E4) * REGION
    small[:, 80] = p
    small[:, 83:85] = 1
    small[:, 88:96] = 4.0 ** np.arange(8) / 2
    ln, mk = g("_lenS").astype(np.int32), g("mask_BS_i1_0").astype(np.int32)
    lenv = np.stack([np.repeat(ln, TXT)] * 2 + [mk.reshape(-1)] * 2)
    ids = g("x_txt").astype(np.int32).reshape(16, 128).T
    lenp = np.repeat(ln, TXT).reshape(16, 128).T
    rowid = np.zeros((128, NQ), np.int32)
    rowid[:, 0:B] = np.arange(B) * L + 1 + p[:, None]
    rowid[:, B:] = np.arange(B) * L + np.where(p == CLS, 0, 129 + p)[:, None]
    t = np.linspace(0, 1, L, dtype=f)
    w = f(2 * np.pi) * np.linspace(0, L - 1, L, dtype=f) / f(L)
    zt = np.stack([t, np.cos(f(1e-4) * w), -np.sin(f(1e-4) * w)]).astype(f)
    halves = lambda v: np.asarray(v).reshape(2, 96).T
    cb = np.stack([halves(g("L0_attn_b3")), halves(g("L0_attn_deltas_abs")), halves(g("L0_attn_bias"))], axis=2)
    fb = np.zeros((16, 4), f)
    fb[:, 0], fb[:, 1], fb[:, 2] = g("L0_attn_b1"), g("L0_attn_b2"), g("L0_attn_freq")

    def expert(w, b):
        r = np.zeros((HC + 1, E4, 2, D), f)
        r[0:HC] = w.reshape(E4, 2, HC, D).transpose(2, 0, 1, 3)
        r[HC, :, 1] = b
        return r.reshape(HC + 1, 2 * E4, D)

    padrow = np.zeros((128, RW), np.int32)
    padrow[:, ROWID] = 1 << 20
    word = g("L0_txt_word_emb")
    return {
        "xt": xt.reshape(PAIRS, 128, KC, 384), "xl": xl, "wp": g("L0_tok_W").reshape(KC, 128, D).transpose(1, 0, 2),
        "tokb": np.tile(g("L0_tok_b"), (128, 1)), "pos": pos.reshape(128, 6 * D), "cls": g("L0_tok_class_token").reshape(1, D),
        "pos0": pt[0:1], "ident": np.eye(128, dtype=f), "blk": np.kron(np.eye(4), np.ones((32, 32))).astype(f),
        "small": small, "idsp": ids, "lenp": lenp, "lenv": lenv, "rowid": rowid,
        "trows": np.stack([word[SEP], word[0], g("L0_txt_type_emb")[0], g("L0_txt_type_emb")[1]]),
        "gb": np.tile(np.concatenate([g("L0_txt_ln_gamma"), g("L0_txt_ln_beta")]), (128, 1)), "word": word,
        "zt": zt, "tgrid": np.tile(t, (96, 1)), "fw1": g("L0_attn_w1").T, "fw2": g("L0_attn_w2").T, "fw3": g("L0_attn_w3").T,
        "fb": fb, "cb": cb, "rw": g("L0_ffn_router_w").reshape(2, HC, E4).transpose(1, 0, 2),
        "w1": expert(g("L0_ffn_w1"), g("L0_ffn_b1")), "w2": expert(g("L0_ffn_w2"), g("L0_ffn_b2")),
        "padrow": padrow, "slots": np.arange(SLOTS, dtype=f).reshape(1, SLOTS), "ltri": np.triu(np.ones((128, 128)), 1).astype(np.float16),
    }


def kernel(**inputs):
    import numpy as np
    import concourse.bacc as bacc
    from concourse.bass_utils import run_bass_kernel_spmd as run

    nc = bacc.Bacc("TRN2", target_bir_lowering=False, num_devices=1)
    arrays, args = {}, {}
    for name, v in _layout(inputs).items():
        shape, dt = _SHAPES[name]
        v = np.ascontiguousarray(v)
        assert v.shape == shape and mybir.dt.from_np(v.dtype) == dt, (name, v.shape, v.dtype)
        arrays[f"in_{name}"] = v
        args[name] = nc.dram_tensor(f"in_{name}", shape, dt, kind="ExternalInput").ap()
    args["out"] = nc.dram_tensor("out_rows", (NTOK, D), F32, kind="ExternalOutput").ap()
    build(nc, args)
    r = run(nc, [arrays], core_ids=[0])
    return r.results[0]["out_rows"].reshape(B, L, D)
```

```python
import concourse.bass as bass
from concourse import mybir

F32 = mybir.dt.float32
F16 = mybir.dt.float16
I32 = mybir.dt.int32
U32 = mybir.dt.uint32
ALU = mybir.AluOpType
ACT = mybir.ActivationFunctionType
AX = mybir.AxisListType.X

B = 64
D = 192
NPATCH = 196
KC = 6
TXT = 32
L = 1 + NPATCH + TXT
NQ = 2 * B
CLS = L - 1 - 128
RW = D + 4
MEAN, RSTD, ROWID, NMR = D, D + 1, D + 2, D + 3
PAIRS = B // 2
VOCAB, SEP = 30522, 102
NTOK = B * L
E4 = 4
HC = 96
REGION = NTOK + 128
DUMMY = E4 * REGION
SLOTS = 120
STEPS = SLOTS // 2
RING = 12
RT = 32
RG = NQ // RT
EARLY = (B * 128 + (B - RT) * (CLS + 1) - 127 * 4) // 128 // (2 * RING) * RING

XS, WS = 16.0, 256.0
US, GS = 1024.0, 512.0
KS = 1.0 / 16
CONV_OUT = 1.0 / (KS * US * 2 * L)
CONV_BIAS = KS * 2 * L

KP = 360
COPY = 2 * D * KP + 128
CG = 4
NG = D // CG
TC = 64
TAPW = 256
RUN = (2 * CG - 1) * KP + TAPW
LN_EPS, TXT_EPS = 1e-5, 1e-12
PI = 3.141592653589793
MAGIC = 12582912.0
PI2A, PI2B = 6.28125, 0.0019350051879882812
PI2C = 2 * PI - PI2A - PI2B


def build(nc, a):
    import contextlib
    ctx = contextlib.ExitStack()
    with ctx:
        def sb(name, shape, dt):
            return ctx.enter_context(nc.sbuf_tensor(name, shape, dt))

        def sem(name):
            return ctx.enter_context(nc.semaphore(name))

        out = a["out"]
        taps_dram = nc.dram_tensor("taps", (2, COPY), F16, kind="Internal").ap()
        tap0_dram = nc.dram_tensor("tap0", (D,), F32, kind="Internal").ap()
        sorted_dram = nc.dram_tensor("sorted_rows", (DUMMY + 128, RW), F32, kind="Internal").ap()

        h = sb("h", [128, NQ, RW], F32)
        ARENA = 104576
        arena = sb("arena", [128, ARENA // 4], F32)
        top = [0]

        def carve(shape, dt):
            n = 1
            for s in shape:
                n *= s
            size = (n * (2 if dt == F16 else 4) + 31) // 32 * 8
            v = arena[:, top[0]:top[0] + size]
            top[0] += size
            assert top[0] * 4 <= ARENA, (top[0] * 4, shape)
            if dt != F32:
                v = v.bitcast(dt)
            v = v[:, 0:n]
            if len(shape) == 2:
                v = v.rearrange("p (a b) -> p a b", b=shape[1])
            elif len(shape) == 3:
                v = v.rearrange("p (a b c) -> p a b c", b=shape[1], c=shape[2])
            elif len(shape) == 4:
                v = v.rearrange("p (a b c d) -> p a b c d", b=shape[1], c=shape[2], d=shape[3])
            return v

        xin = carve([4, KC, 384], F32)
        xhi = carve([2, KC, 384], F16)
        xlo = carve([2, KC, 384], F16)
        whi = carve([KC, D], F16)
        wlo = carve([KC, D], F16)
        posb = carve([6, D], F32)
        lout = carve([2, D], F32)
        tokb = lout[:, 0, :]
        uclh = carve([2, D], F16)
        idsp = carve([16], I32)
        lenp = carve([16], I32)
        tmask = carve([3, 16], F32)
        blk = carve([128], F32)
        trow = carve([D], F32)
        we = carve([16, D], F32)
        tstats = carve([16, 6], F32)
        diag = carve([128], F32)
        coef = carve([2048], F32)
        stats_at = top[0]
        stats = carve([NQ, 6], F32)
        amat = carve([2048], F32)
        lenrep, coefi = amat.bitcast(I32), coef.bitcast(I32)
        wraw = we.rearrange("p a b -> p (a b)")[:, 0:KC * D].rearrange("p (a b) -> p a b", b=D)
        filter_mem = h[0:96, NQ - 28:NQ, :].rearrange("p a b -> p (a b)")
        used = [0]

        def slot(width):
            used[0] += width
            assert used[0] <= 28 * RW
            return filter_mem[:, used[0] - width:used[0]]

        zt, tgrid, ang, red, sin1, sin2 = (slot(L) for _ in range(6))
        cdec = slot(2 * L)
        tap = slot(2 * L).rearrange("p (a b) -> p a b", b=L)
        taphl = slot(2 * KP).bitcast(F16).rearrange("p (a b c) -> p a b c", a=2, b=2)
        fw1, fw2, fw3, fb = slot(16), slot(16), slot(D), slot(4)
        cb = slot(6).rearrange("p (a b) -> p a b", b=3)

        top[0] = 0
        uhi = carve([2, TC, NQ], F16)
        ulo = carve([2, TC, NQ], F16)
        toep = carve([4, RUN], F16)
        assert top[0] <= stats_at
        ctap = carve([4, CG, TAPW], F16)
        assert stats_at + NQ * 6 <= top[0]
        utmp = carve([4, 8, TC], F32)

        top[0] = 0
        ztok = carve([4, 2, D], F32)
        zthi = carve([4, 2, 2, 128], F16)
        ztlo = carve([4, 2, 2, 128], F16)
        rwraw = carve([2, E4], F32)
        rwhi = carve([2, E4], F16)
        rwlo = carve([2, E4], F16)
        logit = carve([RT, E4], F32)
        prob = carve([RT, E4], F32)
        pick = carve([RT, E4], F32)
        onehot = carve([RT, E4], F16)
        rank = carve([RT, E4], F32)
        rmax = carve([RT], F32)
        rsum = carve([RT], F32)
        run = carve([2, E4], F32)
        before = carve([RG, E4], F32)
        destf = carve([RT], F32)
        tabf = carve([4, SLOTS], F32)
        table = carve([2, SLOTS], I32)
        rstats = carve([RT, 6], F32)
        rnmr = carve([RT], F32)
        padrow = carve([RW], I32)
        ltri = carve([128], F16)
        onesm = carve([128], F16)
        w1raw = carve([E4 * 2, D], F32)
        w2raw = carve([E4 * 2, D], F32)
        w1hi = carve([E4 * 2, D], F16)
        w1lo = carve([E4 * 2, D], F16)
        w2hi = carve([E4 * 2, D], F16)
        w2lo = carve([E4 * 2, D], F16)
        row = h[:, 0:2 * RING, :].rearrange("p (k t) c -> p k t c", t=2)
        x2 = carve([4, 2, D], F32)
        xthi = carve([2, 2, 2, 128], F16)
        xtlo = carve([2, 2, 2, 128], F16)
        act1 = carve([2, 2, D], F32)
        gthi = carve([2, 2, 2, 128], F16)
        gtlo = carve([2, 2, 2, 128], F16)

        ident = sb("ident", [128, 128], F32)
        mean = sb("mean", [128, NQ], F32)
        rstd = sb("rstd", [128, NQ], F32)
        s1 = sb("s1", [128, NQ], F32)
        s2 = sb("s2", [128, NQ], F32)
        dest = sb("dest", [128, NQ], I32)
        rowid = sb("rowid", [128, NQ], I32)
        ucls = sb("ucls", [128, 4, D], F32)
        urow = sb("urow", [128, D], F16)
        cls6 = sb("cls6", [128, 8], F32)
        clsm = sb("clsm", [128, 4], F32)
        small = sb("small", [128, 96], F32)
        padid = sb("padid", [128, E4], I32)
        tabn = sb("tabn", [1, 48], F32)
        tabi = sb("tabi", [1, 8], I32)
        psum = [ctx.enter_context(nc.psum_tensor(f"bank{i}", [128, 512], F32)) for i in range(8)]
        s32, s32v, tgt, spart = small[:, 0:32], small[:, 32:64], small[:, 64:66], small[:, 66:67]
        vmask, rbias, pickw, regbase, piota = small[:, 67:68], small[:, 68:72], small[:, 72:76], small[:, 76:80], small[:, 80:81]
        tilej = small[:, 81:81 + RG]

        const_in = sem("const_in")
        x_in = [sem(f"x_in{i}") for i in range(4)]
        w_in = sem("w_in")
        w_split = sem("w_split")
        x_hi, x_lo = sem("x_hi"), sem("x_lo")
        proj, proj_out = sem("proj"), sem("proj_out")
        act_chain = sem("act_chain")
        ask = sem("ask")
        pe_filter = sem("pe_filter")
        dve_filter = sem("dve_filter")
        v = sem("vector_chain")
        taps_out = sem("taps_out")
        tap0_in = sem("tap0_in")
        text_in = sem("text_in")
        text_out = sem("text_out")
        gathered = sem("gathered")
        text_mat, text_mm, text_norm, text_affine, gb_in = (sem("text_mat"), sem("text_mm"), sem("text_norm"),
                                                            sem("text_affine"), sem("gb_in"))
        pchain = sem("pool_chain")
        rows_clear = sem("rows_clear")
        cls_sum = sem("cls_sum")
        h_in = sem("h_in")
        cls_split, urow_in = sem("cls_split"), sem("urow_in")
        zeroed = sem("zeroed")
        stat2 = sem("stat2")
        a_done = sem("a_done")
        u_centre, u_norm, u_norm_act, u_hi, u_lo = sem("u_centre"), sem("u_norm"), sem("u_norm_act"), sem("u_hi"), sem("u_lo")
        toep_in = [sem(f"toep_in{i}") for i in range(4)]
        conv, conv_free = sem("conv"), sem("conv_free")
        cls_out, cls_in = sem("cls_out"), sem("cls_in")
        d_in = sem("d_in")
        d_split, low_split = sem("d_split"), sem("low_split")
        z_stat, z_t, z_hi, z_lo, z_log, z_rank = (sem("z_stat"), sem("z_t"), sem("z_hi"), sem("z_lo"), sem("z_log"),
                                                  sem("z_rank"))
        z_pick, z_exp, routed = sem("z_pick"), sem("z_exp"), sem("routed")
        v1 = sem("vector_chain_routing")
        v2 = sem("vector_chain_table")
        scattered_early = sem("scattered_early")
        scattered, table_out, dummy_in = sem("scattered"), sem("table_out"), sem("dummy_in")
        stores_begun = sem("stores_begun")
        row_in = [sem(f"row_in{i}") for i in range(RING)]
        row_out = [sem(f"row_out{i}") for i in range(RING)]
        zn_act, zn_dve = sem("zn_act"), sem("zn_dve")
        x2_act, x2_dve, r_done, lo1_done, lo2_done, fin_done = (sem("x2_act"), sem("x2_dve"), sem("r_done"), sem("lo1_done"), sem("lo2_done"),
                                                         sem("fin_done"))
        t1_done, l1_done, t2_done, l2_done = sem("t1_done"), sem("l1_done"), sem("t2_done"), sem("l2_done")
        hi1_done, act_done, hi2_done = sem("hi1_done"), sem("act_done"), sem("hi2_done")
        block = ctx.enter_context(nc.Block())
        ds = bass.ds

        CONV_STEPS = D // 4
        CONSTS = 17
        ZB = (0, 1, 4, 5)

        def flat(t):
            return t.rearrange("p a b c -> p (a b c)")

        def bank3(i, n, m):
            return psum[i][:, 0:n * m].rearrange("p (a b) -> p a b", b=m)

        @block.sync
        def _(sp):
            wiring = [(ident[:, :], a["ident"]), (blk, a["blk"]), (small[:, :], a["small"]),
                      (idsp, a["idsp"]), (lenp, a["lenp"]), (rowid[:, :], a["rowid"]),
                      (posb.rearrange("p a b -> p (a b)"), a["pos"]), (tokb, a["tokb"]),
                      (zt[0:3, :], a["zt"]), (tgrid[0:96, :], a["tgrid"]),
                      (fw1[0:3, :], a["fw1"]), (fw2[0:16, :], a["fw2"]), (fw3[0:16, :], a["fw3"]),
                      (fb[0:16, :], a["fb"]), (cb[0:96, :, :], a["cb"]),
                      (ucls[0:1, 0, :], a["cls"]), (ucls[0:1, 3, :], a["pos0"])]
            sp.dma_start(wraw, a["wp"]).then_inc(w_in, 16)
            sp.dma_start(xin[:, 0, :, 0:256], a["xl"]).then_inc(x_in[0], 16)
            sp.dma_start(xin[:, 1, :, :], a["xt"][0]).then_inc(x_in[1], 16)
            for dst, src in wiring:
                sp.dma_start(dst, src).then_inc(const_in, 16)
            for n in range(2, 4):
                sp.dma_start(xin[:, n, :, :], a["xt"][n - 1]).then_inc(x_in[n], 16)
            sp.dma_start(lenrep, a["lenv"][0:1, :].to_broadcast([128, 2048])).then_inc(text_in, 16)
            sp.dma_start(coefi[0:E4, :], a["lenv"]).then_inc(text_in, 16)
            sp.dma_start(trow[0:E4, :], a["trows"]).then_inc(text_in, 16)

            def refill(lo, hi):
                with sp.Fori(lo, hi) as i:
                    for k in range(4):
                        sp.wait_ge(x_hi, 4 * i + k + 1)
                        sp.wait_ge(x_lo, 4 * i + k + 1)
                        sp.dma_start(xin[:, k, :, :], a["xt"][ds(4 * i + k + 3, 1)].rearrange("a p k t -> (a p) k t")).then_inc(x_in[k], 16)

            refill(0, 3)
            sp.wait_ge(dve_filter, 2)
            for half in range(2):
                for copy in range(2):
                    sp.dma_start(taps_dram[copy, half * 96 * 2 * KP:(half * 96 + 96) * 2 * KP].rearrange("(c x) -> c x", x=2 * KP),
                                 taphl[0:96, half, :, :].rearrange("p a b -> p (a b)")).then_inc(taps_out, 16)
                    if half:
                        sp.dma_start(taps_dram[copy:copy + 1, COPY - 128:COPY], taphl[0:1, 0, 0, 0:128]).then_inc(taps_out, 16)
                sp.dma_start(tap0_dram[half * 96:half * 96 + 96].unsqueeze(1), tap[0:96, half, 0:1]).then_inc(taps_out, 16)
            sp.wait_ge(taps_out, 16 * 8)
            sp.dma_start(ucls[0:1, 2, :], tap0_dram.unsqueeze(0)).then_inc(tap0_in, 16)
            sp.wait_ge(cls_sum, 1)
            sp.wait_ge(rows_clear, 1)
            sp.dma_start(h[CLS:CLS + 1, B:NQ, 0:D], ucls[0:1, 0:1, :].to_broadcast([1, B, D])).then_inc(h_in, 16)
            sp.wait_ge(proj_out, 1)
            for n in range(4):
                sp.dma_start(h[64 + n:65 + n, B:NQ, 0:D],
                             lout[64 * (n % 2):64 * (n % 2) + 64, n // 2, :]).then_inc(h_in, 16)
            refill(3, 5)
            sp.wait_ge(text_mm, 16)
            sp.dma_start(amat[:, 0:2 * D], a["gb"]).then_inc(gb_in, 16)
            refill(5, 6)
            sp.wait_ge(cls_split, 1)
            sp.wait_ge(zeroed, 1)
            sp.dma_start(urow[0:1, :], uclh[0:1, 0, :]).then_inc(urow_in, 16)
            sp.dma_start(urow[1:2, :], uclh[0:1, 0, :]).then_inc(urow_in, 16)
            sp.dma_start(urow[2:3, :], uclh[0:1, 1, :]).then_inc(urow_in, 16)
            refill(6, 7)
            sp.wait_ge(x_hi, 29)
            sp.wait_ge(x_lo, 29)
            sp.dma_start(xin[:, 0, :, :], a["xt"][31]).then_inc(x_in[0], 16)
            sp.wait_ge(text_affine, 1)
            hj = h[:, B:NQ, :].rearrange("p (k b) c -> p k b c", b=4)
            for b4 in range(4):
                sp.dma_start(hj[68:100, :, b4, 0:D], we[32 * b4:32 * b4 + 32, :, :]).then_inc(h_in, 16)
            sp.wait_ge(h_in, 16 * 9)
            sp.wait_ge(urow_in, 48)
            sp.wait_ge(a_done, 2)
            sp.wait_ge(zeroed, 2)
            sp.wait_ge(proj, 33)
            for g in range(NG):
                if g >= 4:
                    sp.wait_ge(conv, g - 3)
                src = bass.AP(taps_dram.tensor, g * CG * 2 * KP + 128, [[COPY - 64, 2], [-1, 64], [1, RUN]])
                sp.dma_start(toep[:, g % 4], src).then_inc(toep_in[g % 4], 16)
                src = bass.AP(taps_dram.tensor, g * CG * 2 * KP + 129, [[KP, 2], [2 * KP, CG], [1, TAPW]])
                sp.dma_start(ctap[0:2, g % 4], src).then_inc(toep_in[g % 4], 16)
                src = bass.AP(taps_dram.tensor, g * CG * 2 * KP + 129, [[KP, 1], [2 * KP, CG], [1, TAPW]])
                sp.dma_start(ctap[2:3, g % 4], src).then_inc(toep_in[g % 4], 16)
            sp.wait_ge(cls_out, 1)
            sp.wait_ge(conv_free, 4 + CONV_STEPS)
            sp.dma_start(h[CLS:CLS + 1, B:NQ, 0:D], ucls[0:1, 3:4, :].to_broadcast([1, B, D])).then_inc(cls_in, 16)
            for dst, src in [(rwraw[0:HC], a["rw"]), (w1raw[0:HC + 1], a["w1"]), (w2raw[0:HC + 1], a["w2"]),
                             (padrow, a["padrow"]), (tabf[0:1, 3, :], a["slots"]), (ltri, a["ltri"])]:
                sp.dma_start(dst, src).then_inc(d_in, 16)
            sp.wait_ge(d_in, 96)
            sp.dma_start(sorted_dram[DUMMY:DUMMY + 128], padrow[:, 0:RW].bitcast(F32)).then_inc(dummy_in, 16)
            sp.wait_ge(dummy_in, 16)
            sp.wait_ge(scattered_early, 16 * (NQ - RT))
            sp.wait_ge(table_out, 1)

            def load_rows(s, k):
                for t in range(2):
                    start = sp.value_load(table[0:1, 0, ds(2 * s + t, 1)], min_val=0, max_val=DUMMY)
                    sp.dma_start(row[:, k, t, 0:RW], sorted_dram[ds(start, 128), :]).then_inc(row_in[k], 16)

            def refill_rows(lo, hi):
                with sp.Fori(lo, hi) as i:
                    for k in range(RING):
                        sp.wait_ge(row_out[k], 32 * i + 32)
                        load_rows(RING * i + RING + k, k)

            for s in range(RING):
                load_rows(s, s)
            refill_rows(0, EARLY // RING - 1)
            sp.wait_ge(scattered, 16 * (RT + E4))
            refill_rows(EARLY // RING - 1, STEPS // RING - 1)

        @block.gpsimd
        def _(pool):
            pool.memset(h[96:128, B:NQ, 0:D], 0.0).then_inc(rows_clear, 1)
            pool.wait_ge(rows_clear, 1)
            pool.memset(urow[:, :].bitcast(F32), 0.0).then_inc(zeroed, 1)
            pool.wait_ge(zeroed, 1)
            pool.wait_ge(const_in, 16 * CONSTS)
            pool.wait_ge(w_split, 1)
            for k in range(16):
                pool.indirect_dma_start(we[:, k, :], None, a["word"], bass.IndirectOffsetOnAxis(
                    ap=idsp[:, k:k + 1].bitcast(U32), axis=0)).then_inc(gathered, 16)
            links = [0]

            def link(ins):
                links[0] += 1
                ins.then_inc(pchain, 1)
                pool.wait_ge(pchain, links[0])

            pool.wait_ge(text_in, 48)
            link(pool.tensor_copy(tmask[:, 0, :], lenp))
            link(pool.tensor_scalar(tmask[:, 0, :], tmask[:, 0, :], spart, None, ALU.subtract))
            link(pool.tensor_scalar(tmask[:, 1, :], tmask[:, 0, :], 6.0, None, ALU.is_gt))
            link(pool.tensor_scalar(tmask[:, 2, :], tmask[:, 0, :], 1.0, None, ALU.is_gt))
            link(pool.tensor_tensor(tmask[:, 2, :], tmask[:, 2, :], tmask[:, 1, :], ALU.subtract))
            link(pool.tensor_copy(amat, lenrep))
            link(pool.tensor_copy(coef[0:4], coefi[0:4]))
            link(pool.tensor_tensor(amat.rearrange("p (a b) -> p a b", b=32), amat.rearrange("p (a b) -> p a b", b=32),
                                    s32.unsqueeze(1).to_broadcast([128, 64, 32]), ALU.subtract))
            link(pool.tensor_scalar(amat, amat, 6.0, 0.2, ALU.is_equal, ALU.mult))
            link(pool.tensor_tensor(coef[0:4].rearrange("p (a b) -> p a b", b=32), coef[0:4].rearrange("p (a b) -> p a b", b=32),
                                    s32v[0:4].unsqueeze(1).to_broadcast([4, 64, 32]), ALU.subtract))
            link(pool.tensor_scalar(coef[0:4], coef[0:4], tgt[0:4, 0:1], tgt[0:4, 1:2], ALU.max, ALU.is_equal))
            a3 = amat.rearrange("p (a b) -> p a b", b=128)
            link(pool.tensor_tensor(a3, a3, tmask[:, 2, :].unsqueeze(2).to_broadcast([128, 16, 128]), ALU.mult))
            link(pool.tensor_tensor(a3, a3, blk.unsqueeze(1).to_broadcast([128, 16, 128]), ALU.mult))
            for k in range(16):
                link(pool.tensor_scalar(diag, ident[:, :], tmask[:, 1, k:k + 1], None, ALU.mult))
                link(pool.tensor_tensor(a3[:, k, :], a3[:, k, :], diag, ALU.add))
            pool.sem_inc(text_mat, 1)
            pool.wait_ge(text_norm, 1)
            pool.wait_ge(gb_in, 16)
            gam = amat[:, 0:D].unsqueeze(1).to_broadcast([128, 16, D])
            bet = amat[:, D:2 * D].unsqueeze(1).to_broadcast([128, 16, D])
            link(pool.tensor_tensor(we, we, gam, ALU.mult))
            pool.tensor_tensor(we, we, bet, ALU.add).then_inc(text_affine, 1)
            pool.wait_ge(a_done, 2)
            pool.wait_ge(h_in, 16 * 9)
            pool.wait_ge(proj, 33)
            pool.memset(ctap.rearrange("p a c t -> p (a c t)").bitcast(F32), 0.0).then_inc(zeroed, 1)
            for g in range(RG):
                pool.wait_ge(routed, g + 1)
                for q in range(RT * g, RT * g + RT):
                    pool.indirect_dma_start(sorted_dram[:, :], bass.IndirectOffsetOnAxis(
                        ap=dest[:, q:q + 1].bitcast(U32), axis=0), h[:, q, 0:RW], None,
                        bounds_check=DUMMY - 1, oob_is_err=False).then_inc(scattered_early if g < RG - 1 else scattered, 16)
            pool.wait_ge(table_out, 1)
            pool.wait_ge(d_in, 96)
            for e in range(E4):
                pool.indirect_dma_start(sorted_dram[:, :], bass.IndirectOffsetOnAxis(
                    ap=padid[:, e:e + 1].bitcast(U32), axis=0), padrow[:, 0:RW].bitcast(F32), None).then_inc(scattered, 16)

            def store_rows(s, k):
                pool.wait_ge(fin_done, s + 1)
                pool.sem_inc(stores_begun, 1)
                for t in range(2):
                    pool.indirect_dma_start(out[:, :], bass.IndirectOffsetOnAxis(
                        ap=row[:, k, t, ROWID:ROWID + 1].bitcast(U32), axis=0),
                        row[:, k, t, 0:D], None, bounds_check=NTOK - 1, oob_is_err=False).then_inc(row_out[k], 16)

            with pool.Fori(0, STEPS // RING) as i:
                for k in range(RING):
                    store_rows(RING * i + k, k)
            for k in range(RING):
                pool.wait_ge(row_out[k], 32 * STEPS // RING)

        @block.scalar
        def _(act):
            act.wait_ge(w_in, 16)
            act.activation(whi, wraw, ACT.Copy, scale=WS).then_inc(act_chain, 1)
            act.wait_ge(x_in[0], 16)
            act.activation(xhi[:, 0, :, 0:256], xin[:, 0, :, 0:256], ACT.Copy, scale=XS).then_inc(x_hi, 1)

            def pixels(n, k, turn):
                act.wait_ge(x_in[k], 16 * turn)
                act.activation(xhi[:, k % 2], xin[:, k], ACT.Copy, scale=XS).then_inc(x_hi, 1)
                act.wait_ge(proj, n)

            def steps(lo, hi):
                with act.Fori(lo, hi) as i:
                    for k in range(4):
                        n = 4 * i + k + 1
                        pixels(n, (k + 1) % 4, i + (2 if k == 3 else 1))

            steps(0, 1)
            act.wait_ge(ask, 1)
            act.activation(sin1[0:16], red[0:16], ACT.Sin).then_inc(act_chain, 1)
            steps(1, 2)
            act.wait_ge(ask, 3)
            act.activation(sin2[0:16], red[0:16], ACT.Sin).then_inc(act_chain, 1)
            act.activation(cdec[0:96, 0:L], tgrid[0:96], ACT.Exp, scale=cb[0:96, 0, 1:2]).then_inc(act_chain, 1)
            act.activation(cdec[0:96, L:2 * L], tgrid[0:96], ACT.Exp, scale=cb[0:96, 1, 1:2]).then_inc(act_chain, 1)
            steps(2, 3)
            act.wait_ge(ask, 4)
            act.activation(clsm[0:1, 2:3], clsm[0:1, 1:2], ACT.Sqrt).then_inc(act_chain, 1)
            steps(3, 6)
            act.wait_ge(ask, 5)
            act.activation(s2[:, 0:16], s1[:, 0:16], ACT.Sqrt).then_inc(act_chain, 1)
            steps(6, 8)
            act.wait_ge(ask, 6)
            act.activation(s2[:, 0:B], s1[:, 0:B], ACT.Sqrt).then_inc(act_chain, 1)
            def first_part(third, i, k):
                dst = uhi[:, third % 2, :, ds(32 * i + 8 * k, 8)].rearrange("p c q -> p q c")
                act.activation(dst, utmp[:, k], ACT.Copy).then_inc(u_hi, 1)

            def normalised(third, i, k):
                for t in range(8):
                    q = 32 * i + 8 * k + t
                    ins = act.activation(utmp[:, k, t, :],
                                         h[:, ds(q, 1), 64 * third:64 * third + 64].rearrange("p a c -> p (a c)"),
                                         ACT.Identity, scale=s2[:, ds(q, 1)], bias=s1[:, ds(q, 1)])
                ins.then_inc(u_norm_act, 1)

            act.wait_ge(a_done, 1)
            act.wait_ge(text_affine, 1)
            with act.Fori(0, 2) as i:
                for k in range(4):
                    normalised(0, i, k)
                    act.wait_ge(u_norm_act, 4 * i + k + 1)
                    first_part(0, i, k)
                act.wait_ge(u_lo, 4 * i + 4)
            act.wait_ge(ask, 7)
            act.activation(s2[:, B:NQ], s1[:, B:NQ], ACT.Sqrt).then_inc(act_chain, 1)
            act.wait_ge(a_done, 2)
            for third in range(3):
                if third == 2:
                    act.wait_ge(conv, CONV_STEPS // 3)
                with act.Fori(0 if third else 2, 4) as i:
                    for k in (1, 3):
                        act.wait_ge(u_lo, 16 * third + 4 * i + k - 3)
                        normalised(third, i, k)
                        act.wait_ge(u_norm, 8 * third + 2 * i + (k + 1) // 2 - 4)
                        first_part(third, i, k - 1)
                        act.wait_ge(u_norm_act, 8 * third + 2 * i + (k + 1) // 2 + 4)
                        first_part(third, i, k)
            act.wait_ge(d_in, 96)
            act.activation(rwhi[0:HC], rwraw[0:HC], ACT.Copy, scale=WS).then_inc(d_split, 1)
            with act.Fori(0, RG) as g:
                act.wait_ge(ask, g * 2 + 8)
                act.activation(s2[:, 0:RT], s1[:, 0:RT], ACT.Sqrt).then_inc(act_chain, 1)

                def znorm(t):
                    if t >= 4:
                        act.wait_ge(z_t, g * (RT // 2) + t - 3)
                    act.activation(ztok[:, t % 4, 0, :], h[:, ds(RT * g + 2 * t, 1), 0:D].rearrange("p a c -> p (a c)"),
                                   ACT.Identity, scale=rstd[:, 2 * t:2 * t + 1], bias=rnmr[:, 2 * t:2 * t + 1]).then_inc(zn_act, 1)

                act.wait_ge(z_stat, g + 1)
                znorm(0)
                znorm(1)
                for t in range(RT // 2):
                    if t + 2 < RT // 2:
                        znorm(t + 2)
                    act.wait_ge(z_t, g * (RT // 2) + t + 1)
                    if t >= 4:
                        act.wait_ge(z_log, g * (RT // 2) + t - 3)
                    act.activation(zthi[0:HC, t % 4], psum[ZB[t % 4]][0:HC, :].rearrange("p (a b c) -> p a b c", a=2, b=2),
                                   ACT.Copy, scale=US).then_inc(z_hi, 1)
                act.wait_ge(ask, g * 2 + 9)
                act.activation(prob, logit, ACT.Exp).then_inc(z_exp, 1)

            act.activation(w1hi[0:HC + 1], w1raw[0:HC + 1], ACT.Copy, scale=WS).then_inc(d_split, 1)
            act.activation(w2hi[0:HC + 1], w2raw[0:HC + 1], ACT.Copy, scale=WS).then_inc(d_split, 1)

            def hi1(n, k):
                act.wait_ge(t1_done, n + 1)
                act.activation(xthi[0:HC, k % 2], psum[k % 2][0:HC, :].rearrange("p (a b c) -> p a b c", a=2, b=2),
                               ACT.Copy, scale=US).then_inc(hi1_done, 1)

            def gelu(n, k):
                act.wait_ge(l1_done, n + 1)
                act.activation(act1[:, k % 2], bank3(2 + k % 2, 2, D), ACT.Gelu, scale=1 / (US * WS)).then_inc(act_done, 1)

            def hi2(n, k):
                act.wait_ge(t2_done, n + 1)
                act.activation(gthi[0:HC, k % 2], psum[4 + k % 2][0:HC, :].rearrange("p (a b c) -> p a b c", a=2, b=2),
                               ACT.Copy, scale=GS).then_inc(hi2_done, 1)

            def norm(n, k, use):
                act.wait_ge(row_in[k], use)
                if not isinstance(n, int) or n >= 4:
                    act.wait_ge(t1_done, n - 3)
                    act.wait_ge(r_done, n - 3)
                act.activation(x2[:, k % 4, 0, :], row[:, k, 0, 0:D], ACT.Identity, scale=row[:, k, 0, RSTD:RSTD + 1],
                               bias=row[:, k, 0, NMR:NMR + 1]).then_inc(x2_act, 1)

            def step(n, k, it):
                inside = it is not None
                if inside or n + 1 < STEPS:
                    kk = (k + 1) % RING
                    norm(n + 1, kk, 32 * it + (64 if kk else 96) if inside else 32 * ((n + 1) // RING + 1))
                if inside or n < STEPS:
                    if inside or n >= 2:
                        act.wait_ge(l1_done, n - 1)
                    hi1(n, k)
                if inside or 1 <= n <= STEPS:
                    if inside or n >= 3:
                        act.wait_ge(t2_done, n - 2)
                    gelu(n - 1, (k - 1) % RING)
                if inside or 2 <= n:
                    if inside or n >= 4:
                        act.wait_ge(l2_done, n - 3)
                    hi2(n - 2, (k - 2) % RING)

            norm(0, 0, 32)
            for n in range(RING):
                step(n, n, None)
            with act.Fori(0, STEPS // RING - 2) as i:
                for k in range(RING):
                    step(RING * i + k + RING, k, i)
            for n in range(STEPS - RING, STEPS + 2):
                step(n, n % RING, None)

        @block.tensor
        def _(pe):
            def text(half):
                for k in range(8):
                    kk = half * 8 + k
                    o = psum[4 + k // 2][:, (k % 2) * D:(k % 2) * D + D]
                    pe.matmul(o, amat[:, kk * 128:kk * 128 + 128], we[:, kk, :], start=True, stop=False)
                    pe.matmul(o, coef[0:E4, kk * 128:kk * 128 + 128], trow[0:E4, :], start=False, stop=True).then_inc(text_mm, 1)

            pe.wait_ge(w_split, 1)

            def project(k, o, t):
                xh, xl = xhi[:, k % 2, :, t * 128:t * 128 + 128], xlo[:, k % 2, :, t * 128:t * 128 + 128]
                for c in range(KC):
                    pe.matmul(o, xh[:, c, :], whi[:, c, :], start=(c == 0), stop=False)
                    pe.matmul(o, xh[:, c, :], wlo[:, c, :], start=False, stop=False)
                    mm = pe.matmul(o, xl[:, c, :], whi[:, c, :], start=False, stop=(c == KC - 1))
                return mm

            pe.wait_ge(x_hi, 1)
            pe.wait_ge(x_lo, 1)
            for t in range(2):
                mm = project(0, psum[0][:, t * D:t * D + D], t)
            mm.then_inc(proj, 1)
            pe.wait_ge(const_in, 16 * CONSTS)
            pe.matmul(psum[4][0:16, 0:L], fw1[0:3, :], zt[0:3, :], start=True, stop=True).then_inc(pe_filter, 1)
            def steps(lo, hi):
                with pe.Fori(lo, hi) as i:
                    for k in range(4):
                        n = 4 * i + k + 1
                        pe.wait_ge(x_hi, n + 1)
                        pe.wait_ge(x_lo, n + 1)
                        bank = 2 * ((k + 1) % 2)
                        project(k + 1, psum[bank][:, 0:D], 0)
                        project(k + 1, psum[bank][:, D:2 * D], 1)
                        project(k + 1, psum[bank + 1][:, 0:D], 2).then_inc(proj, 1)
                        pe.wait_ge(proj_out, n)

            steps(0, 1)
            pe.wait_ge(act_chain, 2)
            pe.matmul(psum[4][0:16, 0:L], fw2[0:16, :], sin1[0:16, :], start=True, stop=True).then_inc(pe_filter, 1)
            steps(1, 2)
            pe.wait_ge(act_chain, 3)
            for half in range(2):
                pe.matmul(psum[5 + half][0:96, 0:L], fw3[0:16, half * 96:half * 96 + 96], sin2[0:16, :],
                          start=True, stop=True).then_inc(pe_filter, 1)
            steps(2, 4)
            pe.wait_ge(dve_filter, 2)
            pe.wait_ge(gathered, 256)
            pe.wait_ge(text_mat, 1)
            text(0)
            steps(4, 5)
            pe.wait_ge(text_out, 4)
            text(1)
            steps(5, 8)
            pe.wait_ge(urow_in, 48)
            pe.wait_ge(proj_out, 33)
            for third in range(3):
                pe.wait_ge(u_lo, 16 * (third + 1))
                with pe.Fori(0, 4) as i:
                    for e in range(4):
                        pe.wait_ge(toep_in[e], 48 * (i + 4 * third + 1))
                        pe.wait_ge(conv_free, 4 * i + 16 * third + e + 1)
                        for c in range(CG):
                            th = toep[:, e, 2 * c * KP:2 * c * KP + TAPW]
                            tl = toep[:, e, (2 * c + 1) * KP:(2 * c + 1) * KP + TAPW]
                            ch = 16 * i + 4 * e + c
                            uh = uhi[:, third % 2, ds(ch, 1), :].rearrange("p a q -> p (a q)")
                            ul = ulo[:, third % 2, ds(ch, 1), :].rearrange("p a q -> p (a q)")
                            uh0 = uhi[:, third % 2, ds(ch, 1), 0:B].rearrange("p a q -> p (a q)")
                            ul0 = ulo[:, third % 2, ds(ch, 1), 0:B].rearrange("p a q -> p (a q)")
                            uc = urow[:, ds(64 * third + ch, 1)].to_broadcast([128, B])
                            o = psum[e][:, c * 128:c * 128 + 128]
                            o0, o1 = psum[e][:, c * 128:c * 128 + B], psum[e][:, c * 128 + B:c * 128 + 128]
                            kw = dict(start=False, stop=False, skip_group_check=True)
                            pe.matmul(o, th[:, 0:128], uh, start=(c == 0), stop=False, skip_group_check=True)
                            pe.matmul(o, th[:, 0:128], ul, **kw)
                            pe.matmul(o, tl[:, 0:128], uh, **kw)
                            pe.matmul(o1, th[:, 128:256], uh0, **kw)
                            pe.matmul(o1, th[:, 128:256], ul0, **kw)
                            pe.matmul(o1, tl[:, 128:256], uh0, **kw)
                            pe.matmul(o0, ctap[:, e, c, 0:128], uc, **kw)
                            mm = pe.matmul(o1, ctap[:, e, c, 128:256], uc, start=False, stop=True, skip_group_check=True)
                        mm.then_inc(conv, 1)
            pe.wait_ge(conv_free, 4 + CONV_STEPS)
            pe.wait_ge(d_split, 1)
            pe.wait_ge(low_split, 1)
            PT = RT // 2
            with pe.Fori(0, RG) as g:
                for t in range(PT + 2):
                    if t < PT:
                        pe.wait_ge(zn_act, g * PT + t + 1)
                        pe.wait_ge(zn_dve, g * PT + t + 1)
                        if t >= 4:
                            pe.wait_ge(z_hi, g * PT + t - 3)
                            pe.wait_ge(z_lo, g * PT + t - 3)
                        for tile in range(2):
                            for c in range(2):
                                mm = pe.transpose(psum[ZB[t % 4]][0:HC, (2 * tile + c) * 128:(2 * tile + c) * 128 + 128],
                                                  ztok[:, t % 4, tile, c * HC:c * HC + HC], ident[:, :])
                        mm.then_inc(z_t, 1)
                    if t >= 2:
                        u = t - 2
                        pe.wait_ge(z_hi, g * PT + u + 1)
                        pe.wait_ge(z_lo, g * PT + u + 1)
                        for tile in range(2):
                            at = E4 * (2 * u + tile)
                            o = psum[2][:, at:at + E4]
                            zh, zl = zthi[0:HC, u % 4, tile], ztlo[0:HC, u % 4, tile]
                            for c in range(2):
                                pe.matmul(o, zh[:, c], rwhi[0:HC, c], start=(c == 0), stop=False)
                                pe.matmul(o, zh[:, c], rwlo[0:HC, c], start=False, stop=False)
                                mm = pe.matmul(o, zl[:, c], rwhi[0:HC, c], start=False, stop=(c == 1))
                        mm.then_inc(z_log, 1)
                pe.wait_ge(z_pick, g + 1)
                picks = onehot.rearrange("p a b -> p (a b)")
                pe.matmul(psum[3][:, 0:E4 * RT], ltri, picks, start=True, stop=True)
                pe.matmul(psum[3][:, E4 * RT:2 * E4 * RT], onesm, picks, start=True, stop=True).then_inc(z_rank, 1)
                pe.wait_ge(routed, g + 1)
            pe.wait_ge(table_out, 1)
            pe.wait_ge(d_split, 3)
            pe.wait_ge(low_split, 3)

            def transposes(src, bank, s_done):
                for tile in range(2):
                    for c in range(2):
                        mm = pe.transpose(psum[bank][0:HC, (2 * tile + c) * 128:(2 * tile + c) * 128 + 128],
                                          src[:, tile, c * HC:c * HC + HC], ident[:, :])
                mm.then_inc(s_done, 1)

            def experts(m, words):
                _, w = nc.values_load_multi_w_load_instructions(table[0:1, 1, ds(m, words)], engines=[mybir.EngineType.PE],
                                                                min_val=0, max_val=E4 ** 8 - 1)
                return [[(w[j // 4], 2 * (2 * (j % 4) + tile)) for tile in range(2)] for j in range(4 * words)]

            def unpack(e):
                return [pe.snap(((word >> shift) & (E4 - 1)) * 2) for word, shift in e]

            def layer(es, hi, lo, wh, wl, bank, s_done):
                for tile, e2 in enumerate(es):
                    o = psum[bank][:, tile * D:tile * D + D]
                    for c in range(2):
                        K = HC + c
                        w_h = wh[0:K, ds(e2 + c, 1), :].rearrange("p a d -> p (a d)")
                        w_l = wl[0:K, ds(e2 + c, 1), :].rearrange("p a d -> p (a d)")
                        pe.matmul(o, hi[0:K, tile, c], w_h, start=(c == 0), stop=False)
                        pe.matmul(o, hi[0:K, tile, c], w_l, start=False, stop=False)
                        mm = pe.matmul(o, lo[0:K, tile, c], w_h, start=False, stop=(c == 1))
                mm.then_inc(s_done, 1)

            def step(n, k, it, es, n1, n2):
                inside = it is not None
                if inside or n < STEPS:
                    pe.wait_ge(x2_act, n + 1)
                    pe.wait_ge(x2_dve, n + 1)
                    if inside or n >= 2:
                        pe.wait_ge(hi1_done, n - 1)
                        pe.wait_ge(lo1_done, n - 1)
                    transposes(x2[:, k % 4], k % 2, t1_done)
                if inside or 1 <= n <= STEPS:
                    pe.wait_ge(hi1_done, n)
                    pe.wait_ge(lo1_done, n)
                    if inside or n >= 3:
                        pe.wait_ge(act_done, n - 2)
                    j = (k - 1) % 2
                    es[n1] = unpack(es[n1])
                    layer(es[n1], xthi[:, j], xtlo[:, j], w1hi, w1lo, 2 + j, l1_done)
                if inside or 2 <= n <= STEPS + 1:
                    pe.wait_ge(act_done, n - 1)
                    if inside or n >= 4:
                        pe.wait_ge(hi2_done, n - 3)
                        pe.wait_ge(lo2_done, n - 3)
                    j = k % 2
                    transposes(act1[:, j], 4 + j, t2_done)
                if inside or n >= 3:
                    pe.wait_ge(hi2_done, n - 2)
                    pe.wait_ge(lo2_done, n - 2)
                    if inside or n >= 5:
                        pe.wait_ge(fin_done, n - 4)
                    j = (k - 3) % 2
                    if n2 < 2:
                        es[n2] = unpack(es[n2])
                    layer(es[n2], gthi[:, j], gtlo[:, j], w2hi, w2lo, 6 + j, l2_done)

            es = [None, None] + experts(0, RING // 4)
            for n in range(RING):
                step(n, n, None, es, n - 1 + 2, n - 3 + 2)
            with pe.Fori(0, STEPS // RING - 2) as i:
                es = experts((RING // 4) * i + (RING // 4 - 1), RING // 4 + 1)[1:]
                for k in range(RING):
                    step(RING * i + k + RING, k, i, es, k + 2, k)
            es = experts((STEPS - RING) // 4 - 1, RING // 4 + 1)[1:]
            for n in range(STEPS - RING, STEPS + 3):
                k = n - (STEPS - RING)
                step(n, n % RING, None, es, k + 2, k)

        @block.vector
        def _(dve):
            count = [0]

            def link(ins):
                count[0] += 1
                ins.then_inc(v, 1)
                dve.wait_ge(v, count[0])

            def variance(chain, st, var, mu, tmp, eps):
                st2 = [st[:, :, i] for i in range(6)]
                chain(dve.tensor_tensor(mu, st2[1], st2[4], ALU.add))
                chain(dve.tensor_scalar(mu, mu, 0.5, None, ALU.mult))
                chain(dve.tensor_tensor(var, st2[1], st2[4], ALU.subtract))
                chain(dve.scalar_tensor_tensor(out=var, in0=var, scalar=0.25, in1=var, op0=ALU.mult, op1=ALU.mult))
                chain(dve.tensor_tensor(tmp, st2[2], st2[5], ALU.add))
                chain(dve.scalar_tensor_tensor(out=var, in0=tmp, scalar=1.0 / D, in1=var, op0=ALU.mult, op1=ALU.add))
                dve.tensor_scalar(var, var, eps, None, ALU.add).then_inc(ask, 1)

            def invert(chain, var, tmp, inv, answered):
                dve.wait_ge(act_chain, answered)
                chain(dve.reciprocal(inv, tmp))
                for _ in range(2):
                    chain(dve.tensor_tensor(tmp, inv, inv, ALU.mult))
                    chain(dve.tensor_tensor(tmp, tmp, var, ALU.mult))
                    chain(dve.tensor_scalar(tmp, tmp, -0.5, 1.5, ALU.mult, ALU.add))
                    chain(dve.tensor_tensor(inv, inv, tmp, ALU.mult))

            def deviation(chain, st, var, mu, tmp, inv, eps, answered):
                variance(chain, st, var, mu, tmp, eps)
                invert(chain, var, tmp, inv, answered)

            dve.wait_ge(act_chain, 1)
            dve.scalar_tensor_tensor(out=wlo, in0=wraw, scalar=WS, in1=whi, op0=ALU.mult, op1=ALU.subtract).then_inc(w_split, 1)

            def sine_argument(layer):
                dve.wait_ge(pe_filter, layer + 1)
                link(dve.tensor_scalar(ang[0:16], psum[4][0:16, 0:L], fb[0:16, layer:layer + 1], fb[0:16, 2:3],
                                       ALU.add, ALU.mult))
                link(dve.tensor_scalar(red[0:16], ang[0:16], 1 / (2 * PI), MAGIC, ALU.mult, ALU.add))
                link(dve.tensor_scalar(red[0:16], red[0:16], -MAGIC, None, ALU.add))
                for part in (PI2A, PI2B, PI2C):
                    link(dve.scalar_tensor_tensor(out=ang[0:16], in0=red[0:16], scalar=-part, in1=ang[0:16],
                                                  op0=ALU.mult, op1=ALU.add))
                dve.tensor_scalar(red[0:16], ang[0:16], 3.1415925, -3.1415925, ALU.min, ALU.max).then_inc(ask, 1)

            c0, cu, ck, cp = (ucls[0:1, i, :] for i in range(4))

            def taps():
                dve.wait_ge(act_chain, 5)
                dve.wait_ge(pe_filter, 4)
                for half in range(2):
                    t = tap[0:96, half, :]
                    link(dve.scalar_tensor_tensor(out=t, in0=psum[5 + half][0:96, 0:L], scalar=cb[0:96, half, 0:1],
                                                  in1=cdec[0:96, half * L:half * L + L], op0=ALU.add, op1=ALU.mult))
                    link(dve.tensor_scalar(t, t, KS, None, ALU.mult))
                    link(dve.tensor_tensor(t[:, 0:1], t[:, 0:1], cb[0:96, half, 2:3], ALU.add))
                    link(dve.tensor_copy(taphl[0:96, half, 0, 128:128 + L], t))
                    dve.tensor_tensor(taphl[0:96, half, 1, 128:128 + L], t, taphl[0:96, half, 0, 128:128 + L],
                                      ALU.subtract).then_inc(dve_filter, 1)
                dve.wait_ge(dve_filter, 2)
                dve.tensor_tensor(c0, c0, cp, ALU.add).then_inc(cls_sum, 1)
                dve.wait_ge(cls_sum, 1)
                link(dve.bn_stats(cls6[0:1, 0:6], c0))
                variance(link, cls6[0:1, 0:6].unsqueeze(1), clsm[0:1, 1:2], clsm[0:1, 0:1], clsm[0:1, 2:3], LN_EPS)

            def class_token():
                invert(link, clsm[0:1, 1:2], clsm[0:1, 2:3], clsm[0:1, 3:4], 6)
                link(dve.tensor_scalar(cu, c0, clsm[0:1, 0:1], clsm[0:1, 3:4], ALU.subtract, ALU.mult))
                link(dve.tensor_scalar(uclh[0:1, 0, :], cu, US, None, ALU.mult))
                dve.scalar_tensor_tensor(out=uclh[0:1, 1, :], in0=cu, scalar=US, in1=uclh[0:1, 0, :], op0=ALU.mult,
                                         op1=ALU.subtract).then_inc(cls_split, 1)
                dve.wait_ge(tap0_in, 16)
                link(dve.tensor_tensor(ck, ck, cu, ALU.mult))
                dve.scalar_tensor_tensor(out=cp, in0=ck, scalar=CONV_OUT * US, in1=c0, op0=ALU.mult, op1=ALU.add).then_inc(cls_out, 1)

            def text_rows(half):
                for k in range(4):
                    dve.wait_ge(text_mm, 8 * half + 2 * k + 2)
                    dve.tensor_tensor(we[:, 8 * half + 2 * k:8 * half + 2 * k + 2, :], bank3(4 + k, 2, D),
                                      posb[:, 5:6, :].to_broadcast([128, 2, D]), ALU.add).then_inc(text_out, 1)

            def text_variance():
                dve.wait_ge(text_out, 8)
                for k in range(16):
                    ins = dve.bn_stats(tstats[:, k, :], we[:, k, :])
                link(ins)
                variance(link, tstats, s1[:, 0:16], mean[:, 0:16], s2[:, 0:16], TXT_EPS)

            def text_normalise():
                invert(link, s1[:, 0:16], s2[:, 0:16], rstd[:, 0:16], 7)
                for k in range(16):
                    ins = dve.tensor_scalar(we[:, k, :], we[:, k, :], mean[:, k:k + 1], rstd[:, k:k + 1], ALU.subtract, ALU.mult)
                ins.then_inc(text_norm, 1)

            SC = 1 / (XS * WS)

            def second(n, slot, turn, width):
                dve.wait_ge(x_in[slot], 16 * turn)
                dve.wait_ge(x_hi, n + 1)
                dve.scalar_tensor_tensor(out=xlo[:, slot % 2, :, 0:width], in0=xin[:, slot, :, 0:width], scalar=XS,
                                         in1=xhi[:, slot % 2, :, 0:width], op0=ALU.mult, op1=ALU.subtract).then_inc(x_lo, 1)

            def tokens(n, k):
                dve.wait_ge(proj, n + 1)
                b = 2 * (n - 1)
                o0, o1 = bank3(2 * (k % 2), 2, D), psum[2 * (k % 2) + 1][:, 0:D]
                dve.scalar_tensor_tensor(out=h[:, ds(b, 2), 0:D], in0=o0, scalar=SC, in1=posb[:, 0:2, :],
                                         op0=ALU.mult, op1=ALU.add)
                dve.scalar_tensor_tensor(out=h[0:64, ds(b + B, 1), 0:D].rearrange("p a c -> p (a c)"), in0=o1[0:64],
                                         scalar=SC, in1=posb[0:64, 2, :], op0=ALU.mult, op1=ALU.add)
                dve.scalar_tensor_tensor(out=h[0:64, ds(b + B + 1, 1), 0:D].rearrange("p a c -> p (a c)"), in0=o1[64:128],
                                         scalar=SC, in1=posb[64:128, 2, :], op0=ALU.mult, op1=ALU.add).then_inc(proj_out, 1)
                dve.wait_ge(proj_out, n + 1)
                for t in range(2):
                    ins = dve.bn_stats(stats[:, ds(b + t, 1), :].rearrange("p a c -> p (a c)"),
                                       h[:, ds(b + t, 1), 0:D].rearrange("p a c -> p (a c)"))
                return ins

            second(0, 0, 1, 256)
            second(1, 1, 1, 384)
            dve.wait_ge(const_in, 16 * CONSTS)
            link(dve.tensor_tensor(posb[:, 0:5, :], posb[:, 0:5, :], tokb.unsqueeze(1).to_broadcast([128, 5, D]), ALU.add))
            dve.wait_ge(proj, 1)
            dve.scalar_tensor_tensor(out=lout, in0=bank3(0, 2, D), scalar=SC, in1=posb[:, 3:5, :], op0=ALU.mult,
                                     op1=ALU.add).then_inc(proj_out, 1)
            sine_argument(0)

            def steps(lo, hi):
                with dve.Fori(lo, hi) as i:
                    for k in range(4):
                        n = 4 * i + k + 1
                        dve.wait_ge(proj, n)
                        second(n + 1, (k + 2) % 4, i + (2 if k >= 2 else 1), 384)
                        tokens(n, k + 1)

            steps(0, 1)
            sine_argument(1)
            link(dve.memset(taphl[0:96].rearrange("p a b c -> p (a b c)").bitcast(F32), 0.0))
            link(dve.tensor_scalar(cb[0:96, :, 1], cb[0:96, :, 1], -1.0, None, ALU.mult))
            dve.tensor_scalar(cb[0:96, :, 2], cb[0:96, :, 2], CONV_BIAS, None, ALU.mult).then_inc(ask, 1)
            dve.wait_ge(ask, 3)
            steps(1, 2)
            taps()
            steps(2, 4)
            class_token()
            text_rows(0)
            steps(4, 5)
            text_rows(1)
            text_variance()
            steps(5, 6)
            text_normalise()
            steps(6, 7)
            for n in range(29, 33):
                if n < 32:
                    dve.wait_ge(proj, n)
                    second(n + 1, (n + 1) % 4, (n + 1) // 4 + 1, 384)
                ins = tokens(n, n % 4)
            link(ins)
            def scales(lo, hi, answered):
                deviation(link, stats[:, lo:hi, :], s1[:, lo:hi], mean[:, lo:hi], s2[:, lo:hi], rstd[:, lo:hi], LN_EPS, answered)
                link(dve.tensor_scalar(s2[:, lo:hi], rstd[:, lo:hi], US, None, ALU.mult))
                dve.scalar_tensor_tensor(out=s1[:, lo:hi], in0=mean[:, lo:hi], scalar=-1.0, in1=s2[:, lo:hi], op0=ALU.mult,
                                         op1=ALU.mult).then_inc(a_done, 1)

            dve.wait_ge(urow_in, 48)
            dve.wait_ge(proj, 33)
            scales(0, B, 8)

            def normalise(third, i, k, nth):
                q = ds(32 * i + 8 * k, 8)
                w = [128, 8, TC]
                dve.tensor_tensor(utmp[:, k], h[:, q, 64 * third:64 * third + 64], mean[:, q].unsqueeze(2).to_broadcast(w),
                                  ALU.subtract).then_inc(u_centre, 1)
                dve.wait_ge(u_centre, nth)
                dve.tensor_tensor(utmp[:, k], utmp[:, k], s2[:, q].unsqueeze(2).to_broadcast(w), ALU.mult).then_inc(u_norm, 1)

            def split(third, i, k, nth):
                if nth is not None:
                    dve.wait_ge(u_norm, nth)
                dve.wait_ge(u_hi, 16 * third + 4 * i + k + 1)
                q = ds(32 * i + 8 * k, 8)
                hi = uhi[:, third % 2, :, q].rearrange("p c q -> p q c")
                lo = ulo[:, third % 2, :, q].rearrange("p c q -> p q c")
                dve.tensor_tensor(lo, utmp[:, k], hi, ALU.subtract).then_inc(u_lo, 1)

            def add_channels(third, i, j):
                dve.wait_ge(conv, 16 * third + 4 * i + j + 1)
                hc = h[:, :, ds(64 * third + 16 * i + 4 * j, 4)].rearrange("p q c -> p c q")
                dve.scalar_tensor_tensor(out=hc, in0=bank3(j, 4, NQ), scalar=CONV_OUT, in1=hc, op0=ALU.mult,
                                         op1=ALU.add).then_inc(conv_free, 1)

            dve.sem_inc(conv_free, 4)
            dve.wait_ge(h_in, 16 * 9)
            with dve.Fori(0, 2) as i:
                for k in range(4):
                    for t in range(8):
                        q = B + 32 * i + 8 * k + t
                        ins = dve.bn_stats(stats[:, ds(q, 1), :].rearrange("p a c -> p (a c)"),
                                           h[:, ds(q, 1), 0:D].rearrange("p a c -> p (a c)"))
                    ins.then_inc(stat2, 1)
                    split(0, i, k, None)
            dve.wait_ge(stat2, 8)
            scales(B, NQ, 9)
            dve.wait_ge(a_done, 2)
            dve.wait_ge(u_lo, 8)
            with dve.Fori(2, 4) as i:
                for k in (0, 2):
                    normalise(0, i, k, 2 * i + k // 2 - 3)
                for k in range(4):
                    split(0, i, k, 2 * i + k // 2 - 3)
                dve.wait_ge(u_lo, 4 * i + 3)
            for third in range(1, 3):
                with dve.Fori(0, 4) as i:
                    for k in (0, 2):
                        normalise(third, i, k, 8 * third + 2 * i + k // 2 - 3)
                    for k in range(4):
                        add_channels(third - 1, i, k)
                        if third == 2 and k == 0:
                            dve.wait_ge(conv, 16)
                        split(third, i, k, 8 * third + 2 * i + k // 2 - 3)
                    dve.wait_ge(u_lo, 16 * third + 4 * i + 3)
            with dve.Fori(0, 4) as i:
                for j in range(4):
                    add_channels(2, i, j)

            dve.wait_ge(conv_free, 4 + CONV_STEPS)
            dve.wait_ge(conv, CONV_STEPS)
            link(dve.memset(onesm, 1.0))
            for e in range(2):
                link(dve.tensor_copy(run[:, e, :], regbase))

            def low_weights(n, wl, raw, wh, K):
                dve.wait_ge(d_split, n)
                dve.scalar_tensor_tensor(out=wl[0:K], in0=raw[0:K], scalar=WS, in1=wh[0:K], op0=ALU.mult,
                                         op1=ALU.subtract).then_inc(low_split, 1)

            for one, zero, val in ((xthi, xtlo, US), (gthi, gtlo, GS)):
                dve.memset(one[HC:HC + 1].rearrange("p a b c d -> p (a b c d)"), val)
                dve.memset(zero[HC:HC + 1].rearrange("p a b c d -> p (a b c d)"), 0.0)
            dve.wait_ge(cls_in, 16)
            hrow = h[:, :, ROWID:ROWID + 1].bitcast(I32)
            link(dve.tensor_copy(hrow, rowid[:, :].unsqueeze(2)))
            PER, PT = 39, RT // 2

            def statistics(tile, t):
                return dve.bn_stats(rstats[:, t, :], h[:, ds(tile, 1), 0:D].rearrange("p a c -> p (a c)"))

            for t in range(RT):
                ins = dve.bn_stats(rstats[:, t, :], h[:, t, 0:D])
            link(ins)
            dve.wait_ge(d_in, 96)
            low_weights(1, rwlo, rwraw, rwhi, HC)
            with dve.Fori(0, RG) as g:
                n1 = [0]

                def chain(ins):
                    n1[0] += 1
                    ins.then_inc(v1, 1)
                    dve.wait_ge(v1, g * PER + n1[0])

                n3 = [0]
                q1 = dve.snap(((g + 1) & (RG - 1)) * RT)

                def chain_and(tiles, ins):
                    n1[0] += 1
                    ins.then_inc(v1, 1)
                    for _ in range(tiles):
                        other = statistics(q1 + n3[0], n3[0])
                        n3[0] += 1
                    dve.wait_ge(v1, g * PER + n1[0])
                    return other

                q0 = RT * g
                dve.tensor_copy(before[:, ds(g, 1), :].rearrange("p a e -> p (a e)"), run[:, 0, :])
                mu, inv = mean[:, 0:RT], rstd[:, 0:RT]
                deviation(chain, rstats, s1[:, 0:RT], mu, s2[:, 0:RT], inv, LN_EPS, g + 10)
                chain(dve.scalar_tensor_tensor(out=rnmr, in0=mu, scalar=-1.0, in1=inv, op0=ALU.mult, op1=ALU.mult))
                dve.tensor_copy(h[:, ds(q0, RT), MEAN:MEAN + 1], mu.unsqueeze(2))
                dve.tensor_copy(h[:, ds(q0, RT), RSTD:RSTD + 1], inv.unsqueeze(2))
                dve.tensor_copy(h[:, ds(q0, RT), NMR:NMR + 1], rnmr.unsqueeze(2)).then_inc(z_stat, 1)

                def znorm(t):
                    if t >= 4:
                        dve.wait_ge(z_t, g * PT + t - 3)
                    dve.tensor_scalar(ztok[:, t % 4, 1, :], h[:, ds(q0 + 2 * t + 1, 1), 0:D].rearrange("p a c -> p (a c)"),
                                      mean[:, 2 * t + 1:2 * t + 2], rstd[:, 2 * t + 1:2 * t + 2], ALU.subtract,
                                      ALU.mult).then_inc(zn_dve, 1)

                znorm(0)
                znorm(1)
                for t in range(PT):
                    if t + 2 < PT:
                        znorm(t + 2)
                    dve.wait_ge(z_hi, g * PT + t + 1)
                    if t >= 4:
                        dve.wait_ge(z_log, g * PT + t - 3)
                    dve.scalar_tensor_tensor(out=flat(ztlo[0:HC, t % 4]), in0=psum[ZB[t % 4]][0:HC, :],
                                             scalar=US, in1=flat(zthi[0:HC, t % 4]), op0=ALU.mult, op1=ALU.subtract).then_inc(z_lo, 1)
                dve.wait_ge(z_log, g * PT + PT)
                w = [128, RT, E4]
                chain_and(2, dve.scalar_tensor_tensor(out=logit, in0=bank3(2, RT, E4), scalar=1 / (US * WS),
                                               in1=rbias.unsqueeze(1).to_broadcast(w), op0=ALU.mult, op1=ALU.add))
                chain_and(2, dve.tensor_reduce(rmax, logit, AX, ALU.max))
                dve.tensor_tensor(logit, logit, rmax.unsqueeze(2).to_broadcast(w), ALU.subtract).then_inc(ask, 1)
                for _ in range(6):
                    statistics(q1 + n3[0], n3[0])
                    n3[0] += 1
                dve.wait_ge(z_exp, g + 1)
                chain_and(2, dve.tensor_reduce(rsum, prob, AX, ALU.add))
                chain_and(2, dve.reciprocal(rsum, rsum))
                chain_and(1, dve.tensor_tensor(prob, prob, rsum.unsqueeze(2).to_broadcast(w), ALU.mult))
                chain_and(1, dve.tensor_reduce(rmax, prob, AX, ALU.max))
                chain_and(1, dve.tensor_tensor(pick, prob, rmax.unsqueeze(2).to_broadcast(w), ALU.is_equal))
                chain_and(1, dve.tensor_tensor(pick, pick, pickw.unsqueeze(1).to_broadcast(w), ALU.mult))
                chain_and(1, dve.tensor_reduce(rmax, pick, AX, ALU.max))
                chain_and(1, dve.tensor_tensor(pick, pick, rmax.unsqueeze(2).to_broadcast(w), ALU.is_equal))
                chain_and(1, dve.tensor_scalar(rmax, piota.to_broadcast([128, RT]), CLS + 0.5, None, ALU.is_gt))
                chain_and(1, dve.tensor_scalar(rmax, rmax, tilej[:, ds(g, 1)], None, ALU.mult))
                chain_and(1, dve.tensor_scalar(rsum, rmax, -1.0, 1.0, ALU.mult, ALU.add))
                chain_and(1, dve.tensor_tensor(pick, pick, rsum.unsqueeze(2).to_broadcast(w), ALU.mult))
                dve.tensor_copy(onehot, pick).then_inc(z_pick, 1)
                dve.wait_ge(z_rank, g + 1)
                total = psum[3][:, E4 * RT:2 * E4 * RT].rearrange("p (a b) -> p a b", b=E4)
                chain_and(1, dve.tensor_copy(prob, total))
                chain_and(1, dve.memset(logit, 1.0))
                for e in range(E4):
                    ins = dve.tensor_tensor_scan(rank[:, :, e], logit[:, :, e], prob[:, :, e], run[:, 0, e:e + 1],
                                                 ALU.mult, ALU.add)
                chain_and(1, ins)
                dve.tensor_copy(run[:, 1, :], rank[:, RT - 1, :])
                chain_and(1, dve.tensor_tensor(prob, rank, prob, ALU.subtract))
                chain_and(1, dve.tensor_tensor(prob, prob, bank3(3, RT, E4), ALU.add))
                chain_and(1, dve.tensor_tensor(prob, prob, pick, ALU.mult))
                chain_and(1, dve.tensor_reduce(destf, prob, AX, ALU.add))
                chain_and(1, dve.scalar_tensor_tensor(out=destf, in0=rmax, scalar=float(1 << 20), in1=destf, op0=ALU.mult, op1=ALU.add))
                chain(dve.tensor_copy(run[:, 0, :], run[:, 1, :]))
                dve.tensor_copy(dest[:, ds(q0, RT)], destf).then_inc(routed, 1)
                assert n1[0] == PER, n1[0]

            n2 = [0]

            def tlink(ins):
                n2[0] += 1
                ins.then_inc(v2, 1)
                dve.wait_ge(v2, n2[0])

            dve.wait_ge(routed, RG)
            tlink(dve.tensor_scalar(destf[:, 0:4], run[:, 0, :], piota, None, ALU.add))
            tlink(dve.tensor_copy(padid[:, :], destf[:, 0:4]))
            tn, base = tabn[0:1, :], regbase[0:1]
            tlink(dve.tensor_tensor(tn[:, 0:4], before[0:1, RG - 1, :], base, ALU.subtract))
            tlink(dve.tensor_tensor(tn[:, 4:8], run[0:1, 0, :], base, ALU.subtract))
            tlink(dve.tensor_scalar(tn[:, 4:8], tn[:, 4:8], 127.0, None, ALU.add))
            tlink(dve.tensor_copy(tabi[0:1, :], tn[:, 0:8]))
            tlink(dve.tensor_scalar(tabi[0:1, :], tabi[0:1, :], 7, None, ALU.logical_shift_right))
            tlink(dve.tensor_copy(tn[:, 0:8], tabi[0:1, :]))
            tlink(dve.tensor_tensor(tn[:, 4:8], tn[:, 4:8], tn[:, 0:4], ALU.subtract))
            tlink(dve.memset(tn[:, 8:9], 0.0))
            tlink(dve.memset(tn[:, 24:32], 1.0))
            tlink(dve.tensor_tensor_scan(tn[:, 9:17], tn[:, 24:32], tn[:, 0:8], tn[:, 8:9], ALU.mult, ALU.add))
            off = tn[:, 32:40]
            tlink(dve.tensor_copy(off[:, 0:4], base))
            tlink(dve.scalar_tensor_tensor(out=off[:, 4:8], in0=tn[:, 0:4], scalar=128.0, in1=base, op0=ALU.mult, op1=ALU.add))
            tlink(dve.scalar_tensor_tensor(out=off, in0=tn[:, 8:16], scalar=-128.0, in1=off, op0=ALU.mult, op1=ALU.add))
            tlink(dve.tensor_tensor(tn[:, 40:47], tn[:, 33:40], tn[:, 32:39], ALU.subtract))
            f = [tabf[0:1, i, :] for i in range(4)]
            tlink(dve.tensor_scalar(f[0], f[3], 128.0, None, ALU.mult))
            tlink(dve.memset(f[1], 0.0))
            for k in range(1, 2 * E4):
                tlink(dve.tensor_scalar(f[2], f[3], tn[:, 8 + k:9 + k], None, ALU.is_ge))
                dve.scalar_tensor_tensor(out=f[1], in0=f[2], scalar=2.0 if k != E4 else -2.0 * (E4 - 1), in1=f[1], op0=ALU.mult,
                                         op1=ALU.add)
                tlink(dve.scalar_tensor_tensor(out=f[0], in0=f[2], scalar=tn[:, 39 + k:40 + k], in1=f[0], op0=ALU.mult, op1=ALU.add))
            tlink(dve.tensor_scalar(f[2], f[3], tn[:, 16:17], None, ALU.is_ge))
            tlink(dve.tensor_scalar(f[3], f[0], -1.0, float(DUMMY), ALU.mult, ALU.add))
            tlink(dve.tensor_tensor(f[3], f[3], f[2], ALU.mult))
            tlink(dve.tensor_tensor(f[0], f[0], f[3], ALU.add))
            tlink(dve.tensor_copy(table[0:1, 0, :], f[0]))
            words = f[1].rearrange("p (a b) -> p a b", b=8)
            tlink(dve.tensor_tensor(words, words, small[0:1, 88:96].unsqueeze(1).to_broadcast([1, SLOTS // 8, 8]), ALU.mult))
            tlink(dve.tensor_reduce(f[2][:, 0:SLOTS // 8], words, AX, ALU.add))
            dve.tensor_copy(table[0:1, 1, 0:SLOTS // 8], f[2][:, 0:SLOTS // 8]).then_inc(table_out, 1)
            low_weights(2, w1lo, w1raw, w1hi, HC + 1)
            low_weights(3, w2lo, w2raw, w2hi, HC + 1)

            def norm(n, k, use):
                dve.wait_ge(row_in[k], use)
                if not isinstance(n, int) or n >= 4:
                    dve.wait_ge(t1_done, n - 3)
                dve.tensor_scalar(x2[:, k % 4, 1, :], row[:, k, 1, 0:D], row[:, k, 1, MEAN:MEAN + 1],
                                  row[:, k, 1, RSTD:RSTD + 1], ALU.subtract, ALU.mult).then_inc(x2_dve, 1)

            def residual(n, k):
                dve.wait_ge(x2_act, n + 1)
                dve.wait_ge(x2_dve, n + 1)
                dve.tensor_tensor(row[:, k, :, 0:D], row[:, k, :, 0:D], x2[:, k % 4], ALU.add).then_inc(r_done, 1)

            def low(n, k, bank, hi, lo, scale, s_hi, s_lo):
                dve.wait_ge(s_hi, n + 1)
                dve.scalar_tensor_tensor(out=flat(lo[0:HC, k % 2]), in0=psum[bank + k % 2][0:HC, :], scalar=scale,
                                         in1=flat(hi[0:HC, k % 2]), op0=ALU.mult, op1=ALU.subtract).then_inc(s_lo, 1)

            def final(n, k):
                dve.wait_ge(l2_done, n + 1)
                dve.wait_ge(r_done, n + 1)
                dve.scalar_tensor_tensor(out=row[:, k, :, 0:D], in0=bank3(6 + k % 2, 2, D), scalar=1 / (GS * WS),
                                         in1=row[:, k, :, 0:D], op0=ALU.mult, op1=ALU.add).then_inc(fin_done, 1)

            def step(n, k, it):
                inside = it is not None
                if inside or n + 1 < STEPS:
                    kk = (k + 1) % RING
                    norm(n + 1, kk, 32 * it + (64 if kk else 96) if inside else 32 * ((n + 1) // RING + 1))
                if inside or n < STEPS:
                    if inside or n >= 2:
                        dve.wait_ge(l1_done, n - 1)
                    low(n, k, 0, xthi, xtlo, US, hi1_done, lo1_done)
                    residual(n, k)
                if inside or 2 <= n <= STEPS + 1:
                    if inside or n >= 4:
                        dve.wait_ge(l2_done, n - 3)
                    low(n - 2, (k - 2) % RING, 4, gthi, gtlo, GS, hi2_done, lo2_done)
                if inside or n >= 3:
                    final(n - 3, (k - 3) % RING)

            norm(0, 0, 32)
            for n in range(RING):
                step(n, n, None)
            with dve.Fori(0, STEPS // RING - 2) as i:
                for k in range(RING):
                    step(RING * i + k + RING, k, i)
            for n in range(STEPS - RING, STEPS + 3):
                step(n, n % RING, None)


_SHAPES = {
    "xt": ((PAIRS, 128, KC, 384), F32), "xl": ((128, KC, 256), F32), "wp": ((128, KC, D), F32), "tokb": ((128, D), F32),
    "pos": ((128, 6 * D), F32), "cls": ((1, D), F32), "pos0": ((1, D), F32), "ident": ((128, 128), F32),
    "blk": ((128, 128), F32), "small": ((128, 96), F32), "idsp": ((128, 16), I32), "lenp": ((128, 16), I32),
    "lenv": ((E4, 2048), I32), "rowid": ((128, NQ), I32), "trows": ((E4, D), F32), "gb": ((128, 2 * D), F32),
    "word": ((VOCAB, D), F32), "zt": ((3, L), F32), "tgrid": ((96, L), F32), "fw1": ((3, 16), F32),
    "fw2": ((16, 16), F32), "fw3": ((16, D), F32), "fb": ((16, 4), F32), "cb": ((96, 2, 3), F32),
    "rw": ((HC, 2, E4), F32), "w1": ((HC + 1, 2 * E4, D), F32), "w2": ((HC + 1, 2 * E4, D), F32),
    "padrow": ((128, RW), I32), "slots": ((1, SLOTS), F32), "ltri": ((128, 128), F16),
}


def _layout(i):
    import numpy as np
    f = np.float32
    g = lambda k: np.asarray(i[k])
    x = g("x").reshape(B, 3, 14, 16, 14, 16).transpose(1, 3, 5, 0, 2, 4).reshape(KC, 128, B, NPATCH)
    xt = np.empty((PAIRS, 128, KC, 3, 128), f)
    y = x.reshape(KC, 128, PAIRS, 2, NPATCH).transpose(2, 1, 0, 3, 4)
    xt[:, :, :, 0:2, :] = y[..., 0:128]
    xt[:, :, :, 2, 0:64] = y[:, :, :, 0, 128:192]
    xt[:, :, :, 2, 64:128] = y[:, :, :, 1, 128:192]
    xl = x[:, :, :, 192:196].transpose(1, 0, 3, 2).reshape(128, KC, 256)
    pt = g("L0_tok_pos_table")
    pos = np.zeros((128, 6, D), f)
    pos[:, 0] = pos[:, 1] = pt[1:129]
    pos[0:64, 2] = pos[64:128, 2] = pt[129:193]
    for n in range(4):
        pos[64 * (n % 2):64 * (n % 2) + 64, 3 + n // 2] = pt[193 + n]
    pos[:, 5] = np.concatenate([g("L0_txt_pos_emb")[0:TXT]] * 4)
    p = np.arange(128)
    small = np.zeros((128, 96), f)
    small[:, 0:32] = np.arange(32)
    small[0:2, 32:64] = np.arange(32)
    small[0:4, 64:66] = [[4, 5], [4, 4], [-1e9, 0], [-1e9, 1]]
    small[:, 66] = p % 32
    small[:, 68:72] = g("L0_ffn_router_b")
    small[:, 72:76] = [4, 3, 2, 1]
    small[:, 76:80] = np.arange(E4) * REGION
    small[:, 80] = p
    small[:, 83:85] = 1
    small[:, 88:96] = 4.0 ** np.arange(8) / 2
    ln, mk = g("_lenS").astype(np.int32), g("mask_BS_i1_0").astype(np.int32)
    lenv = np.stack([np.repeat(ln, TXT)] * 2 + [mk.reshape(-1)] * 2)
    ids = g("x_txt").astype(np.int32).reshape(16, 128).T
    lenp = np.repeat(ln, TXT).reshape(16, 128).T
    rowid = np.zeros((128, NQ), np.int32)
    rowid[:, 0:B] = np.arange(B) * L + 1 + p[:, None]
    rowid[:, B:] = np.arange(B) * L + np.where(p == CLS, 0, 129 + p)[:, None]
    t = np.linspace(0, 1, L, dtype=f)
    w = f(2 * np.pi) * np.linspace(0, L - 1, L, dtype=f) / f(L)
    zt = np.stack([t, np.cos(f(1e-4) * w), -np.sin(f(1e-4) * w)]).astype(f)
    halves = lambda v: np.asarray(v).reshape(2, 96).T
    cb = np.stack([halves(g("L0_attn_b3")), halves(g("L0_attn_deltas_abs")), halves(g("L0_attn_bias"))], axis=2)
    fb = np.zeros((16, 4), f)
    fb[:, 0], fb[:, 1], fb[:, 2] = g("L0_attn_b1"), g("L0_attn_b2"), g("L0_attn_freq")

    def expert(w, b):
        r = np.zeros((HC + 1, E4, 2, D), f)
        r[0:HC] = w.reshape(E4, 2, HC, D).transpose(2, 0, 1, 3)
        r[HC, :, 1] = b
        return r.reshape(HC + 1, 2 * E4, D)

    padrow = np.zeros((128, RW), np.int32)
    padrow[:, ROWID] = 1 << 20
    word = g("L0_txt_word_emb")
    return {
        "xt": xt.reshape(PAIRS, 128, KC, 384), "xl": xl, "wp": g("L0_tok_W").reshape(KC, 128, D).transpose(1, 0, 2),
        "tokb": np.tile(g("L0_tok_b"), (128, 1)), "pos": pos.reshape(128, 6 * D), "cls": g("L0_tok_class_token").reshape(1, D),
        "pos0": pt[0:1], "ident": np.eye(128, dtype=f), "blk": np.kron(np.eye(4), np.ones((32, 32))).astype(f),
        "small": small, "idsp": ids, "lenp": lenp, "lenv": lenv, "rowid": rowid,
        "trows": np.stack([word[SEP], word[0], g("L0_txt_type_emb")[0], g("L0_txt_type_emb")[1]]),
        "gb": np.tile(np.concatenate([g("L0_txt_ln_gamma"), g("L0_txt_ln_beta")]), (128, 1)), "word": word,
        "zt": zt, "tgrid": np.tile(t, (96, 1)), "fw1": g("L0_attn_w1").T, "fw2": g("L0_attn_w2").T, "fw3": g("L0_attn_w3").T,
        "fb": fb, "cb": cb, "rw": g("L0_ffn_router_w").reshape(2, HC, E4).transpose(1, 0, 2),
        "w1": expert(g("L0_ffn_w1"), g("L0_ffn_b1")), "w2": expert(g("L0_ffn_w2"), g("L0_ffn_b2")),
        "padrow": padrow, "slots": np.arange(SLOTS, dtype=f).reshape(1, SLOTS), "ltri": np.triu(np.ones((128, 128)), 1).astype(np.float16),
    }


def kernel(**inputs):
    import numpy as np
    import concourse.bacc as bacc
    from concourse.bass_utils import run_bass_kernel_spmd as run

    nc = bacc.Bacc("TRN2", target_bir_lowering=False, num_devices=1)
    arrays, args = {}, {}
    for name, v in _layout(inputs).items():
        shape, dt = _SHAPES[name]
        v = np.ascontiguousarray(v)
        assert v.shape == shape and mybir.dt.from_np(v.dtype) == dt, (name, v.shape, v.dtype)
        arrays[f"in_{name}"] = v
        args[name] = nc.dram_tensor(f"in_{name}", shape, dt, kind="ExternalInput").ap()
    args["out"] = nc.dram_tensor("out_rows", (NTOK, D), F32, kind="ExternalOutput").ap()
    build(nc, args)
    r = run(nc, [arrays], core_ids=[0])
    return r.results[0]["out_rows"].reshape(B, L, D)
```
